# Optimizing a Trainium2 kernel written in Bass

```python
import numpy as np
import jax
import jax.numpy as jnp

def _softmax(x, axis=-1):
    return jax.nn.softmax(x, axis=axis)

def _gelu(x):
    return jax.nn.gelu(x, approximate=True)

def _silu(x):
    return jax.nn.silu(x)

def _sigmoid(x):
    return jax.nn.sigmoid(x)

def _layernorm(x, axis=-1, eps=1e-05):
    m = jnp.mean(x, axis=axis, keepdims=True)
    v = jnp.var(x, axis=axis, keepdims=True)
    return (x - m) / jnp.sqrt(v + eps)

def _scatter_add(tgt, idx, src, axis=0):
    return tgt.at[idx].add(src)

def _segment_sum(src, seg, n):
    return jax.ops.segment_sum(src, seg, n)
kernel_name = 'mk_early_fusion_embed_d1_tok_img768_r4_fc3607'

def setup_inputs(seed: int=0):
    np.random.seed(seed)
    _w = jnp.asarray

    def _rec_inputs():
        import jax
        import jax.numpy as jnp
        _rk = jax.random.key(seed)
        x = -1.80045e-05 + 0.999906 * jax.random.normal(jax.random.fold_in(_rk, 1), (64, 3, 96, 96), jnp.float32)
        x_txt = jax.random.randint(jax.random.fold_in(_rk, 51), (64, 32), 0, 12564, jnp.int32)
        return (x, x_txt)
    x, x_txt = _rec_inputs()

    def _L0_tok_setup():
        import jax, jax.numpy as jnp
        import numpy as np
        IMAGE_SIZE = 96
        PATCH = 16
        CHANNELS = 3
        TOKEN_DIM = 192
        NUM_PATCHES = (IMAGE_SIZE // PATCH) ** 2
        PATCH_DIM = CHANNELS * PATCH * PATCH
        N_TOKENS = NUM_PATCHES + 1

        def _fixed_pos_embedding(n_tokens, dim):
            i = np.arange(n_tokens, dtype=np.float32)[:, None]
            j = np.arange(dim, dtype=np.float32)[None, :]
            j_even = np.where(j % 2 == 0, j, j - 1)
            angle = i / np.power(10000.0, j_even / dim)
            tab = np.where(j % 2 == 0, np.sin(angle), np.cos(angle)).astype(np.float32)
            return jnp.asarray(tab)

        def _make_patches(image):
            B, C, H, Wd = image.shape
            p = PATCH
            hp, wp = (H // p, Wd // p)
            x = image.reshape(B, C, hp, p, wp, p)
            x = x.transpose(0, 1, 2, 4, 3, 5)
            return x.reshape(B, hp * wp, C * p * p)
        key = jax.random.key(seed)
        k_img, k_w, k_b, k_cls = jax.random.split(key, 4)
        image = jax.random.normal(k_img, (128, CHANNELS, IMAGE_SIZE, IMAGE_SIZE), dtype=jnp.float32)
        W = jax.random.normal(k_w, (TOKEN_DIM, PATCH_DIM), dtype=jnp.float32) / np.sqrt(PATCH_DIM)
        b = jax.random.normal(k_b, (TOKEN_DIM,), dtype=jnp.float32) * 0.01
        class_token = jax.random.normal(k_cls, (1, TOKEN_DIM), dtype=jnp.float32)
        pos_embedding = _fixed_pos_embedding(N_TOKENS, TOKEN_DIM)
        return {'image': image, 'W': W, 'b': b, 'class_token': class_token, 'pos_embedding': pos_embedding}
    _L0_tok_all = _L0_tok_setup()
    _L0_tok_in = {k: v for k, v in _L0_tok_all.items() if k in ('W', 'b', 'class_token', 'pos_embedding')}
    del _L0_tok_all

    def _L0_txt_setup():
        import jax, jax.numpy as jnp
        import numpy as np
        VOCAB = 50257
        EMBED_DIM = 192
        NUM_TUNE = 256
        key = jax.random.key(seed)
        k_ids, k_tune, k_base, k_train = jax.random.split(key, 4)
        input_ids = jax.random.randint(k_ids, (8, 1024), 0, VOCAB, dtype=jnp.int64)
        tune_ids = jnp.sort(jax.random.randint(k_tune, (NUM_TUNE,), 0, VOCAB, dtype=jnp.int64))
        base_weight = jax.random.normal(k_base, (VOCAB, EMBED_DIM), dtype=jnp.float32)
        train_weight = jax.random.normal(k_train, (NUM_TUNE, EMBED_DIM), dtype=jnp.float32)
        return {'input_ids': input_ids, 'tune_ids': tune_ids, 'base_weight': base_weight, 'train_weight': train_weight}
    _L0_txt_all = _L0_txt_setup()
    _L0_txt_in = {k: v for k, v in _L0_txt_all.items() if k in ('tune_ids', 'base_weight', 'train_weight')}
    del _L0_txt_all

    def _L0_attn_setup():
        import jax, jax.numpy as jnp
        import numpy as np
        B, N, C = (2, 1024, 192)
        H = 12
        HD = C // H
        THETA = 10000.0

        def _rope_tables(n, hd, dtype):
            inv = 1.0 / THETA ** (jnp.arange(0, hd, 2, dtype=jnp.float32) / hd)
            freqs = jnp.arange(n, dtype=jnp.float32)[:, None] * inv[None, :]
            cos = jnp.concatenate([jnp.cos(freqs), jnp.cos(freqs)], axis=-1).astype(dtype)
            sin = jnp.concatenate([jnp.sin(freqs), jnp.sin(freqs)], axis=-1).astype(dtype)
            return (cos, sin)

        def _rotate_half(x):
            x1, x2 = (x[..., :x.shape[-1] // 2], x[..., x.shape[-1] // 2:])
            return jnp.concatenate([-x2, x1], axis=-1)
        key = jax.random.key(seed)
        k1, k2, k3 = jax.random.split(key, 3)
        x = jax.random.normal(k1, (B, N, C), dtype=jnp.float32)
        w_qkv = jax.random.normal(k2, (3 * C, C), dtype=jnp.float32) * C ** (-0.5)
        b_qkv = jnp.zeros((3 * C,), dtype=jnp.float32)
        w_proj = jax.random.normal(k3, (C, C), dtype=jnp.float32) * C ** (-0.5)
        b_proj = jnp.zeros((C,), dtype=jnp.float32)
        return {'x': x, 'w_qkv': w_qkv, 'b_qkv': b_qkv, 'w_proj': w_proj, 'b_proj': b_proj}
    _L0_attn_all = _L0_attn_setup()
    _L0_attn_in = {k: v for k, v in _L0_attn_all.items() if k in ('w_qkv', 'b_qkv', 'w_proj', 'b_proj')}
    del _L0_attn_all

    def _L0_ffn_setup():
        import jax, jax.numpy as jnp
        import numpy as np
        B, N, DIM, HEADS = (4, 256, 192, 12)
        HIDDEN, E, TOPK = (768, 8, 2)
        EPS = 1e-05

        def _layernorm(x, g, b):
            mu = jnp.mean(x, axis=-1, keepdims=True)
            var = jnp.var(x, axis=-1, keepdims=True)
            return (x - mu) * jax.lax.rsqrt(var + EPS) * g + b
        key = jax.random.key(seed)
        ks = jax.random.split(key, 10)
        s = 0.02
        return {'x': jax.random.normal(ks[0], (B, N, DIM), dtype=jnp.float32), 'ln1_g': jnp.ones((DIM,), jnp.float32), 'ln1_b': jnp.zeros((DIM,), jnp.float32), 'qkv_w': jax.random.normal(ks[1], (3 * DIM, DIM), jnp.float32) * s, 'proj_w': jax.random.normal(ks[2], (DIM, DIM), jnp.float32) * s, 'proj_b': jnp.zeros((DIM,), jnp.float32), 'ln2_g': jnp.ones((DIM,), jnp.float32), 'ln2_b': jnp.zeros((DIM,), jnp.float32), 'gate_w': jax.random.normal(ks[3], (E, DIM), jnp.float32) * s, 'gate_b': jnp.zeros((E,), jnp.float32), 'w1': jax.random.normal(ks[4], (E, HIDDEN, DIM), jnp.float32) * s, 'b1': jnp.zeros((E, HIDDEN), jnp.float32), 'w2': jax.random.normal(ks[5], (E, DIM, HIDDEN), jnp.float32) * s, 'b2': jnp.zeros((E, DIM), jnp.float32)}
    _L0_ffn_all = _L0_ffn_setup()
    _L0_ffn_in = {k: v for k, v in _L0_ffn_all.items() if k in ('ln1_g', 'ln1_b', 'qkv_w', 'proj_w', 'proj_b', 'ln2_g', 'ln2_b', 'gate_w', 'gate_b', 'w1', 'b1', 'w2', 'b2')}
    del _L0_ffn_all
    return {'x': x, 'x_txt': x_txt, 'L0_tok_W': _L0_tok_in['W'], 'L0_tok_b': _L0_tok_in['b'], 'L0_tok_class_token': _L0_tok_in['class_token'], 'L0_tok_pos_embedding': _L0_tok_in['pos_embedding'], 'L0_txt_tune_ids': _L0_txt_in['tune_ids'], 'L0_txt_base_weight': _L0_txt_in['base_weight'], 'L0_txt_train_weight': _L0_txt_in['train_weight'], 'L0_attn_w_qkv': _L0_attn_in['w_qkv'], 'L0_attn_b_qkv': _L0_attn_in['b_qkv'], 'L0_attn_w_proj': _L0_attn_in['w_proj'], 'L0_attn_b_proj': _L0_attn_in['b_proj'], 'L0_ffn_ln1_g': _L0_ffn_in['ln1_g'], 'L0_ffn_ln1_b': _L0_ffn_in['ln1_b'], 'L0_ffn_qkv_w': _L0_ffn_in['qkv_w'], 'L0_ffn_proj_w': _L0_ffn_in['proj_w'], 'L0_ffn_proj_b': _L0_ffn_in['proj_b'], 'L0_ffn_ln2_g': _L0_ffn_in['ln2_g'], 'L0_ffn_ln2_b': _L0_ffn_in['ln2_b'], 'L0_ffn_gate_w': _L0_ffn_in['gate_w'], 'L0_ffn_gate_b': _L0_ffn_in['gate_b'], 'L0_ffn_w1': _L0_ffn_in['w1'], 'L0_ffn_b1': _L0_ffn_in['b1'], 'L0_ffn_w2': _L0_ffn_in['w2'], 'L0_ffn_b2': _L0_ffn_in['b2']}

def reference(x, x_txt, L0_tok_W, L0_tok_b, L0_tok_class_token, L0_tok_pos_embedding, L0_txt_tune_ids, L0_txt_base_weight, L0_txt_train_weight, L0_attn_w_qkv, L0_attn_b_qkv, L0_attn_w_proj, L0_attn_b_proj, L0_ffn_ln1_g, L0_ffn_ln1_b, L0_ffn_qkv_w, L0_ffn_proj_w, L0_ffn_proj_b, L0_ffn_ln2_g, L0_ffn_ln2_b, L0_ffn_gate_w, L0_ffn_gate_b, L0_ffn_w1, L0_ffn_b1, L0_ffn_w2, L0_ffn_b2):
    import jax
    import jax.numpy as jnp

    def _L0_tok_ref(image, W, b, class_token, pos_embedding):
        import jax, jax.numpy as jnp
        import numpy as np
        IMAGE_SIZE = 96
        PATCH = 16
        CHANNELS = 3
        TOKEN_DIM = 192
        NUM_PATCHES = (IMAGE_SIZE // PATCH) ** 2
        PATCH_DIM = CHANNELS * PATCH * PATCH
        N_TOKENS = NUM_PATCHES + 1

        def _fixed_pos_embedding(n_tokens, dim):
            i = np.arange(n_tokens, dtype=np.float32)[:, None]
            j = np.arange(dim, dtype=np.float32)[None, :]
            j_even = np.where(j % 2 == 0, j, j - 1)
            angle = i / np.power(10000.0, j_even / dim)
            tab = np.where(j % 2 == 0, np.sin(angle), np.cos(angle)).astype(np.float32)
            return jnp.asarray(tab)

        def _make_patches(image):
            B, C, H, Wd = image.shape
            p = PATCH
            hp, wp = (H // p, Wd // p)
            x = image.reshape(B, C, hp, p, wp, p)
            x = x.transpose(0, 1, 2, 4, 3, 5)
            return x.reshape(B, hp * wp, C * p * p)
        patches = _make_patches(image)
        tokens = jnp.einsum('bnd,td->bnt', patches, W) + b
        B = tokens.shape[0]
        cls = jnp.broadcast_to(class_token[None, :, :], (B, 1, TOKEN_DIM))
        tokens = jnp.concatenate([cls, tokens], axis=1)
        return tokens + pos_embedding[None, :, :]

    def _L0_txt_ref(input_ids, tune_ids, base_weight, train_weight):
        import jax, jax.numpy as jnp
        import numpy as np
        VOCAB = 50257
        EMBED_DIM = 192
        NUM_TUNE = 256
        id2row = jnp.full((VOCAB,), -1, dtype=jnp.int32)
        id2row = id2row.at[tune_ids].set(jnp.arange(NUM_TUNE, dtype=jnp.int32))
        out = base_weight[input_ids]
        rows = id2row[input_ids]
        mask = rows >= 0
        override = train_weight[jnp.maximum(rows, 0)]
        return jnp.where(mask[..., None], override, out)

    def _L0_attn_ref(x, w_qkv, b_qkv, w_proj, b_proj):
        import jax, jax.numpy as jnp
        import numpy as np
        B, N, C = (2, 1024, 192)
        H = 12
        HD = C // H
        THETA = 10000.0

        def _rope_tables(n, hd, dtype):
            inv = 1.0 / THETA ** (jnp.arange(0, hd, 2, dtype=jnp.float32) / hd)
            freqs = jnp.arange(n, dtype=jnp.float32)[:, None] * inv[None, :]
            cos = jnp.concatenate([jnp.cos(freqs), jnp.cos(freqs)], axis=-1).astype(dtype)
            sin = jnp.concatenate([jnp.sin(freqs), jnp.sin(freqs)], axis=-1).astype(dtype)
            return (cos, sin)

        def _rotate_half(x):
            x1, x2 = (x[..., :x.shape[-1] // 2], x[..., x.shape[-1] // 2:])
            return jnp.concatenate([-x2, x1], axis=-1)
        b, n, c = x.shape
        scale = HD ** (-0.5)
        qkv = jnp.einsum('bnc,dc->bnd', x, w_qkv) + b_qkv
        qkv = qkv.reshape(b, n, 3, H, HD).transpose(2, 0, 3, 1, 4)
        q, k, v = (qkv[0], qkv[1], qkv[2])
        cos, sin = _rope_tables(n, HD, x.dtype)
        q = q * cos + _rotate_half(q) * sin
        k = k * cos + _rotate_half(k) * sin
        attn = jnp.einsum('bhqd,bhkd->bhqk', q, k) * scale
        attn = jax.nn.softmax(attn, axis=-1)
        out = jnp.einsum('bhqk,bhkd->bhqd', attn, v)
        out = out.transpose(0, 2, 1, 3).reshape(b, n, c)
        return jnp.einsum('bnc,dc->bnd', out, w_proj) + b_proj

    def _L0_ffn_ref(x, ln1_g, ln1_b, qkv_w, proj_w, proj_b, ln2_g, ln2_b, gate_w, gate_b, w1, b1, w2, b2):
        import jax, jax.numpy as jnp
        import numpy as np
        B, N, DIM, HEADS = (4, 256, 192, 12)
        HIDDEN, E, TOPK = (768, 8, 2)
        EPS = 1e-05

        def _layernorm(x, g, b):
            mu = jnp.mean(x, axis=-1, keepdims=True)
            var = jnp.var(x, axis=-1, keepdims=True)
            return (x - mu) * jax.lax.rsqrt(var + EPS) * g + b
        b, n, d = x.shape
        hd = d // HEADS
        scale = hd ** (-0.5)
        h = _layernorm(x, ln1_g, ln1_b)
        qkv = h @ qkv_w.T
        qkv = qkv.reshape(b, n, 3, HEADS, hd).transpose(2, 0, 3, 1, 4)
        q, k, v = (qkv[0], qkv[1], qkv[2])
        attn = jax.nn.softmax(jnp.einsum('bhnd,bhmd->bhnm', q, k) * scale, axis=-1)
        a = jnp.einsum('bhnm,bhmd->bhnd', attn, v)
        a = a.transpose(0, 2, 1, 3).reshape(b, n, d)
        a = a @ proj_w.T + proj_b
        x = x + a
        h2 = _layernorm(x, ln2_g, ln2_b)
        t = h2.reshape(-1, d)
        T = t.shape[0]
        logits = t @ gate_w.T + gate_b
        top_val, top_idx = jax.lax.top_k(logits, TOPK)
        score = jax.nn.softmax(top_val, axis=-1)
        cw = jnp.zeros((T, E), t.dtype).at[jnp.arange(T)[:, None], top_idx].add(score)
        out = jnp.zeros_like(t)
        for e in range(E):
            he = jax.nn.gelu(t @ w1[e].T + b1[e], approximate=False)
            ye = he @ w2[e].T + b2[e]
            out = out + cw[:, e:e + 1] * ye
        return x + out.reshape(b, n, d)
    h = _L0_tok_ref(x, L0_tok_W, L0_tok_b, L0_tok_class_token, L0_tok_pos_embedding)
    h = jnp.concatenate([h, _L0_txt_ref(x_txt, L0_txt_tune_ids, L0_txt_base_weight, L0_txt_train_weight)], axis=1)
    h = h + _L0_attn_ref(_layernorm(h, axis=-1), L0_attn_w_qkv, L0_attn_b_qkv, L0_attn_w_proj, L0_attn_b_proj)
    h = h + _L0_ffn_ref(_layernorm(h, axis=-1), L0_ffn_ln1_g, L0_ffn_ln1_b, L0_ffn_qkv_w, L0_ffn_proj_w, L0_ffn_proj_b, L0_ffn_ln2_g, L0_ffn_ln2_b, L0_ffn_gate_w, L0_ffn_gate_b, L0_ffn_w1, L0_ffn_b1, L0_ffn_w2, L0_ffn_b2)
    return h

_drawn_inputs = setup_inputs


def setup_inputs(seed=0):
    import zlib

    import numpy as np

    out = dict(_drawn_inputs(seed))
    spreads = {'L0_attn_b_qkv': (0.0, 0.1),
     'L0_attn_b_proj': (0.0, 0.1),
     'L0_ffn_ln1_g': (1.0, 0.6),
     'L0_ffn_ln1_b': (0.0, 0.8),
     'L0_ffn_proj_b': (0.0, 0.1),
     'L0_ffn_ln2_g': (1.0, 0.6),
     'L0_ffn_ln2_b': (0.0, 0.714),
     'L0_ffn_gate_b': (0.0, 0.28),
     'L0_ffn_b1': (0.0, 0.781),
     'L0_ffn_b2': (0.0, 0.301)}
    factors = {'L0_tok_b': 6.522, 'L0_ffn_qkv_w': 3.938, 'L0_ffn_proj_w': 3.5}
    for name, (base, spread) in spreads.items():
        noise = np.random.default_rng([zlib.crc32(name.encode()), seed]).standard_normal(out[name].shape)
        drawn = base * np.exp(spread * noise) if base else spread * noise
        out[name] = jnp.asarray(drawn.astype(out[name].dtype))
    for name, factor in factors.items():
        out[name] = (out[name] * factor).astype(out[name].dtype)
    return out
```

```python
from contextlib import ExitStack

import concourse.bass as bass
from concourse import mybir

F32 = mybir.dt.float32
F32R = mybir.dt.float32r
BF16 = mybir.dt.bfloat16
I32 = mybir.dt.int32
U32 = mybir.dt.uint32
ALU = mybir.AluOpType
ACT = mybir.ActivationFunctionType
AX_X = mybir.AxisListType.X

P = 128
BATCH, IMG, TXT = 64, 36, 32
SEQ = 1 + IMG + TXT
TOKENS = BATCH * SEQ
TILES = 36
GROUPS = TILES // 4
ROWS = TILES * P
PAD = ROWS - TOKENS
C = 192
CB = C - P
HEADS, HD = 12, 16
PATCH = 768
TUNE = 256
EPS = 1e-5
CHUNK_B = 4
CHUNK = CHUNK_B * SEQ
CHUNKS = BATCH // CHUNK_B
PARTS = 96
EXPERTS, HIDDEN, TOPK = 8, 768, 2
SLOTS = 512
REGION = TOKENS + SLOTS
MOE_TILES = (TOPK * TOKENS + EXPERTS * (SLOTS - 1)) // SLOTS
DUMP = EXPERTS * REGION


def after(eng, sem, count):
    if not isinstance(count, int) or count > 0:
        eng.wait_ge(sem, count)


def hold(eng, sem, count, turn):
    eng.wait_ge(sem, count)
    eng.sem_inc(turn, 1)


class Memory:

    def __init__(self, nc, ctx, phase):
        self.nc, self.ctx, self.phase = nc, ctx, phase + "_"
        self.sems = []
        ctx.callback(self.clear)

    def clear(self):
        if self.sems:
            self.nc.clear_and_free_semaphores(self.sems)
            self.nc.all_engine_barrier()

    def sb(self, name, shape, dt=F32):
        return self.ctx.enter_context(self.nc.sbuf_tensor(self.phase + name, shape, dt))

    def psum(self, name, shape, dt=F32):
        return self.ctx.enter_context(self.nc.psum_tensor(self.phase + name, shape, dt))

    def sem(self, name):
        self.sems.append(self.nc.alloc_semaphore(self.phase + name))
        return self.sems[-1]


def embed(nc, d, rows_d):
    with ExitStack() as ctx:
        m = Memory(nc, ctx, "emb")
        w = m.sb("tok_w", [P, 6, C])
        patch = [m.sb(f"patch{k}", [P, 6, P]) for k in range(2)]
        place = m.sb("place", [P, IMG // 2, C])
        bias = m.sb("tok_bias", [P, C])
        emb = [m.sb(f"emb{k}", [P, C]) for k in range(2)]
        cls = m.sb("cls", [BATCH, 2, C])
        zero = m.sb("zero", [P, C])
        ids = m.sb("ids", [P, 16], I32)
        idf = m.sb("idf", [P, 16])
        tune = m.sb("tune", [P, TUNE], I32)
        tunef = m.sb("tunef", [P, TUNE])
        number = m.sb("number", [P, TUNE])
        hit = m.sb("hit", [P, 16, TUNE])
        last = m.sb("last", [P, 16])
        mask = m.sb("mask", [P, 16])
        keep = m.sb("keep", [P, 16])
        rowf = m.sb("rowf", [P, 16])
        row = m.sb("row", [P, 16], I32)
        base = m.sb("base", [P, 16, C])
        train = m.sb("train", [P, 16, C])
        acc = [m.psum(f"emb_acc{k}", [P, 512]) for k in range(2)]
        w_in, place_in, cls_in, ids_in = (m.sem(x) for x in ("w_in", "place_in", "cls_in", "ids_in"))
        patch_in = [m.sem(f"patch_in{k}") for k in range(2)]
        place_done, cls_done, zero_done = m.sem("place_done"), m.sem("cls_done"), m.sem("zero_done")
        acc_done, emb_done = m.sem("acc_done"), m.sem("emb_done")
        stored = [m.sem(f"stored{k}") for k in range(2)]
        text = m.sem("text_step")
        row_done, base_in, train_in, text_done, rest = (
            m.sem(x) for x in ("row_done", "base_in", "train_in", "text_done", "rest_stored"))
        token = rows_d[0:TOKENS, :].rearrange("(b s) c -> b s c", s=SEQ)

        with nc.Block() as block:
            @block.sync
            def _(sp):
                sp.dma_start(w[:, :, :], d["tok_wT"].rearrange("(k p) c -> p k c", p=P)).then_inc(w_in, 16)

                def load(t, k):
                    sp.dma_start(patch[k][:, :, :].rearrange("p k n -> p (k n)"),
                                 d["patches"][bass.ds(t, 1)].rearrange("a p n -> (a p) n")).then_inc(patch_in[k], 16)

                load(0, 0)
                load(9, 1)
                for half in range(2):
                    sp.dma_start(place[64 * half:64 * half + 64, :, :],
                                 d["pos"][1 + half:1 + half + 35:2, :].partition_broadcast(64)).then_inc(place_in, 16)
                sp.dma_start(bias[:, :], d["tok_b"].partition_broadcast(P)).then_inc(place_in, 16)
                sp.dma_start(cls[:, 0, :], d["cls"][0:1, :].rearrange("a c -> (a c)").partition_broadcast(BATCH)).then_inc(cls_in, 16)
                sp.dma_start(cls[:, 1, :], d["pos"][0:1, :].rearrange("a c -> (a c)").partition_broadcast(BATCH)).then_inc(cls_in, 16)

                def store(t, k, n):
                    sp.wait_ge(emb_done, n)
                    for half in range(2):
                        sp.dma_start(token[:, bass.ds(2 * t + 1 + half, 1), :].rearrange("b a c -> b (a c)"),
                                     emb[k][64 * half:64 * half + 64, :]).then_inc(stored[k], 16)

                with sp.Fori(0, 8) as i:
                    for k in range(2):
                        sp.wait_ge(acc_done, 2 * i + 1 + k)
                        load(i + 1 + 9 * k, k)
                    for k in range(2):
                        store(i + 9 * k, k, 2 * i + 1 + k)
                for k in range(2):
                    store(8 + 9 * k, k, 17 + k)
                sp.wait_ge(stored[0], 16 * 18)
                sp.wait_ge(stored[1], 16 * 18)

            @block.scalar
            def _(act):
                act.dma_start(ids[:, :], d["ids"]).then_inc(ids_in, 16)
                act.dma_start(tune[:, :], d["tune_ids"].partition_broadcast(P)).then_inc(ids_in, 16)
                act.dma_start(number[:, :], d["number"]).then_inc(ids_in, 16)
                act.wait_ge(zero_done, 1)
                act.dma_start(rows_d[TOKENS:TOKENS + P, :], zero[:, :]).then_inc(rest, 16)
                act.dma_start(rows_d[TOKENS + P:ROWS, :], zero[0:PAD - P, :]).then_inc(rest, 16)
                act.wait_ge(cls_done, 1)
                act.dma_start(token[:, 0, :], cls[:, 0, :]).then_inc(rest, 16)
                act.wait_ge(text_done, 1)
                for half in range(2):
                    act.dma_start(token[:, 1 + IMG + half::2, :], base[64 * half:64 * half + 64, :, :]).then_inc(rest, 16)
                act.wait_ge(rest, 16 * 5)

            @block.gpsimd
            def _(pool):
                pool.wait_ge(ids_in, 48)
                for j in range(16):
                    pool.indirect_dma_start(base[:, j, :], None, d["base_w"],
                                            bass.IndirectOffsetOnAxis(ids[:, j:j + 1], 0)).then_inc(base_in, 16)
                pool.wait_ge(row_done, 1)
                for j in range(16):
                    pool.indirect_dma_start(train[:, j, :], None, d["train_w"],
                                            bass.IndirectOffsetOnAxis(row[:, j:j + 1], 0)).then_inc(train_in, 16)

            @block.tensor
            def _(pe):
                pe.wait_ge(w_in, 16)

                def tile(k, loads, n):
                    pe.wait_ge(patch_in[k], 16 * loads)
                    after(pe, emb_done, n)
                    for s in range(6):
                        mm = pe.matmul(acc[k][:, 0:C], patch[k][:, s, :], w[:, s, :], start=(s == 0), stop=(s == 5))
                    mm.then_inc(acc_done, 1)

                for k in range(2):
                    tile(k, 1, 0)
                with pe.Fori(1, 9) as i:
                    for k in range(2):
                        tile(k, i + 1, 2 * i - 1 + k)

            @block.vector
            def _(dve):
                dve.memset(zero[:, :], 0.0).then_inc(zero_done, 1)
                dve.wait_ge(cls_in, 32)
                dve.tensor_tensor(cls[:, 0, :], cls[:, 0, :], cls[:, 1, :], ALU.add).then_inc(cls_done, 1)
                dve.wait_ge(ids_in, 48)
                dve.tensor_copy(idf[:, :], ids[:, :]).then_inc(text, 1)
                dve.tensor_copy(tunef[:, :], tune[:, :]).then_inc(text, 1)
                dve.wait_ge(text, 2)
                wide = [P, 16, TUNE]
                dve.tensor_tensor(hit[:, :, :], tunef[:, :].unsqueeze(1).to_broadcast(wide),
                                  idf[:, :].unsqueeze(2).to_broadcast(wide), ALU.is_equal).then_inc(text, 1)
                dve.wait_ge(text, 3)
                dve.tensor_tensor(hit[:, :, :], hit[:, :, :], number[:, :].unsqueeze(1).to_broadcast(wide),
                                  ALU.mult).then_inc(text, 1)
                dve.wait_ge(text, 4)
                dve.tensor_reduce(last[:, :], hit[:, :, :], AX_X, ALU.max).then_inc(text, 1)
                dve.wait_ge(text, 5)
                dve.tensor_scalar(mask[:, :], last[:, :], 0.5, None, ALU.is_gt).then_inc(text, 1)
                dve.tensor_scalar(keep[:, :], last[:, :], 0.5, None, ALU.is_lt).then_inc(text, 1)
                dve.tensor_scalar(rowf[:, :], last[:, :], -1.0, 0.0, ALU.add, ALU.max).then_inc(text, 1)
                dve.wait_ge(text, 8)
                dve.tensor_copy(row[:, :], rowf[:, :]).then_inc(row_done, 1)
                dve.wait_ge(place_in, 48)
                dve.tensor_tensor(place[:, :, :], place[:, :, :],
                                  bias[:, :].unsqueeze(1).to_broadcast([P, IMG // 2, C]), ALU.add).then_inc(place_done, 1)
                dve.wait_ge(place_done, 1)

                def tile(t, k, n, stores):
                    dve.wait_ge(acc_done, n)
                    after(dve, stored[k], stores)
                    dve.tensor_tensor(emb[k][:, :], acc[k][:, 0:C],
                                      place[:, bass.ds(t, 1), :].rearrange("p a c -> p (a c)"),
                                      ALU.add).then_inc(emb_done, 1)

                for k in range(2):
                    tile(9 * k, k, 1 + k, 0)
                with dve.Fori(1, 9) as i:
                    for k in range(2):
                        tile(i + 9 * k, k, 2 * i + 1 + k, 32 * i)
                dve.wait_ge(base_in, 256)
                wide = [P, 16, C]
                dve.tensor_tensor(base[:, :, :], base[:, :, :], keep[:, :].unsqueeze(2).to_broadcast(wide), ALU.mult).then_inc(text, 1)
                dve.wait_ge(train_in, 256)
                dve.tensor_tensor(train[:, :, :], train[:, :, :], mask[:, :].unsqueeze(2).to_broadcast(wide), ALU.mult).then_inc(text, 1)
                dve.wait_ge(text, 10)
                dve.tensor_tensor(base[:, :, :], base[:, :, :], train[:, :, :], ALU.add).then_inc(text_done, 1)


class NormGroup:

    def __init__(self, m, name):
        self.stats = m.sb(name + "_stats", [P, 4, 6])
        self.mv = m.sb(name + "_mv", [P, 4, 2])
        self.inv = m.sb(name + "_inv", [P, 4])
        self.rstd = m.sb(name + "_rstd", [P, 4])
        self.stat_done, self.mv_done, self.eps_done, self.inv_done, self.rstd_done, self.turn = (
            m.sem(f"{name}_{x}") for x in ("stat", "mv", "eps", "inv", "rstd", "turn"))


def norm_stats(dve, n, rows, g, ready=None):
    if ready:
        hold(dve, ready, 4 * g, n.turn)
    for k in range(4):
        dve.bn_stats(n.stats[:, k, :], rows[k]).then_inc(n.stat_done, 1)
    hold(dve, n.stat_done, 4 * g, n.turn)
    for k in range(4):
        dve.bn_aggr(n.mv[:, k, :], n.stats[:, k, :]).then_inc(n.mv_done, 1)
    dve.wait_ge(n.mv_done, 4 * g)
    dve.tensor_scalar(n.inv[:, :], n.mv[:, :, 1], EPS, None, ALU.add).then_inc(n.eps_done, 1)
    dve.wait_ge(n.eps_done, g)
    dve.reciprocal(n.inv[:, :], n.inv[:, :]).then_inc(n.inv_done, 1)


def norm_root(act, n, g):
    act.wait_ge(n.inv_done, g)
    act.activation(n.rstd[:, :], n.inv[:, :], ACT.Sqrt).then_inc(n.rstd_done, 1)


def norm_apply(dve, n, outs, rows, g, done):
    dve.wait_ge(n.rstd_done, g)
    for k in range(4):
        dve.tensor_scalar(outs[k], rows[k], n.mv[:, k, 0:1], n.rstd[:, k:k + 1],
                          ALU.subtract, ALU.mult).then_inc(done, 1)


def cols(x, start, n):
    return x[:, bass.ds(start, n)]


def tile_of(x, t):
    return x[:, bass.ds(t, 1), :].rearrange("p a c -> p (a c)")


def first_norm(nc, d, rows_d, h, xa_all, xb_all):
    with ExitStack() as ctx:
        m = Memory(nc, ctx, "norm")
        ident = m.sb("ident", [P, P])
        xn = [m.sb(f"xn{k}", [P, C]) for k in range(4)]
        n = NormGroup(m, "n0")
        ta = m.psum("ta", [P, 512])
        tb = m.psum("tb", [P, 512])
        rows_in = [m.sem(f"rows_in{g}") for g in range(GROUPS)]
        ident_in, xn_done, t_done, ta_out, tb_out = (
            m.sem(x) for x in ("ident_in", "xn_done", "t_done", "ta_out", "tb_out"))
        all_in = m.sem("all_in")
        with nc.Block() as block:
            @block.sync
            def _(sp):
                sp.dma_start(ident[:, :], d["ident"]).then_inc(ident_in, 16)
                for g in range(GROUPS):
                    sp.dma_start(h[:, 4 * g:4 * g + 4, :],
                                 rows_d[512 * g:512 * g + 512, :].rearrange("(t p) c -> p t c", p=P)).then_inc(rows_in[g], 16)
                for g in range(GROUPS):
                    sp.wait_ge(rows_in[g], 16)
                    sp.sem_inc(all_in, 1)

            @block.vector
            def _(dve):
                def group(g):
                    hold(dve, all_in, g + 1, n.turn)
                    rows = [tile_of(h, 4 * g + k) for k in range(4)]
                    norm_stats(dve, n, rows, g + 1)
                    after(dve, t_done, g)
                    norm_apply(dve, n, [x[:, :] for x in xn], rows, g + 1, xn_done)
                    dve.wait_ge(t_done, g + 1)
                    dve.tensor_copy(cols(xb_all, 512 * g, 512), tb[0:CB, :]).then_inc(tb_out, 1)

                group(0)
                with dve.Fori(1, GROUPS) as g:
                    group(g)

            @block.scalar
            def _(act):
                def group(g):
                    norm_root(act, n, g + 1)
                    act.wait_ge(t_done, g + 1)
                    act.activation(cols(xa_all, 512 * g, 512), ta[:, :], ACT.Copy).then_inc(ta_out, 1)

                group(0)
                with act.Fori(1, GROUPS) as g:
                    group(g)

            @block.tensor
            def _(pe):
                pe.wait_ge(ident_in, 16)

                def group(g):
                    after(pe, ta_out, g)
                    after(pe, tb_out, g)
                    for k in range(4):
                        pe.wait_ge(xn_done, 4 * g + k + 1)
                        pe.transpose(ta[:, P * k:P * k + P], xn[k][:, 0:P], ident[:, :])
                        mm = pe.transpose(tb[0:CB, P * k:P * k + P], xn[k][:, P:C], ident[:, :])
                    mm.then_inc(t_done, 1)

                group(0)
                with pe.Fori(1, GROUPS) as g:
                    group(g)


VALUE_AT = {0: 0, 1: 1, 5: 2, 6: 3}
QK_AT = {2: 0, 3: 1, 4: 2}


def projections(c, step, full):
    order = [s for s in range(8) if s in VALUE_AT or (full and s in QK_AT)]
    return 10 + 7 * c + order.index(step)


def attention(nc, d, parts_d, xa_all, xb_all, ot_all, w_name, bias_name, rope):
    with ExitStack() as ctx:
        m = Memory(nc, ctx, w_name)
        kb = CB + 1 if bias_name else CB
        wa = m.sb("wa", [P, 3 * C])
        wb = m.sb("wb", [kb, 3 * C])
        xa = [m.sb(f"xa{k}", [P, CHUNK]) for k in range(2)]
        xb = [m.sb(f"xb{k}", [kb, CHUNK]) for k in range(2)]
        qk = m.sb("qk", [P, 3, CHUNK])
        rest = m.sb("rest", [P, 3, CHUNK])
        part = [m.sb(f"part{k}", [P, 3, CHUNK], BF16) for k in range(3)]
        qs = [m.sb(f"qs{k}", [PARTS, HEADS, CHUNK], BF16) for k in range(2)]
        ks = [m.sb(f"ks{k}", [PARTS, HEADS, CHUNK], BF16) for k in range(2)]
        vp = [m.sb(f"vp{k}", [SEQ, CHUNK_B, HEADS, 2 * HD]) for k in range(2)]
        pt = [m.sb(f"pt{k}", [SEQ, 6, SEQ]) for k in range(2)]
        nm = [m.sb(f"nm{k}", [SEQ, HEADS]) for k in range(2)]
        nmr = [m.sb(f"nmr{k}", [SEQ, HEADS]) for k in range(2)]
        ms = [m.sb(f"ms{k}", [SEQ, 3, HEADS], BF16) for k in range(2)]
        mt = [m.sb(f"mt{k}", [PARTS, SEQ], BF16) for k in range(2)]
        pick1 = m.sb("pick1", [PARTS, HEADS])
        pick = m.sb("pick", [PARTS, HEADS, SEQ], BF16)
        identf = m.sb("identf", [P, P])
        identb = m.sb("identb", [P, P], BF16)
        rec = m.sb("rec", [P, 3, SEQ])
        if rope:
            swapped = m.sb("swapped", [P, 3, CHUNK])
            cos = m.sb("cos", [P, CHUNK])
            sin = m.sb("sin", [P, CHUNK])
        s_ps = [m.psum(f"s_ps{k}", [P, 512]) for k in range(2)]
        st_ps = [m.psum(f"st_ps{k}", [P, 512]) for k in range(2)]
        o_ps = [m.psum(f"o_ps{k}", [P, 512]) for k in range(2)]
        proj_ps = m.psum("proj_ps", [P, 512])
        mt_ps = m.psum("mt_ps", [P, 1024], BF16)

        const_in, const_done = m.sem("const_in"), m.sem("const_done")
        x_in = [m.sem(f"x_in{k}") for k in range(2)]
        proj_done, proj_out = m.sem("proj_done"), m.sem("proj_out")
        swap_done, cos_done, sin_done, rope_done = (m.sem(x) for x in ("swap", "cos_mul", "sin_mul", "rope"))
        p1_done, r1_done, p2_done, p3_done = (m.sem(x) for x in ("p1", "r1", "p2", "p3"))
        stack_in = [m.sem(f"stack_in{k}") for k in range(2)]
        parts_out = [m.sem(f"parts_out{k}") for k in range(3)]
        s_done, max_done, msplit, mt_done, mt_out = (m.sem(x) for x in ("s_done", "max_done", "msplit", "mt_done", "mt_out"))
        st_done, exp_done, pv_done = m.sem("st_done"), m.sem("exp_done"), m.sem("pv_done")
        dve_turn, pe_turn, sp_turn = (m.sem(x) for x in ("dve_turn", "pe_turn", "sp_turn"))
        den_done, rec_done, norm_done = m.sem("den_done"), m.sem("rec_done"), m.sem("norm_done")
        N_CONST = 4 + (1 if bias_name else 0) + (2 if rope else 0)
        N_STACK = 16 * 2 * (PARTS // HD)
        N_DONE = 7 + (2 if bias_name else 0)

        def load_x(eng, i, k):
            start = CHUNK * (2 * i + k)
            eng.dma_start(xa[k][:, :], cols(xa_all, start, CHUNK)).then_inc(x_in[k], 16)
            eng.dma_start(xb[k][0:CB, :], cols(xb_all, start, CHUNK)).then_inc(x_in[k], 16)

        def run(eng_fori, pair):
            pair(0, False)
            with eng_fori(1, CHUNKS // 2 - 1) as i:
                pair(i, False)
            pair(CHUNKS // 2 - 1, True)

        with nc.Block() as block:
            @block.sync
            def _(sp):
                sp.dma_start(wa[:, :], d[w_name][0:P, :]).then_inc(const_in, 16)
                sp.dma_start(wb[0:CB, :], d[w_name][P:C, :]).then_inc(const_in, 16)
                if bias_name:
                    sp.dma_start(wb[CB:CB + 1, :], d[bias_name].rearrange("(a n) -> a n", a=1)).then_inc(const_in, 16)
                sp.dma_start(pick1[:, :], d["pick"]).then_inc(const_in, 16)
                sp.dma_start(identf[:, :], d["ident"]).then_inc(const_in, 16)
                load_x(sp, 0, 0)
                load_x(sp, 0, 1)
                if rope:
                    sp.dma_start(cos[:, :], d["cos"]).then_inc(const_in, 16)
                    sp.dma_start(sin[:, :], d["sin"]).then_inc(const_in, 16)

                def stack(i, k, used):
                    c = 2 * i + k
                    if not isinstance(i, int) or i:
                        hold(sp, stack_in[k], N_STACK * i, sp_turn)
                    for n, made in enumerate((p1_done, p2_done, p3_done)):
                        sp.wait_ge(made, c + 1)
                        for a in range(2):
                            sp.dma_start(parts_d[k, n, a].rearrange("(m p) t -> p m t", p=CB),
                                         part[n][CB * a:CB * a + CB, :, :]).then_inc(parts_out[n], 16)
                    for n in range(3):
                        hold(sp, parts_out[n], 32 * (c + 1), sp_turn)
                    after(sp, st_done, used)
                    for a, dst, which in ((0, qs[k], (0, 0, 1, 1, 0, 2)), (1, ks[k], (0, 1, 0, 1, 2, 0))):
                        for r, n in enumerate(which):
                            sp.dma_start(dst[HD * r:HD * r + HD, :, :],
                                         parts_d[k, n, a].rearrange("(h e) t -> e h t", e=HD)).then_inc(stack_in[k], 16)

                stack(0, 0, 0)

                def chunk(i, k, full, more):
                    c = 2 * i + k
                    if full:
                        sp.wait_ge(proj_done, 10 + 7 * c)
                        load_x(sp, i + 1, k)
                    if more:
                        stack(*((i, 1) if k == 0 else (i + 1, 0)), 8 * c)

                def pair(i, last):
                    for k in range(2):
                        chunk(i, k, not last, not (last and k == 1))

                run(sp.Fori, pair)

            @block.scalar
            def _(act):
                def project_out_qk(n, j, chunk_no):
                    act.wait_ge(proj_done, n + 1)
                    if j == 0:
                        after(act, r1_done, chunk_no)
                    act.activation(qk[:, j, :], proj_ps[:, 0:CHUNK], ACT.Copy).then_inc(proj_out, 1)

                def project_out_v(n, k, b, used):
                    act.wait_ge(proj_done, n + 1)
                    after(act, pv_done, used)
                    act.activation(vp[k][:, b, :, 0:HD], proj_ps[0:SEQ, 0:C].rearrange("p (h e) -> p h e", e=HD),
                                   ACT.Copy).then_inc(proj_out, 1)

                def part1(i, k):
                    if rope:
                        act.wait_ge(rope_done, 2 * i + k + 1)
                    after(act, parts_out[0], 32 * (2 * i + k))
                    act.activation(part[0][:, :, :], qk[:, :, :], ACT.Copy).then_inc(p1_done, 1)

                def part2(i, k):
                    act.wait_ge(r1_done, 2 * i + k + 1)
                    after(act, parts_out[1], 32 * (2 * i + k))
                    act.activation(part[1][:, :, :], rest[:, :, :], ACT.Copy).then_inc(p2_done, 1)

                act.wait_ge(const_done, N_DONE)
                for n in range(3):
                    project_out_qk(n, n, 0)
                if not rope:
                    act.wait_ge(proj_out, 3)
                part1(0, 0)
                for b in range(4):
                    project_out_v(3 + b, 0, b, 0)
                part2(0, 0)
                for n in range(3):
                    project_out_qk(7 + n, n, 1)
                if not rope:
                    act.wait_ge(proj_out, 10)
                part1(0, 1)
                part2(0, 1)

                def chunk(i, k, first, full, more):
                    c = 2 * i + k
                    for s in range(8):
                        g = 8 * c + s
                        if s % 2 == 0:
                            b_no = 4 * c + s // 2
                            act.wait_ge(mt_done, b_no + 1)
                            after(act, st_done, 2 * b_no - 2)
                            act.activation(mt[s // 2 % 2][0:3 * HEADS, :], mt_ps[0:3 * HEADS, 0:SEQ], ACT.Copy).then_inc(mt_out, 1)
                        act.wait_ge(st_done, g + 1)
                        after(act, pv_done, g - 1)
                        act.activation(pt[s % 2][:, :, :],
                                       st_ps[s % 2][0:SEQ, 0:6 * SEQ].rearrange("p (h t) -> p h t", t=SEQ),
                                       ACT.Exp, scale=HD ** -0.5).then_inc(exp_done, 1)
                        if more and s in VALUE_AT:
                            project_out_v(projections(c, s, full), 1 - k, VALUE_AT[s], 8 * c)
                        if full and s in QK_AT:
                            project_out_qk(projections(c, s, full), QK_AT[s], c + 2)
                        if s == 1 and more and not first:
                            part2(*((i, 1) if k == 0 else (i + 1, 0)))
                        if s == 7 and full:
                            if not rope:
                                act.wait_ge(proj_out, projections(c, 4, full) + 1)
                            part1(i + 1, k)

                def pair(i, last):
                    for k in range(2):
                        chunk(i, k, isinstance(i, int) and i == 0 and k == 0, not last, not (last and k == 1))

                run(act.Fori, pair)

            @block.gpsimd
            def _(pool):
                pool.memset(vp[0][:, :, :, HD:], 1.0).then_inc(const_done, 1)
                pool.memset(vp[1][:, :, :, HD:], 1.0).then_inc(const_done, 1)
                pool.memset(ot_all[:, :, TOKENS:ROWS], 0.0).then_inc(const_done, 1)
                pool.wait_ge(const_in, 16 * N_CONST)

                def chunk(i, k):
                    c = 2 * i + k
                    ready = 10 + 7 * (c - 2) + 5
                    if isinstance(c, int) and c < 2:
                        ready = (3, 10)[c]
                    after(pool, p3_done, c)
                    if rope:
                        pool.wait_ge(proj_out, ready)
                        pool.tensor_tensor(rest[:, :, :], qk[:, :, :], cos[:, :].unsqueeze(1).to_broadcast([P, 3, CHUNK]),
                                           ALU.mult).then_inc(cos_done, 1)
                        pool.wait_ge(rope_done, c + 1)
                    pool.wait_ge(p1_done, c + 1)
                    pool.tensor_tensor(rest[:, :, :], qk[:, :, :], part[0][:, :, :], ALU.subtract).then_inc(r1_done, 1)
                    pool.wait_ge(p2_done, c + 1)
                    after(pool, parts_out[2], 32 * c)
                    pool.tensor_tensor(part[2][:, :, :], rest[:, :, :], part[1][:, :, :], ALU.subtract).then_inc(p3_done, 1)

                chunk(0, 0)
                chunk(0, 1)
                with pool.Fori(1, CHUNKS // 2) as i:
                    for k in range(2):
                        chunk(i, k)

            @block.vector
            def _(dve):
                if bias_name:
                    for k in range(2):
                        dve.memset(xb[k][CB:CB + 1, :], 1.0).then_inc(const_done, 1)
                for k in range(2):
                    dve.memset(mt[k][:, :], 0.0).then_inc(const_done, 1)
                dve.wait_ge(const_in, 16 * N_CONST)
                dve.tensor_copy(identb[:, :], identf[:, :]).then_inc(const_done, 1)
                dve.tensor_copy(pick[:, :, :], pick1[:, :].unsqueeze(2).to_broadcast([PARTS, HEADS, SEQ])).then_inc(const_done, 1)

                def rope_swap(c, ready):
                    after(dve, rope_done, c)
                    hold(dve, proj_out, ready, dve_turn)
                    dve.stream_shuffle(swapped[:, :, :], qk[:, :, :], [l ^ 8 for l in range(32)]).then_inc(swap_done, 1)

                def rope_add(c):
                    dve.wait_ge(swap_done, c + 1)
                    dve.tensor_tensor(swapped[:, :, :], swapped[:, :, :], sin[:, :].unsqueeze(1).to_broadcast([P, 3, CHUNK]),
                                      ALU.mult).then_inc(sin_done, 1)
                    dve.wait_ge(sin_done, c + 1)
                    dve.wait_ge(cos_done, c + 1)
                    dve.tensor_tensor(qk[:, :, :], swapped[:, :, :], rest[:, :, :], ALU.add).then_inc(rope_done, 1)

                def negmax(g, par):
                    dve.wait_ge(s_done, g + 1)
                    half, b2 = par
                    dve.tensor_reduce(nm[b2][:, 6 * half:6 * half + 6],
                                      s_ps[half][0:SEQ, 0:6 * SEQ].rearrange("p (h t) -> p h t", t=SEQ),
                                      AX_X, ALU.max, negate=True).then_inc(max_done, 1)

                def split_max(b_no, b2):
                    x, r, s = nm[b2], nmr[b2], ms[b2]
                    dve.wait_ge(max_done, 2 * b_no + 2)
                    after(dve, mt_done, b_no - 1)
                    dve.tensor_copy(s[:, 0, :], x[:, :]).then_inc(msplit, 1)
                    dve.wait_ge(msplit, 4 * b_no + 1)
                    dve.tensor_tensor(r[:, :], x[:, :], s[:, 0, :], ALU.subtract).then_inc(msplit, 1)
                    dve.wait_ge(msplit, 4 * b_no + 2)
                    dve.tensor_copy(s[:, 1, :], r[:, :]).then_inc(msplit, 1)
                    dve.wait_ge(msplit, 4 * b_no + 3)
                    dve.tensor_tensor(s[:, 2, :], r[:, :], s[:, 1, :], ALU.subtract).then_inc(msplit, 1)

                def normalize(b_no, b2):
                    after(dve, norm_done, b_no)
                    hold(dve, pv_done, 2 * b_no + 2, dve_turn)
                    o = o_ps[b2][:, 0:3 * SEQ].rearrange("p (g t) -> p g t", t=SEQ)
                    dve.stream_shuffle(rec[:, :, :], o, [HD + l % HD for l in range(32)]).then_inc(den_done, 1)
                    dve.wait_ge(den_done, b_no + 1)
                    dve.reciprocal(rec[:, :, :], rec[:, :, :]).then_inc(rec_done, 1)
                    dve.wait_ge(rec_done, b_no + 1)
                    dve.tensor_tensor(ot_all[:, :, bass.ds(b_no * SEQ, SEQ)], o, rec[:, :, :], ALU.mult).then_inc(norm_done, 1)

                if rope:
                    rope_swap(0, 3)
                    rope_add(0)
                    rope_swap(1, 10)
                    rope_add(1)
                negmax(0, (0, 0))
                negmax(1, (1, 0))
                split_max(0, 0)
                negmax(2, (0, 1))

                def chunk(i, k, first, full, more):
                    c = 2 * i + k
                    for s in range(8):
                        g = 8 * c + s
                        if more or s < 5:
                            negmax(g + 3, ((s + 1) % 2, (s + 3) // 2 % 2))
                            if s % 2 == 0:
                                split_max(4 * c + s // 2 + 1, (s // 2 + 1) % 2)
                        if s % 2 == 0 and not (first and s == 0):
                            normalize(4 * c + s // 2 - 1, (s // 2 + 1) % 2)
                        if rope and full:
                            if s == 5:
                                rope_swap(c + 2, projections(c, 4, full) + 1)
                            if s == 6:
                                rope_add(c + 2)

                def pair(i, last):
                    for k in range(2):
                        chunk(i, k, isinstance(i, int) and i == 0 and k == 0, not last, not (last and k == 1))

                run(dve.Fori, pair)
                normalize(BATCH - 1, 1)
                dve.wait_ge(norm_done, BATCH)

            @block.tensor
            def _(pe):
                def project_qk(n, k, j, loads):
                    pe.wait_ge(x_in[k], 32 * loads)
                    after(pe, proj_out, n)
                    w = slice(P * j, P * j + P)
                    pe.matmul(proj_ps[:, 0:CHUNK], wa[:, w], xa[k][:, :], start=True, stop=False)
                    pe.matmul(proj_ps[:, 0:CHUNK], wb[:, w], xb[k][:, :], start=False, stop=True).then_inc(proj_done, 1)

                def project_v(n, k, b, loads):
                    pe.wait_ge(x_in[k], 32 * loads)
                    after(pe, proj_out, n)
                    t = slice(SEQ * b, SEQ * b + SEQ)
                    pe.matmul(proj_ps[0:SEQ, 0:C], xa[k][:, t], wa[:, 2 * C:3 * C], start=True, stop=False)
                    pe.matmul(proj_ps[0:SEQ, 0:C], xb[k][:, t], wb[:, 2 * C:3 * C], start=False, stop=True).then_inc(proj_done, 1)

                def score(g, i, k, b, half):
                    if b == 0 and half == 0:
                        pe.wait_ge(stack_in[k], N_STACK * (i + 1))
                    after(pe, max_done, g - 1)
                    for j in range(6):
                        t = slice(SEQ * b, SEQ * b + SEQ)
                        mm = pe.matmul(s_ps[half][0:SEQ, SEQ * j:SEQ * j + SEQ], qs[k][:, 6 * half + j, t],
                                       ks[k][:, 6 * half + j, t], start=True, stop=True)
                    mm.then_inc(s_done, 1)

                pe.wait_ge(const_in, 16 * N_CONST)
                pe.wait_ge(const_done, N_DONE)
                for j in range(3):
                    project_qk(j, 0, j, 1)
                for b in range(4):
                    project_v(3 + b, 0, b, 1)
                for j in range(3):
                    project_qk(7 + j, 1, j, 1)
                for g in range(3):
                    score(g, 0, 0, g // 2, g % 2)

                def values(c, k, b, half):
                    b_no, b2 = 4 * c + b, b % 2
                    pe.wait_ge(exp_done, 2 * b_no + half + 1)
                    if half == 0:
                        after(pe, norm_done, b_no - 1)
                    for j in range(6):
                        head = 6 * half + j
                        lane = 2 * HD * (head % 4)
                        col = SEQ * (head // 4)
                        mm = pe.matmul(o_ps[b2][lane:lane + 2 * HD, col:col + SEQ], vp[k][:, b, head, :],
                                       pt[half][:, j, :], start=True, stop=True, tile_position=(0, lane))
                    mm.then_inc(pv_done, 1)

                def chunk(i, k, first, full, more):
                    c = 2 * i + k
                    for s in range(8):
                        g = 8 * c + s
                        b_no, b, half, b2 = 4 * c + s // 2, s // 2, s % 2, s // 2 % 2
                        if half == 0:
                            after(pe, mt_out, b_no)
                            hold(pe, msplit, 4 * b_no + 4, pe_turn)
                            pe.transpose(mt_ps[0:3 * HEADS, 0:SEQ], ms[b2][:, :, :].rearrange("p a h -> p (a h)"),
                                         identb[0:SEQ, 0:SEQ]).then_inc(mt_done, 1)
                        if more or s < 5:
                            ahead = (i, k) if s < 5 else ((i, 1) if k == 0 else (i + 1, 0))
                            score(g + 3, *ahead, (s + 3) // 2 % 4, (s + 3) % 2)
                        if more and s in VALUE_AT:
                            project_v(projections(c, s, full), 1 - k, VALUE_AT[s], i + 1 + k)
                        if full and s in QK_AT:
                            project_qk(projections(c, s, full), k, QK_AT[s], i + 2)
                        if half == 0:
                            pe.wait_ge(mt_out, b_no + 1)
                        after(pe, exp_done, g - 1)
                        t = slice(SEQ * b, SEQ * b + SEQ)
                        for j in range(6):
                            o = st_ps[half][0:SEQ, SEQ * j:SEQ * j + SEQ]
                            pe.matmul(o, ks[k][:, 6 * half + j, t], qs[k][:, 6 * half + j, t], start=True, stop=False)
                            mm = pe.matmul(o, pick[:, 6 * half + j, :], mt[b2][:, :], start=False, stop=True)
                        mm.then_inc(st_done, 1)
                        if not (first and s == 0):
                            if s == 0:
                                values(c - 1, 1 - k, 3, 1)
                            else:
                                values(c, k, (s - 1) // 2, (s - 1) % 2)

                def pair(i, last):
                    for k in range(2):
                        chunk(i, k, isinstance(i, int) and i == 0 and k == 0, not last, not (last and k == 1))

                run(pe.Fori, pair)
                values(CHUNKS - 1, 1, 3, 1)



def load_heads(sp, ots, ots_in, acc_done, ot_all, g):
    for k in range(4):
        after(sp, acc_done, 4 * g - 3 + k if not isinstance(g, int) or g else 0)
        sp.dma_start(ots[k][:, :, :], ot_all[:, :, bass.ds(512 * g + P * k, P)]).then_inc(ots_in[k], 16)


def project_heads(pe, ots, ots_in, acc, acc_done, wp, g, acc_used):
    for k in range(4):
        pe.wait_ge(ots_in[k], 16 * (g + 1))
        after(pe, acc_used, 4 * g - 3 + k if not isinstance(g, int) or g else 0)
        for s in range(3):
            mm = pe.matmul(acc[k][:, 0:C], ots[k][:, s, :], wp[:, s, :], start=(s == 0), stop=(s == 2))
        mm.then_inc(acc_done, 1)


def groups(fori, group):
    group(0)
    with fori(1, GROUPS) as g:
        group(g)


def between(nc, d, h, ot_all, xa_all, xb_all, kept_d):
    with ExitStack() as ctx:
        m = Memory(nc, ctx, "mid")
        ident = m.sb("ident", [P, P])
        wp = m.sb("wp", [P, 3, C])
        bias = m.sb("proj_bias", [P, C])
        gain = m.sb("gain", [P, 4])
        ots = [m.sb(f"ots{k}", [P, 3, P]) for k in range(4)]
        hp = m.sb("hp", [P, 4, C])
        xn = [m.sb(f"xn{k}", [P, C]) for k in range(4)]
        n1, n2 = NormGroup(m, "n1"), NormGroup(m, "n2")
        acc = [m.psum(f"acc{k}", [P, 512]) for k in range(4)]
        ta = m.psum("ta", [P, 512])
        tb = m.psum("tb", [P, 512])
        const_in = m.sem("const_in")
        ots_in = [m.sem(f"ots_in{k}") for k in range(4)]
        acc_done, bias_done, hp_done, kept, y_done, xn_done, t_done, t_out = (
            m.sem(x) for x in ("acc_done", "bias_done", "hp_done", "kept", "y_done", "xn_done", "t_done", "t_out"))
        with nc.Block() as block:
            @block.sync
            def _(sp):
                sp.dma_start(ident[:, :], d["ident"]).then_inc(const_in, 16)
                sp.dma_start(wp[:, :, :], d["proj1_w"]).then_inc(const_in, 16)
                sp.dma_start(bias[:, :], d["proj1_b"].partition_broadcast(P)).then_inc(const_in, 16)
                for j, name in enumerate(("ln1_g", "ln1_b")):
                    sp.dma_start(gain[:, j:j + 1], d[name][0:P].rearrange("(p a) -> p a", a=1)).then_inc(const_in, 16)
                    sp.dma_start(gain[0:CB, 2 + j:3 + j], d[name][P:C].rearrange("(p a) -> p a", a=1)).then_inc(const_in, 16)
                load_heads(sp, ots, ots_in, acc_done, ot_all, 0)

                def group(g, last=False):
                    if not last:
                        load_heads(sp, ots, ots_in, acc_done, ot_all, g + 1)
                    sp.wait_ge(hp_done, 4 * g + 4)
                    sp.dma_start(kept_d[bass.ds(512 * g, 512), :].rearrange("(t p) c -> p t c", p=P), hp[:, :, :]).then_inc(kept, 16)

                with sp.Fori(0, GROUPS - 1) as g:
                    group(g)
                group(GROUPS - 1, True)
                sp.wait_ge(kept, 16 * GROUPS)

            @block.gpsimd
            def _(pool):
                pool.wait_ge(const_in, 16 * 7)
                with pool.Fori(0, GROUPS) as g:
                    x = h[:, bass.ds(4 * g, 4), :]
                    pool.tensor_tensor(x, x, bias[:, :].unsqueeze(1).to_broadcast([P, 4, C]), ALU.add).then_inc(bias_done, 1)

            @block.vector
            def _(dve):
                def group(g):
                    rows = [tile_of(h, 4 * g + k) for k in range(4)]
                    hs = [hp[:, k, :] for k in range(4)]
                    dve.wait_ge(bias_done, g + 1)
                    after(dve, kept, 16 * g)
                    for k in range(4):
                        dve.wait_ge(acc_done, 4 * g + k + 1)
                        dve.tensor_tensor(hs[k], acc[k][:, 0:C], rows[k], ALU.add).then_inc(hp_done, 1)
                    norm_stats(dve, n1, hs, g + 1, hp_done)
                    norm_apply(dve, n1, rows, hs, g + 1, y_done)
                    norm_stats(dve, n2, rows, g + 1, y_done)
                    after(dve, t_done, g)
                    norm_apply(dve, n2, [x[:, :] for x in xn], rows, g + 1, xn_done)

                groups(dve.Fori, group)

            @block.scalar
            def _(act):
                act.wait_ge(const_in, 16 * 7)

                def group(g):
                    norm_root(act, n1, g + 1)
                    norm_root(act, n2, g + 1)
                    act.wait_ge(t_done, g + 1)
                    act.activation(cols(xa_all, 512 * g, 512), ta[:, :], ACT.Identity, scale=gain[:, 0:1], bias=gain[:, 1:2]).then_inc(t_out, 1)
                    act.activation(cols(xb_all, 512 * g, 512), tb[0:CB, :], ACT.Identity, scale=gain[0:CB, 2:3], bias=gain[0:CB, 3:4]).then_inc(t_out, 1)

                groups(act.Fori, group)

            @block.tensor
            def _(pe):
                pe.wait_ge(const_in, 16 * 7)

                def transposes(g):
                    after(pe, t_out, 2 * g)
                    for k in range(4):
                        pe.wait_ge(xn_done, 4 * g + k + 1)
                        pe.transpose(ta[:, P * k:P * k + P], xn[k][:, 0:P], ident[:, :])
                        mm = pe.transpose(tb[0:CB, P * k:P * k + P], xn[k][:, P:C], ident[:, :])
                    mm.then_inc(t_done, 1)

                project_heads(pe, ots, ots_in, acc, acc_done, wp, 0, hp_done)
                with pe.Fori(1, GROUPS) as g:
                    project_heads(pe, ots, ots_in, acc, acc_done, wp, g, hp_done)
                    transposes(g - 1)
                transposes(GROUPS - 1)


def dispatch(nc, d, h, ot_all, kept_d, queue_d, keep):
    with ExitStack() as ctx:
        m = Memory(nc, ctx, "disp")
        ident = m.sb("ident", [P, P])
        wp = m.sb("wp", [P, 3, C])
        bias = m.sb("proj_bias", [P, C])
        gain = m.sb("gain", [P, 4])
        gate_a = m.sb("gate_a", [P, EXPERTS])
        gate_c = m.sb("gate_c", [CB, EXPERTS])
        gate_b = m.sb("gate_b", [P, EXPERTS])
        trif = m.sb("trif", [P, P])
        tri = m.sb("tri", [P, P], BF16)
        ones = m.sb("ones", [P, P], BF16)
        eight = m.sb("eight", [P, EXPERTS])
        region = m.sb("region", [P, EXPERTS])
        valid = m.sb("valid", [P, TILES])
        dump = m.sb("dump", [P, TILES, 2])
        ots = [m.sb(f"ots{k}", [P, 3, P]) for k in range(4)]
        xp = m.sb("xp", [P, 4, C])
        hk = m.sb("hk", [P, 4, C])
        z = m.sb("z", [P, 4, C])
        za = m.sb("za", [P, 512])
        zb = m.sb("zb", [CB, 512])
        lg = m.sb("lg", [P, 4, EXPERTS])
        v8 = m.sb("v8", [P, 4, EXPERTS])
        i8 = m.sb("i8", [P, 4, EXPERTS], U32)
        idf = m.sb("idf", [P, 4, 2])
        mb = m.sb("mb", [P, 4, EXPERTS], BF16)
        seen_f = m.sb("seen_f", [P, EXPERTS])
        seen = m.sb("seen", [P, EXPERTS], BF16)
        group_sum = m.sb("group_sum", [P, EXPERTS])
        rank = m.sb("rank", [P, 4, EXPERTS])
        prod = m.sb("prod", [P, 4, 2, EXPERTS])
        slot_i = m.sb("slot_i", [P, 8], I32)
        n = NormGroup(m, "n3")
        acc = [m.psum(f"acc{k}", [P, 512]) for k in range(4)]
        ta = m.psum("ta", [P, 512])
        tb = m.psum("tb", [P, 512])
        lg_ps = m.psum("lg_ps", [P, 512])
        rk_ps = m.psum("rk_ps", [P, 512])
        const_in = m.sem("const_in")
        N_CONST = 15
        ots_in = [m.sem(f"ots_in{k}") for k in range(4)]
        (acc_done, bias_done, xp_done, hk_in, sum_done, z_done, t_done, z_out, lg_done, lg_out, top, pick, seen_done,
         rank_done, slot, sent, prep) = (m.sem(x) for x in (
             "acc_done", "bias_done", "xp_done", "hk_in", "sum_done", "z_done", "t_done", "z_out", "lg_done", "lg_out",
             "top", "pick", "seen_done", "rank_done", "slot", "sent", "prep"))
        pool_turn = m.sem("pool_turn")
        chosen, top2, slots, counts = keep
        with nc.Block() as block:
            @block.sync
            def _(sp):
                def const(dst, src):
                    sp.dma_start(dst, src).then_inc(const_in, 16)

                const(ident[:, :], d["ident"])
                const(wp[:, :, :], d["proj2_w"])
                const(bias[:, :], d["proj2_b"].partition_broadcast(P))
                for j, name in enumerate(("ln2_g", "ln2_b")):
                    const(gain[:, j:j + 1], d[name][0:P].rearrange("(p a) -> p a", a=1))
                    const(gain[0:CB, 2 + j:3 + j], d[name][P:C].rearrange("(p a) -> p a", a=1))
                const(gate_a[:, :], d["gate_wT"][0:P, :])
                const(gate_c[:, :], d["gate_wT"][P:C, :])
                const(gate_b[:, :], d["gate_b"].partition_broadcast(P))
                const(trif[:, :], d["tri"])
                const(eight[:, :], d["eight"])
                const(region[:, :], d["region"])
                const(valid[:, :], d["valid"])
                const(dump[:, :, :], d["dump"])
                load_heads(sp, ots, ots_in, acc_done, ot_all, 0)

                def group(g, last=False):
                    after(sp, sum_done, g)
                    sp.dma_start(hk[:, :, :], kept_d[bass.ds(512 * g, 512), :].rearrange("(t p) c -> p t c", p=P)).then_inc(hk_in, 16)
                    if not last:
                        load_heads(sp, ots, ots_in, acc_done, ot_all, g + 1)

                group(0)
                with sp.Fori(1, GROUPS - 1) as g:
                    group(g)
                group(GROUPS - 1, True)

            @block.gpsimd
            def _(pool):
                pool.memset(ones[:, :], 1.0).then_inc(prep, 1)
                pool.wait_ge(const_in, 16 * N_CONST)

                def add_bias(g):
                    x = h[:, bass.ds(4 * g, 4), :]
                    pool.tensor_tensor(x, x, bias[:, :].unsqueeze(1).to_broadcast([P, 4, C]), ALU.add).then_inc(bias_done, 1)

                def group(g, last=False):
                    if not last:
                        add_bias(g + 1)
                    pool.wait_ge(hk_in, 16 * (g + 1))
                    pool.wait_ge(xp_done, 4 * g + 4)
                    pool.tensor_tensor(h[:, bass.ds(4 * g, 4), :], hk[:, :, :], xp[:, :, :], ALU.add).then_inc(sum_done, 1)
                    hold(pool, slot, 4 * g + 4, pool_turn)
                    for j in range(8):
                        pool.indirect_dma_start(queue_d, bass.IndirectOffsetOnAxis(slot_i[:, j:j + 1], 0),
                                                z[:, j // 2, :], None).then_inc(sent, 16)

                add_bias(0)
                with pool.Fori(0, GROUPS - 1) as g:
                    group(g)
                group(GROUPS - 1, True)
                pool.wait_ge(sent, 128 * GROUPS)

            @block.vector
            def _(dve):
                dve.memset(seen_f[:, :], 0.0).then_inc(prep, 1)
                dve.memset(seen[:, :], 0.0).then_inc(prep, 1)
                dve.wait_ge(const_in, 16 * N_CONST)
                dve.tensor_copy(tri[:, :], trif[:, :]).then_inc(prep, 1)

                def group(g):
                    rows = [tile_of(h, 4 * g + k) for k in range(4)]
                    xs = [xp[:, k, :] for k in range(4)]
                    dve.wait_ge(bias_done, g + 1)
                    after(dve, sum_done, g)
                    for k in range(4):
                        dve.wait_ge(acc_done, 4 * g + k + 1)
                        dve.tensor_tensor(xs[k], acc[k][:, 0:C], rows[k], ALU.add).then_inc(xp_done, 1)
                    norm_stats(dve, n, xs, g + 1, xp_done)
                    after(dve, sent, 128 * g)
                    norm_apply(dve, n, [z[:, k, :] for k in range(4)], xs, g + 1, z_done)
                    dve.wait_ge(lg_done, g + 1)
                    dve.tensor_tensor(lg[:, :, :], lg_ps[:, 0:32].rearrange("p (k e) -> p k e", e=EXPERTS),
                                      gate_b[:, :].unsqueeze(1).to_broadcast([P, 4, EXPERTS]), ALU.add).then_inc(lg_out, 1)
                    hold(dve, lg_out, g + 1, n.turn)
                    for k in range(4):
                        dve.max(v8[:, k, :], lg[:, k, :]).then_inc(top, 1)
                    hold(dve, top, 8 * g + 4, n.turn)
                    for k in range(4):
                        dve.max_index(i8[:, k, :], v8[:, k, :], lg[:, k, :]).then_inc(top, 1)
                    dve.tensor_copy(top2[:, bass.ds(4 * g, 4), :], v8[:, :, 0:2]).then_inc(pick, 1)
                    dve.wait_ge(top, 8 * g + 8)
                    dve.tensor_copy(idf[:, :, :], i8[:, :, 0:2]).then_inc(pick, 1)
                    dve.wait_ge(pick, 5 * g + 2)
                    picked = chosen[:, bass.ds(4 * g, 4), :, :]
                    for j in range(2):
                        dve.tensor_tensor(picked[:, :, j, :], eight[:, :].unsqueeze(1).to_broadcast([P, 4, EXPERTS]),
                                          idf[:, :, j:j + 1].to_broadcast([P, 4, EXPERTS]), ALU.is_equal).then_inc(pick, 1)
                    dve.wait_ge(pick, 5 * g + 4)
                    v = valid[:, bass.ds(4 * g, 4)]
                    dve.tensor_tensor(picked.rearrange("p t j e -> p t (j e)"), picked.rearrange("p t j e -> p t (j e)"),
                                      v.unsqueeze(2).to_broadcast([P, 4, 16]), ALU.mult).then_inc(pick, 1)
                    dve.wait_ge(pick, 5 * g + 5)
                    after(dve, rank_done, g)
                    dve.tensor_tensor(mb[:, :, :], picked[:, :, 0, :], picked[:, :, 1, :], ALU.add).then_inc(seen_done, 1)
                    dve.wait_ge(seen_done, 2 * g + 1)
                    dve.tensor_reduce(group_sum[:, :], mb[:, :, :].rearrange("p k e -> p e k"), AX_X, ALU.add).then_inc(slot, 1)
                    dve.wait_ge(rank_done, g + 1)
                    dve.tensor_tensor(rank[:, :, :], rk_ps[:, 0:32].rearrange("p (k e) -> p k e", e=EXPERTS),
                                      region[:, :].unsqueeze(1).to_broadcast([P, 4, EXPERTS]), ALU.add).then_inc(slot, 1)
                    dve.wait_ge(slot, 4 * g + 2)
                    dve.tensor_tensor(seen_f[:, :], seen_f[:, :], group_sum[:, :], ALU.add).then_inc(lg_out_2, 1)
                    for j in range(2):
                        dve.tensor_tensor(prod[:, :, j, :], picked[:, :, j, :], rank[:, :, :], ALU.mult).then_inc(prod_done, 1)
                    dve.wait_ge(prod_done, 2 * g + 2)
                    dve.wait_ge(lg_out_2, g + 1)
                    dve.tensor_copy(seen[:, :], seen_f[:, :]).then_inc(seen_done, 1)
                    sl = slots[:, bass.ds(4 * g, 4), :]
                    dve.tensor_reduce(sl, prod[:, :, :, :], AX_X, ALU.add).then_inc(slot, 1)
                    dve.wait_ge(slot, 4 * g + 3)
                    dve.tensor_tensor(slot_i[:, :].rearrange("p (k j) -> p k j", j=2), sl,
                                      dump[:, bass.ds(4 * g, 4), :], ALU.add).then_inc(slot, 1)

                lg_out_2, prod_done = m.sem("seen_sum"), m.sem("prod_done")
                groups(dve.Fori, group)
                dve.wait_ge(rank_done, GROUPS + 1)
                dve.tensor_copy(counts[:, :], rk_ps[:, 64:64 + EXPERTS]).then_inc(prep, 1)
                dve.wait_ge(prep, 5)

            @block.scalar
            def _(act):
                act.wait_ge(const_in, 16 * N_CONST)

                def group(g):
                    norm_root(act, n, g + 1)
                    act.wait_ge(t_done, g + 1)
                    after(act, lg_done, g)
                    act.activation(za[:, :], ta[:, :], ACT.Identity, scale=gain[:, 0:1], bias=gain[:, 1:2]).then_inc(z_out, 1)
                    act.activation(zb[:, :], tb[0:CB, :], ACT.Identity, scale=gain[0:CB, 2:3], bias=gain[0:CB, 3:4]).then_inc(z_out, 1)

                groups(act.Fori, group)

            @block.tensor
            def _(pe):
                pe.wait_ge(const_in, 16 * N_CONST)
                pe.wait_ge(prep, 4)

                def route(g):
                    after(pe, z_out, 2 * g)
                    for k in range(4):
                        pe.wait_ge(z_done, 4 * g + k + 1)
                        pe.transpose(ta[:, P * k:P * k + P], z[:, k, 0:P], ident[:, :])
                        mm = pe.transpose(tb[0:CB, P * k:P * k + P], z[:, k, P:C], ident[:, :])
                    mm.then_inc(t_done, 1)
                    pe.wait_ge(z_out, 2 * g + 2)
                    after(pe, lg_out, g)
                    for k in range(4):
                        o = lg_ps[:, EXPERTS * k:EXPERTS * k + EXPERTS]
                        pe.matmul(o, za[:, P * k:P * k + P], gate_a[:, :], start=True, stop=False)
                        mm = pe.matmul(o, zb[:, P * k:P * k + P], gate_c[:, :], start=False, stop=True)
                    mm.then_inc(lg_done, 1)
                    pe.wait_ge(seen_done, 2 * g + 1)
                    after(pe, slot, 4 * g)
                    for k in range(4):
                        o = rk_ps[:, EXPERTS * k:EXPERTS * k + EXPERTS]
                        pe.matmul(o, tri[:, :], mb[:, k, :], start=True, stop=False)
                        for j in range(k):
                            pe.matmul(o, ones[:, :], mb[:, j, :], start=False, stop=False)
                        mm = pe.matmul(o, ones[:, :], seen[:, :], start=False, stop=True)
                    mm.then_inc(rank_done, 1)

                project_heads(pe, ots, ots_in, acc, acc_done, wp, 0, xp_done)
                with pe.Fori(1, GROUPS) as g:
                    project_heads(pe, ots, ots_in, acc, acc_done, wp, g, xp_done)
                    route(g - 1)
                route(GROUPS - 1)
                pe.wait_ge(seen_done, 2 * GROUPS)
                pe.wait_ge(slot, 4 * GROUPS)
                pe.matmul(rk_ps[:, 64:64 + EXPERTS], ones[:, :], seen[:, :], start=True, stop=True).then_inc(rank_done, 1)


def plan(nc, d, queue_d, keep, places, shares, table):
    chosen, top2, slots, counts = keep
    with ExitStack() as ctx:
        m = Memory(nc, ctx, "plan")
        eight = m.sb("eight", [P, EXPERTS])
        region = m.sb("region", [P, EXPERTS])
        number = m.sb("number", [P, TUNE])
        cf = m.sb("cf", [P, EXPERTS])
        ci = m.sb("ci", [P, EXPERTS], I32)
        ct = m.sb("ct", [P, EXPERTS], I32)
        tiles = m.sb("tiles", [P, EXPERTS])
        end = [m.sb(f"end{k}", [P, EXPERTS]) for k in range(2)]
        begin = m.sb("begin", [P, EXPERTS])
        fill = m.sb("fill", [P, EXPERTS], I32)
        tn = m.sb("tn", [P, MOE_TILES])
        cmp = m.sb("cmp", [P, MOE_TILES, EXPERTS])
        te = m.sb("te", [P, MOE_TILES])
        hot = m.sb("hot", [P, MOE_TILES, EXPERTS])
        first = m.sb("first", [P, MOE_TILES])
        real = m.sb("real", [P, MOE_TILES])
        local = m.sb("local", [P, MOE_TILES])
        base = m.sb("base", [P, MOE_TILES])
        shift = m.sb("shift", [P, EXPERTS])
        wide = m.sb("wide", [P, TILES * 2, EXPERTS])
        moved = m.sb("moved", [P, TILES * 2])
        diff = m.sb("diff", [P, TILES])
        ex = m.sb("ex", [P, TILES])
        den = m.sb("den", [P, TILES])
        filler = m.sb("filler", [P, 4, C])
        const_in, step, filled, ex_done, diff_done = (
            m.sem(x) for x in ("const_in", "step", "filled", "ex_done", "diff_done"))
        table_done = m.sem("table_done")
        with nc.Block() as block:
            @block.sync
            def _(sp):
                sp.dma_start(eight[:, :], d["eight"]).then_inc(const_in, 16)
                sp.dma_start(region[:, :], d["region"]).then_inc(const_in, 16)
                sp.dma_start(number[:, :], d["number"]).then_inc(const_in, 16)
                sp.wait_ge(table_done, 2)
                for e in range(EXPERTS):
                    start = sp.value_load(fill[0:1, e:e + 1], min_val=e * REGION, max_val=e * REGION + TOKENS)
                    sp.dma_start(queue_d[bass.ds(start, SLOTS), :].rearrange("(t p) c -> p t c", p=P),
                                 filler[:, :, :]).then_inc(filled, 16)
                sp.wait_ge(filled, 16 * EXPERTS)

            @block.scalar
            def _(act):
                act.wait_ge(diff_done, 1)
                act.activation(ex[:, :], diff[:, :], ACT.Exp).then_inc(ex_done, 1)

            @block.vector
            def _(dve):
                said = [0]

                def then(ins):
                    said[0] += 1
                    ins.then_inc(step, 1)
                    dve.wait_ge(step, said[0])

                dve.tensor_tensor(diff[:, :], top2[:, :, 1], top2[:, :, 0], ALU.subtract).then_inc(diff_done, 1)
                dve.memset(filler[:, :, :], 0.0).then_inc(table_done, 1)
                dve.wait_ge(const_in, 48)
                then(dve.tensor_scalar(ci[:, :], counts[:, :], float(SLOTS - 1), None, ALU.add))
                then(dve.tensor_scalar(ct[:, :], ci[:, :], SLOTS.bit_length() - 1, None, ALU.logical_shift_right))
                then(dve.tensor_copy(tiles[:, :], ct[:, :]))
                dve.tensor_tensor(fill[:, :], counts[:, :], region[:, :], ALU.add).then_inc(table_done, 1)
                src = tiles
                for k, by in enumerate((1, 2, 4)):
                    dst = end[k % 2]
                    then(dve.tensor_copy(dst[:, :], src[:, :]))
                    then(dve.tensor_tensor(dst[:, by:], src[:, by:], src[:, :EXPERTS - by], ALU.add))
                    src = dst
                then(dve.tensor_tensor(begin[:, :], src[:, :], tiles[:, :], ALU.subtract))
                shape = [P, MOE_TILES, EXPERTS]
                then(dve.tensor_scalar(tn[:, :], number[:, 0:MOE_TILES], -1.0, None, ALU.add))
                then(dve.tensor_tensor(cmp[:, :, :], tn[:, :].unsqueeze(2).to_broadcast(shape),
                                       src[:, :].unsqueeze(1).to_broadcast(shape), ALU.is_ge))
                then(dve.tensor_reduce(te[:, :], cmp[:, :, :], AX_X, ALU.add))
                then(dve.tensor_tensor(hot[:, :, :], te[:, :].unsqueeze(2).to_broadcast(shape),
                                       eight[:, :].unsqueeze(1).to_broadcast(shape), ALU.is_equal))
                then(dve.tensor_tensor(hot[:, :, :], hot[:, :, :], begin[:, :].unsqueeze(1).to_broadcast(shape), ALU.mult))
                then(dve.tensor_reduce(first[:, :], hot[:, :, :], AX_X, ALU.add))
                then(dve.tensor_scalar(real[:, :], te[:, :], EXPERTS - 0.5, None, ALU.is_lt))
                then(dve.tensor_tensor(local[:, :], tn[:, :], first[:, :], ALU.subtract))
                then(dve.tensor_scalar(local[:, :], local[:, :], float(SLOTS), None, ALU.mult))
                then(dve.tensor_scalar(base[:, :], te[:, :], float(REGION), None, ALU.mult))
                then(dve.tensor_tensor(base[:, :], base[:, :], local[:, :], ALU.add))
                then(dve.tensor_tensor(table[:, 0, :], te[:, :], real[:, :], ALU.mult))
                then(dve.tensor_tensor(table[:, 1, :], base[:, :], real[:, :], ALU.mult))
                then(dve.tensor_scalar(shift[:, :], begin[:, :], float(SLOTS), None, ALU.mult))
                then(dve.tensor_tensor(shift[:, :], shift[:, :], region[:, :], ALU.subtract))
                then(dve.tensor_tensor(wide[:, :, :], chosen[:, :, :, :].rearrange("p t j e -> p (t j) e"),
                                       shift[:, :].unsqueeze(1).to_broadcast([P, TILES * 2, EXPERTS]), ALU.mult))
                then(dve.tensor_reduce(moved[:, :], wide[:, :, :], AX_X, ALU.add))
                then(dve.tensor_tensor(places[:, :], moved[:, :], slots[:, :, :].rearrange("p t j -> p (t j)"), ALU.add))
                dve.wait_ge(ex_done, 1)
                then(dve.tensor_scalar(den[:, :], ex[:, :], 1.0, None, ALU.add))
                then(dve.reciprocal(den[:, :], den[:, :]))
                then(dve.tensor_copy(shares[:, :, 0], den[:, :]))
                then(dve.tensor_tensor(shares[:, :, 1], den[:, :], ex[:, :], ALU.mult))


def experts(nc, d, queue_d, out_d, table):
    with ExitStack() as ctx:
        m = Memory(nc, ctx, "moe")
        ident = m.sb("ident", [P, P])
        gain = m.sb("gain", [P, 4])
        xr = [m.sb(f"xr{k}", [P, 4, C + CB]) for k in range(2)]
        raw = [m.sb(f"raw{k}", [P, 2, HIDDEN]) for k in range(2)]
        hi = [m.sb(f"hi{k}", [P, 2, HIDDEN], F32R) for k in range(2)]
        lo = [m.sb(f"lo{k}", [P, HIDDEN], F32R) for k in range(2)]
        w2 = [m.sb(f"w2_{k}", [P, 6, C]) for k in range(2)]
        b1 = [m.sb(f"b1_{k}", [P, 6]) for k in range(2)]
        b2 = [m.sb(f"b2_{k}", [P, C]) for k in range(2)]
        xf = m.sb("xf", [P, 2, SLOTS])
        xh = [m.sb(f"xh{k}", [P, 2, SLOTS], F32R) for k in range(2)]
        xl = [m.sb(f"xl{k}", [P, 2, SLOTS], F32R) for k in range(2)]
        ht = [m.sb(f"ht{k}", [P, 6, SLOTS]) for k in range(2)]
        y = [m.sb(f"y{k}", [P, 4, C]) for k in range(2)]
        ta = m.psum("ta", [P, 512])
        tc = m.psum("tc", [P, 512])
        up = [m.psum(f"up{k}", [P, 512]) for k in range(2)]
        down = [m.psum(f"down{k}", [P, 512]) for k in range(2)]
        const_in = m.sem("const_in")
        w1_in, w2_in, x_in = ([m.sem(f"{n}{k}") for k in range(2)] for n in ("w1_in", "w2_in", "x_in"))
        (t_done, xf_done, hi_done, lo_done, xh_done, xl_done, up_done, gelu_done, down_done, y_done) = (
            m.sem(x) for x in ("t_done", "xf_done", "hi_done", "lo_done", "xh_done", "xl_done", "up_done",
                               "gelu_done", "down_done", "y_done"))
        stored = [m.sem(f"stored{k}") for k in range(2)]

        def run(fori, tile):
            for k in range(2):
                tile(0, k, True)
            with fori(1, MOE_TILES // 2) as i:
                for k in range(2):
                    tile(i, k, True)
            tile(MOE_TILES // 2, 0, False)

        with nc.Block() as block:
            @block.sync
            def _(sp):
                sp.dma_start(ident[:, :], d["ident"]).then_inc(const_in, 16)
                for j, name in enumerate(("ln2_g", "ln2_b")):
                    sp.dma_start(gain[:, j:j + 1], d[name][0:P].rearrange("(p a) -> p a", a=1)).then_inc(const_in, 16)
                    for half in range(2):
                        sp.dma_start(gain[CB * half:CB * half + CB, 2 + j:3 + j],
                                     d[name][P:C].rearrange("(p a) -> p a", a=1)).then_inc(const_in, 16)

                def load(i, k, used):
                    t = 2 * i + k
                    e = sp.value_load(table[0:1, 0, bass.ds(t, 1)], min_val=0, max_val=EXPERTS - 1)
                    row = sp.value_load(table[0:1, 1, bass.ds(t, 1)], min_val=0, max_val=EXPERTS * REGION - SLOTS)
                    after(sp, t_done, t - 1 if used else 0)
                    rows = queue_d[bass.ds(row, SLOTS), :].rearrange("(t p) c -> p t c", p=P)
                    sp.dma_start(xr[k][:, :, 0:C], rows).then_inc(x_in[k], 16)
                    sp.dma_start(xr[k][:, :, C:C + CB], rows[:, :, P:C]).then_inc(x_in[k], 16)
                    after(sp, lo_done, 2 * t - 2 if used else 0)
                    w = d["w1T"][bass.ds(e, 1)].rearrange("a c f -> (a c) f")
                    sp.dma_start(raw[k][:, 0, :], w[0:P, :]).then_inc(w1_in[k], 16)
                    for half in range(2):
                        sp.dma_start(raw[k][CB * half:CB * half + CB, 1, :], w[P:C, :]).then_inc(w1_in[k], 16)
                    after(sp, y_done, 4 * t - 4 if used else 0)
                    sp.dma_start(w2[k][:, :, :], d["w2T"][bass.ds(e, 1)].rearrange("a p s c -> (a p) s c")).then_inc(w2_in[k], 16)
                    sp.dma_start(b1[k][:, :], d["b1T"][bass.ds(e, 1)].rearrange("a p s -> (a p) s")).then_inc(w2_in[k], 16)
                    sp.dma_start(b2[k][:, :], d["b2"][bass.ds(e, 1), :].rearrange("a c -> (a c)").partition_broadcast(P)).then_inc(w2_in[k], 16)

                def store(t, k):
                    sp.wait_ge(y_done, 4 * t + 4)
                    sp.dma_start(out_d[bass.ds(SLOTS * t, SLOTS), :].rearrange("(t p) c -> p t c", p=P), y[k][:, :, :]).then_inc(stored[k], 16)

                load(0, 0, False)
                load(0, 1, False)
                with sp.Fori(0, MOE_TILES // 2 - 1) as i:
                    for k in range(2):
                        load(i + 1, k, True)
                        store(2 * i + k, k)
                load(MOE_TILES // 2, 0, True)
                for t in range(MOE_TILES - 3, MOE_TILES):
                    store(t, t % 2)
                sp.wait_ge(stored[0], 16 * (MOE_TILES // 2 + 1))
                sp.wait_ge(stored[1], 16 * (MOE_TILES // 2))

            @block.scalar
            def _(act):
                act.wait_ge(const_in, 16 * 7)

                def weights_hi(i, k):
                    t = 2 * i + k
                    act.wait_ge(w1_in[k], 48 * (i + 1))
                    after(act, up_done, 6 * t - 6 if not isinstance(t, int) or t > 1 else 0)
                    act.activation(hi[k][:, :, :], raw[k][:, :, :], ACT.Copy).then_inc(hi_done, 1)

                def affine(t):
                    act.wait_ge(t_done, t + 1)
                    after(act, xl_done, 2 * t)
                    act.activation(xf[:, 0, :], ta[:, :], ACT.Identity, scale=gain[:, 0:1], bias=gain[:, 1:2]).then_inc(xf_done, 1)
                    act.activation(xf[:, 1, :], tc[:, :], ACT.Identity, scale=gain[:, 2:3], bias=gain[:, 3:4]).then_inc(xf_done, 1)

                weights_hi(0, 0)
                affine(0)

                def tile(i, k, more):
                    t = 2 * i + k
                    act.wait_ge(w2_in[k], 48 * (i + 1))
                    after(act, down_done, 4 * t - 4 if not isinstance(t, int) or t > 1 else 0)
                    for j in range(6):
                        act.wait_ge(up_done, 6 * t + j + 1)
                        act.activation(ht[k][:, j, :], up[j % 2][:, :], ACT.Gelu, bias=b1[k][:, j:j + 1]).then_inc(gelu_done, 1)
                        if j == 2 and more:
                            weights_hi(*((i, 1) if k == 0 else (i + 1, 0)))
                    if more:
                        affine(t + 1)

                run(act.Fori, tile)

            @block.vector
            def _(dve):
                def split(i, k):
                    t = 2 * i + k
                    dve.wait_ge(hi_done, t + 1)
                    dve.tensor_tensor(lo[k][:, :], raw[k][:, 0, :], hi[k][:, 0, :].bitcast(F32), ALU.subtract).then_inc(lo_done, 1)
                    low = slice(CB, P)
                    dve.tensor_tensor(hi[k][low, 1, :], raw[k][low, 1, :], hi[k][low, 1, :].bitcast(F32), ALU.subtract).then_inc(lo_done, 1)

                def split_x(i, k):
                    t = 2 * i + k
                    dve.wait_ge(xf_done, 2 * t + 2)
                    after(dve, up_done, 6 * t - 6 if not isinstance(t, int) or t > 1 else 0)
                    dve.tensor_copy(xh[k][:, :, :], xf[:, :, :]).then_inc(xh_done, 1)
                    dve.wait_ge(xh_done, t + 1)
                    dve.tensor_tensor(xl[k][:, 0, :], xf[:, 0, :], xh[k][:, 0, :].bitcast(F32), ALU.subtract).then_inc(xl_done, 1)
                    dve.tensor_tensor(xl[k][0:CB, 1, :], xf[0:CB, 1, :], xh[k][0:CB, 1, :].bitcast(F32), ALU.subtract).then_inc(xl_done, 1)

                split(0, 0)
                split_x(0, 0)

                def tile(i, k, more):
                    t = 2 * i + k
                    nxt = (i, 1) if k == 0 else (i + 1, 0)
                    if more:
                        split(*nxt)
                        split_x(*nxt)
                    after(dve, stored[k], 16 * i)
                    dve.wait_ge(w2_in[k], 48 * (i + 1))
                    for j in range(4):
                        dve.wait_ge(down_done, 4 * t + j + 1)
                        dve.tensor_tensor(y[k][:, j, :], down[j % 2][:, 0:C], b2[k][:, :], ALU.add).then_inc(y_done, 1)

                run(dve.Fori, tile)

            @block.tensor
            def _(pe):
                pe.wait_ge(const_in, 16 * 7)

                def transposes(i, k):
                    t = 2 * i + k
                    pe.wait_ge(x_in[k], 32 * (i + 1))
                    after(pe, xf_done, 2 * t)
                    for j in range(4):
                        pe.transpose(ta[:, P * j:P * j + P], xr[k][:, j, 0:P], ident[:, :])
                        mm = pe.transpose(tc[:, P * j:P * j + P], xr[k][:, j, P:C + CB], ident[:, :])
                    mm.then_inc(t_done, 1)

                transposes(0, 0)

                def tile(i, k, more):
                    t = 2 * i + k
                    pe.wait_ge(lo_done, 2 * t + 2)
                    pe.wait_ge(xl_done, 2 * t + 2)
                    for j in range(6):
                        after(pe, gelu_done, 6 * t + j - 1)
                        o, f = up[j % 2][:, :], slice(P * j, P * j + P)
                        pe.matmul(o, hi[k][:, 0, f], xh[k][:, 0, :], start=True, stop=False)
                        pe.matmul(o, hi[k][:, 0, f], xl[k][:, 0, :], start=False, stop=False)
                        pe.matmul(o, lo[k][:, f], xh[k][:, 0, :], start=False, stop=False)
                        pe.matmul(o, hi[k][:, 1, f], xh[k][:, 1, :], start=False, stop=False)
                        pe.matmul(o, hi[k][0:CB, 1, f], xl[k][0:CB, 1, :], start=False, stop=True).then_inc(up_done, 1)
                    if more:
                        transposes(*((i, 1) if k == 0 else (i + 1, 0)))
                    pe.wait_ge(w2_in[k], 48 * (i + 1))
                    pe.wait_ge(gelu_done, 6 * t + 6)
                    for j in range(4):
                        after(pe, y_done, 4 * t + j - 1)
                        for s in range(6):
                            mm = pe.matmul(down[j % 2][:, 0:C], ht[k][:, s, P * j:P * j + P], w2[k][:, s, :],
                                           start=(s == 0), stop=(s == 5))
                        mm.then_inc(down_done, 1)

                run(pe.Fori, tile)


def combine(nc, h, out_d, y_d, places, shares):
    with ExitStack() as ctx:
        m = Memory(nc, ctx, "comb")
        got = [m.sb(f"got{k}", [P, 8, C]) for k in range(2)]
        done = [m.sb(f"done{k}", [P, 4, C]) for k in range(2)]
        got_in = [m.sem(f"got_in{k}") for k in range(2)]
        stored = [m.sem(f"stored{k}") for k in range(2)]
        half_done, row_done = m.sem("half_done"), m.sem("row_done")
        FULL = TOKENS // P
        with nc.Block() as block:
            @block.gpsimd
            def _(pool):
                for g in range(GROUPS):
                    k = g % 2
                    after(pool, row_done, 4 * g - 4)
                    for j in range(8):
                        if 4 * g + j // 2 <= FULL:
                            at = 8 * g + j
                            pool.indirect_dma_start(got[k][:, j, :], None, y_d,
                                                    bass.IndirectOffsetOnAxis(places[:, at:at + 1], 0)).then_inc(got_in[k], 16)

            @block.vector
            def _(dve):
                for g in range(GROUPS):
                    k = g % 2
                    n_in = sum(16 for q in range(k, g + 1, 2) for j in range(8) if 4 * q + j // 2 <= FULL)
                    dve.wait_ge(got_in[k], n_in)
                    after(dve, stored[k], 16 * (g // 2))
                    for j in range(4):
                        t = 4 * g + j
                        if t > FULL:
                            continue
                        dve.scalar_tensor_tensor(out=h[:, t, :], in0=got[k][:, 2 * j, :], scalar=shares[:, t, 0:1],
                                                 in1=h[:, t, :], op0=ALU.mult, op1=ALU.add).then_inc(half_done, 1)
                    for j in range(4):
                        t = 4 * g + j
                        if t > FULL:
                            continue
                        dve.wait_ge(half_done, t + 1)
                        dve.scalar_tensor_tensor(out=done[k][:, j, :], in0=got[k][:, 2 * j + 1, :], scalar=shares[:, t, 1:2],
                                                 in1=h[:, t, :], op0=ALU.mult, op1=ALU.add).then_inc(row_done, 1)

            @block.sync
            def _(sp):
                for g in range(GROUPS):
                    k = g % 2
                    if 4 * g + 4 <= FULL:
                        sp.wait_ge(row_done, 4 * g + 4)
                        sp.dma_start(out_d[512 * g:512 * g + 512, :].rearrange("(t p) c -> p t c", p=P), done[k][:, :, :]).then_inc(stored[k], 16)
                    else:
                        sp.wait_ge(row_done, FULL + 1)
                        whole = FULL - 4 * g
                        sp.dma_start(out_d[512 * g:P * FULL, :].rearrange("(t p) c -> p t c", p=P), done[k][:, 0:whole, :]).then_inc(stored[k], 16)
                        sp.dma_start(out_d[P * FULL:TOKENS, :], done[k][0:TOKENS - P * FULL, whole, :]).then_inc(stored[k], 16)
                sp.wait_ge(stored[0], 16 * 6)
                sp.wait_ge(stored[1], 16 * 4)


def vit_moe_layer(nc, d, out):
    rows_d = nc.dram_tensor("rows_scratch", [ROWS, C], F32, kind="Internal").ap()
    kept_d = nc.dram_tensor("kept_scratch", [ROWS, C], F32, kind="Internal").ap()
    queue_d = nc.dram_tensor("queue_scratch", [DUMP + 4 * P, C], F32, kind="Internal").ap()
    y_d = nc.dram_tensor("y_scratch", [MOE_TILES * SLOTS, C], F32, kind="Internal").ap()
    parts_d = nc.dram_tensor("parts_scratch", [2, 3, 2, C, CHUNK], BF16, kind="Internal").ap()
    out_rows = out.rearrange("b s c -> (b s) c")
    embed(nc, d, rows_d)
    with ExitStack() as ctx:
        m = Memory(nc, ctx, "all")
        h = m.sb("h", [P, TILES, C])
        keep = (m.sb("chosen", [P, TILES, 2, EXPERTS]), m.sb("top2", [P, TILES, 2]), m.sb("slots", [P, TILES, 2]),
                m.sb("counts", [P, EXPERTS]))
        with ExitStack() as wide:
            w = Memory(nc, wide, "all")
            ot_all = w.sb("ot_all", [P, 3, ROWS])
            with ExitStack() as feats:
                f = Memory(nc, feats, "all")
                xa_all = f.sb("xa_all", [P, ROWS])
                xb_all = f.sb("xb_all", [CB, ROWS])
                first_norm(nc, d, rows_d, h, xa_all, xb_all)
                attention(nc, d, parts_d, xa_all, xb_all, ot_all, "qkv1_w", "qkv1_b", True)
                between(nc, d, h, ot_all, xa_all, xb_all, kept_d)
                attention(nc, d, parts_d, xa_all, xb_all, ot_all, "qkv2_w", None, False)
            dispatch(nc, d, h, ot_all, kept_d, queue_d, keep)
        places = m.sb("places", [P, TILES * 2], I32)
        shares = m.sb("shares", [P, TILES, 2])
        table = m.sb("table", [P, 2, MOE_TILES], I32)
        plan(nc, d, queue_d, keep, places, shares, table)
        experts(nc, d, queue_d, y_d, table)
        combine(nc, h, out_rows, y_d, places, shares)


def kernel(**inputs):
    import numpy as _np
    import concourse.bacc as _bacc
    from concourse import mybir as _mybir
    from concourse.bass_utils import run_bass_kernel_spmd as _run

    arrays = lay_out(inputs)
    nc = _bacc.Bacc("TRN2", target_bir_lowering=False, num_devices=1)
    d = {name: nc.dram_tensor(name + "_dram", a.shape, _mybir.dt.from_np(a.dtype), kind="ExternalInput").ap()
         for name, a in arrays.items()}
    out = nc.dram_tensor("out_dram", (BATCH, SEQ, C), F32, kind="ExternalOutput").ap()
    vit_moe_layer(nc, d, out)
    r = _run(nc, [{name + "_dram": a for name, a in arrays.items()}], core_ids=[0])
    return r.results[0]["out_dram"]


def lay_out(inputs):
    import numpy as np

    a = {k: np.asarray(v) for k, v in inputs.items()}
    side = 96 // 16
    x = a["x"].reshape(BATCH, 3, side, 16, side, 16).transpose(0, 1, 2, 4, 3, 5).reshape(BATCH, IMG, PATCH)
    x = x.transpose(1, 0, 2).reshape(IMG // 2, P, 6, P)
    out = {"patches": x.transpose(0, 3, 2, 1).reshape(IMG // 2, P, 6 * P)}
    out["ids"] = a["x_txt"].T.reshape(16, P).T
    out["tune_ids"] = a["L0_txt_tune_ids"]
    out["base_w"], out["train_w"] = a["L0_txt_base_weight"], a["L0_txt_train_weight"]
    out["tok_wT"], out["tok_b"] = a["L0_tok_W"].T, a["L0_tok_b"]
    out["cls"], out["pos"] = a["L0_tok_class_token"], a["L0_tok_pos_embedding"]
    order = np.concatenate([w * C + CB * n + np.r_[0:CB] for n in range(3) for w in range(2)] + [2 * C + np.r_[0:C]])
    out["qkv1_w"], out["qkv1_b"] = a["L0_attn_w_qkv"].T[:, order], a["L0_attn_b_qkv"][order]
    out["qkv2_w"] = a["L0_ffn_qkv_w"].T[:, order]
    for name, w in (("proj1_w", a["L0_attn_w_proj"]), ("proj2_w", a["L0_ffn_proj_w"])):
        wide = np.zeros((3, 4, 2, HD, C), w.dtype)
        wide[:, :, 0] = w.T.reshape(3, 4, HD, C)
        out[name] = wide.reshape(3, P, C).transpose(1, 0, 2)
    out["proj1_b"], out["proj2_b"] = a["L0_attn_b_proj"], a["L0_ffn_proj_b"]
    for name in ("ln1_g", "ln1_b", "ln2_g", "ln2_b", "gate_b", "b2"):
        out[name] = a["L0_ffn_" + name]
    out["gate_wT"] = a["L0_ffn_gate_w"].T
    out["w1T"] = a["L0_ffn_w1"].transpose(0, 2, 1)
    out["b1T"] = a["L0_ffn_b1"].reshape(EXPERTS, 6, P).transpose(0, 2, 1)
    out["w2T"] = a["L0_ffn_w2"].transpose(0, 2, 1).reshape(EXPERTS, 6, P, C).transpose(0, 2, 1, 3)
    f = np.float32
    inv = (f(1.0) / np.power(f(10000.0), np.arange(0, HD, 2, dtype=f) / f(HD))).astype(f)
    angle = (np.arange(SEQ, dtype=f)[:, None] * inv[None, :]).astype(f)
    cos, sin = np.cos(angle).T, np.sin(angle).T
    out["cos"] = np.tile(np.concatenate([cos, cos]), (P // HD, CHUNK_B)).astype(f)
    out["sin"] = np.tile(np.concatenate([-sin, sin]), (P // HD, CHUNK_B)).astype(f)
    out["ident"] = np.eye(P, dtype=f)
    pick = np.zeros((PARTS, HEADS), f)
    for j in range(3):
        pick[HEADS * j:HEADS * j + HEADS] = np.eye(HEADS)
    out["pick"] = pick
    out["tri"] = np.triu(np.ones((P, P), f), 1)
    out["number"] = np.tile(np.arange(1, TUNE + 1, dtype=f), (P, 1))
    out["eight"] = np.tile(np.arange(EXPERTS, dtype=f), (P, 1))
    out["region"] = np.tile(np.arange(EXPERTS, dtype=f) * REGION, (P, 1))
    token = np.arange(TILES)[None, :] * P + np.arange(P)[:, None]
    out["valid"] = (token < TOKENS).astype(f)
    dump = np.zeros((P, TILES, 2), f)
    for j in range(2):
        dump[:, :, j] = np.where(token < TOKENS, 0, DUMP + 2 * (token - TOKENS) + j)
    out["dump"] = dump
    return {k: np.ascontiguousarray(v) for k, v in out.items()}
```

```python
from contextlib import ExitStack

import concourse.bass as bass
from concourse import mybir

F32 = mybir.dt.float32
F32R = mybir.dt.float32r
BF16 = mybir.dt.bfloat16
I32 = mybir.dt.int32
U32 = mybir.dt.uint32
ALU = mybir.AluOpType
ACT = mybir.ActivationFunctionType
AX_X = mybir.AxisListType.X

P = 128
BATCH, IMG, TXT = 64, 36, 32
SEQ = 1 + IMG + TXT
TOKENS = BATCH * SEQ
TILES = 36
GROUPS = TILES // 4
ROWS = TILES * P
PAD = ROWS - TOKENS
C = 192
CB = C - P
HEADS, HD = 12, 16
PATCH = 768
TUNE = 256
EPS = 1e-5
CHUNK_B = 4
CHUNK = CHUNK_B * SEQ
CHUNKS = BATCH // CHUNK_B
PARTS = 96
EXPERTS, HIDDEN, TOPK = 8, 768, 2
SLOTS = 512
REGION = TOKENS + SLOTS
MOE_TILES = (TOPK * TOKENS + EXPERTS * (SLOTS - 1)) // SLOTS
DUMP = EXPERTS * REGION
SURPLUS = DUMP + 4 * P
Y_ROWS = 2 * ROWS + (EXPERTS + 2) * SLOTS
QUEUED = 1 + C


def after(eng, sem, count):
    if not isinstance(count, int) or count > 0:
        eng.wait_ge(sem, count)


def hold(eng, sem, count, turn):
    eng.wait_ge(sem, count)
    eng.sem_inc(turn, 1)


class Memory:

    def __init__(self, nc, ctx, phase):
        self.nc, self.ctx, self.phase = nc, ctx, phase + "_"
        self.sems = []
        ctx.callback(self.clear)

    def clear(self):
        if self.sems:
            self.nc.clear_and_free_semaphores(self.sems)
            self.nc.all_engine_barrier()

    def sb(self, name, shape, dt=F32):
        return self.ctx.enter_context(self.nc.sbuf_tensor(self.phase + name, shape, dt))

    def psum(self, name, shape, dt=F32):
        return self.ctx.enter_context(self.nc.psum_tensor(self.phase + name, shape, dt))

    def sem(self, name):
        self.sems.append(self.nc.alloc_semaphore(self.phase + name))
        return self.sems[-1]


def embed(nc, d, rows_d):
    with ExitStack() as ctx:
        m = Memory(nc, ctx, "emb")
        w = m.sb("tok_w", [P, 6, C])
        patch = [m.sb(f"patch{k}", [P, 6, P]) for k in range(2)]
        place = m.sb("place", [P, IMG // 2, C])
        bias = m.sb("tok_bias", [P, C])
        emb = [m.sb(f"emb{k}", [P, C]) for k in range(2)]
        cls = m.sb("cls", [BATCH, 2, C])
        zero = m.sb("zero", [P, C])
        ids = m.sb("ids", [P, 16], I32)
        idf = m.sb("idf", [P, 16])
        tune = m.sb("tune", [P, TUNE], I32)
        tunef = m.sb("tunef", [P, TUNE])
        number = m.sb("number", [P, TUNE])
        hit = m.sb("hit", [P, 16, TUNE])
        last = m.sb("last", [P, 16])
        mask = m.sb("mask", [P, 16])
        keep = m.sb("keep", [P, 16])
        rowf = m.sb("rowf", [P, 16])
        row = m.sb("row", [P, 16], I32)
        base = m.sb("base", [P, 16, C])
        train = m.sb("train", [P, 16, C])
        acc = [m.psum(f"emb_acc{k}", [P, 512]) for k in range(2)]
        w_in, place_in, cls_in, ids_in = (m.sem(x) for x in ("w_in", "place_in", "cls_in", "ids_in"))
        patch_in = [m.sem(f"patch_in{k}") for k in range(2)]
        place_done, cls_done, zero_done = m.sem("place_done"), m.sem("cls_done"), m.sem("zero_done")
        acc_done, emb_done = m.sem("acc_done"), m.sem("emb_done")
        stored = [m.sem(f"stored{k}") for k in range(2)]
        text = m.sem("text_step")
        row_done, base_in, train_in, text_done, rest = (
            m.sem(x) for x in ("row_done", "base_in", "train_in", "text_done", "rest_stored"))
        token = rows_d[0:TOKENS, :].rearrange("(b s) c -> b s c", s=SEQ)

        with nc.Block() as block:
            @block.sync
            def _(sp):
                sp.dma_start(w[:, :, :], d["tok_wT"].rearrange("(k p) c -> p k c", p=P)).then_inc(w_in, 16)

                def load(t, k):
                    sp.dma_start(patch[k][:, :, :].rearrange("p k n -> p (k n)"),
                                 d["patches"][bass.ds(t, 1)].rearrange("a p n -> (a p) n")).then_inc(patch_in[k], 16)

                load(0, 0)
                load(9, 1)
                for half in range(2):
                    sp.dma_start(place[64 * half:64 * half + 64, :, :],
                                 d["pos"][1 + half:1 + half + 35:2, :].partition_broadcast(64)).then_inc(place_in, 16)
                sp.dma_start(bias[:, :], d["tok_b"].partition_broadcast(P)).then_inc(place_in, 16)
                sp.dma_start(cls[:, 0, :], d["cls"][0:1, :].rearrange("a c -> (a c)").partition_broadcast(BATCH)).then_inc(cls_in, 16)
                sp.dma_start(cls[:, 1, :], d["pos"][0:1, :].rearrange("a c -> (a c)").partition_broadcast(BATCH)).then_inc(cls_in, 16)

                def store(t, k, n):
                    sp.wait_ge(emb_done, n)
                    for half in range(2):
                        sp.dma_start(token[:, bass.ds(2 * t + 1 + half, 1), :].rearrange("b a c -> b (a c)"),
                                     emb[k][64 * half:64 * half + 64, :]).then_inc(stored[k], 16)

                with sp.Fori(0, 8) as i:
                    for k in range(2):
                        sp.wait_ge(acc_done, 2 * i + 1 + k)
                        load(i + 1 + 9 * k, k)
                    for k in range(2):
                        store(i + 9 * k, k, 2 * i + 1 + k)
                for k in range(2):
                    store(8 + 9 * k, k, 17 + k)
                sp.wait_ge(stored[0], 16 * 18)
                sp.wait_ge(stored[1], 16 * 18)

            @block.scalar
            def _(act):
                act.dma_start(ids[:, :], d["ids"]).then_inc(ids_in, 16)
                act.dma_start(tune[:, :], d["tune_ids"].partition_broadcast(P)).then_inc(ids_in, 16)
                act.dma_start(number[:, :], d["number"]).then_inc(ids_in, 16)
                act.wait_ge(zero_done, 1)
                act.dma_start(rows_d[TOKENS:TOKENS + P, :], zero[:, :]).then_inc(rest, 16)
                act.dma_start(rows_d[TOKENS + P:ROWS, :], zero[0:PAD - P, :]).then_inc(rest, 16)
                act.wait_ge(cls_done, 1)
                act.dma_start(token[:, 0, :], cls[:, 0, :]).then_inc(rest, 16)
                act.wait_ge(text_done, 1)
                for half in range(2):
                    act.dma_start(token[:, 1 + IMG + half::2, :], base[64 * half:64 * half + 64, :, :]).then_inc(rest, 16)
                act.wait_ge(rest, 16 * 5)

            @block.gpsimd
            def _(pool):
                pool.wait_ge(ids_in, 48)
                for j in range(16):
                    pool.indirect_dma_start(base[:, j, :], None, d["base_w"],
                                            bass.IndirectOffsetOnAxis(ids[:, j:j + 1], 0)).then_inc(base_in, 16)
                pool.wait_ge(row_done, 1)
                for j in range(16):
                    pool.indirect_dma_start(train[:, j, :], None, d["train_w"],
                                            bass.IndirectOffsetOnAxis(row[:, j:j + 1], 0)).then_inc(train_in, 16)

            @block.tensor
            def _(pe):
                pe.wait_ge(w_in, 16)

                def tile(k, loads, n):
                    pe.wait_ge(patch_in[k], 16 * loads)
                    after(pe, emb_done, n)
                    for s in range(6):
                        mm = pe.matmul(acc[k][:, 0:C], patch[k][:, s, :], w[:, s, :], start=(s == 0), stop=(s == 5))
                    mm.then_inc(acc_done, 1)

                for k in range(2):
                    tile(k, 1, 0)
                with pe.Fori(1, 9) as i:
                    for k in range(2):
                        tile(k, i + 1, 2 * i - 1 + k)

            @block.vector
            def _(dve):
                dve.memset(zero[:, :], 0.0).then_inc(zero_done, 1)
                dve.wait_ge(cls_in, 32)
                dve.tensor_tensor(cls[:, 0, :], cls[:, 0, :], cls[:, 1, :], ALU.add).then_inc(cls_done, 1)
                dve.wait_ge(ids_in, 48)
                dve.tensor_copy(idf[:, :], ids[:, :]).then_inc(text, 1)
                dve.tensor_copy(tunef[:, :], tune[:, :]).then_inc(text, 1)
                dve.wait_ge(text, 2)
                wide = [P, 16, TUNE]
                dve.tensor_tensor(hit[:, :, :], tunef[:, :].unsqueeze(1).to_broadcast(wide),
                                  idf[:, :].unsqueeze(2).to_broadcast(wide), ALU.is_equal).then_inc(text, 1)
                dve.wait_ge(text, 3)
                dve.tensor_tensor(hit[:, :, :], hit[:, :, :], number[:, :].unsqueeze(1).to_broadcast(wide),
                                  ALU.mult).then_inc(text, 1)
                dve.wait_ge(text, 4)
                dve.tensor_reduce(last[:, :], hit[:, :, :], AX_X, ALU.max).then_inc(text, 1)
                dve.wait_ge(text, 5)
                dve.tensor_scalar(mask[:, :], last[:, :], 0.5, None, ALU.is_gt).then_inc(text, 1)
                dve.tensor_scalar(keep[:, :], last[:, :], 0.5, None, ALU.is_lt).then_inc(text, 1)
                dve.tensor_scalar(rowf[:, :], last[:, :], -1.0, 0.0, ALU.add, ALU.max).then_inc(text, 1)
                dve.wait_ge(text, 8)
                dve.tensor_copy(row[:, :], rowf[:, :]).then_inc(row_done, 1)
                dve.wait_ge(place_in, 48)
                dve.tensor_tensor(place[:, :, :], place[:, :, :],
                                  bias[:, :].unsqueeze(1).to_broadcast([P, IMG // 2, C]), ALU.add).then_inc(place_done, 1)
                dve.wait_ge(place_done, 1)

                def tile(t, k, n, stores):
                    dve.wait_ge(acc_done, n)
                    after(dve, stored[k], stores)
                    dve.tensor_tensor(emb[k][:, :], acc[k][:, 0:C],
                                      place[:, bass.ds(t, 1), :].rearrange("p a c -> p (a c)"),
                                      ALU.add).then_inc(emb_done, 1)

                for k in range(2):
                    tile(9 * k, k, 1 + k, 0)
                with dve.Fori(1, 9) as i:
                    for k in range(2):
                        tile(i + 9 * k, k, 2 * i + 1 + k, 32 * i)
                dve.wait_ge(base_in, 256)
                wide = [P, 16, C]
                dve.tensor_tensor(base[:, :, :], base[:, :, :], keep[:, :].unsqueeze(2).to_broadcast(wide), ALU.mult).then_inc(text, 1)
                dve.wait_ge(train_in, 256)
                dve.tensor_tensor(train[:, :, :], train[:, :, :], mask[:, :].unsqueeze(2).to_broadcast(wide), ALU.mult).then_inc(text, 1)
                dve.wait_ge(text, 10)
                dve.tensor_tensor(base[:, :, :], base[:, :, :], train[:, :, :], ALU.add).then_inc(text_done, 1)


class NormGroup:

    def __init__(self, m, name):
        self.stats = m.sb(name + "_stats", [P, 4, 6])
        self.mv = m.sb(name + "_mv", [P, 4, 2])
        self.inv = m.sb(name + "_inv", [P, 4])
        self.rstd = m.sb(name + "_rstd", [P, 4])
        self.stat_done, self.mv_done, self.eps_done, self.inv_done, self.rstd_done, self.turn = (
            m.sem(f"{name}_{x}") for x in ("stat", "mv", "eps", "inv", "rstd", "turn"))


def norm_stats(dve, n, rows, g, ready=None):
    if ready:
        hold(dve, ready, 4 * g, n.turn)
    for k in range(4):
        dve.bn_stats(n.stats[:, k, :], rows[k]).then_inc(n.stat_done, 1)
    hold(dve, n.stat_done, 4 * g, n.turn)
    for k in range(4):
        dve.bn_aggr(n.mv[:, k, :], n.stats[:, k, :]).then_inc(n.mv_done, 1)
    dve.wait_ge(n.mv_done, 4 * g)
    dve.tensor_scalar(n.inv[:, :], n.mv[:, :, 1], EPS, None, ALU.add).then_inc(n.eps_done, 1)
    dve.wait_ge(n.eps_done, g)
    dve.reciprocal(n.inv[:, :], n.inv[:, :]).then_inc(n.inv_done, 1)


def norm_root(act, n, g):
    act.wait_ge(n.inv_done, g)
    act.activation(n.rstd[:, :], n.inv[:, :], ACT.Sqrt).then_inc(n.rstd_done, 1)


def norm_apply(dve, n, outs, rows, g, done):
    dve.wait_ge(n.rstd_done, g)
    for k in range(4):
        dve.tensor_scalar(outs[k], rows[k], n.mv[:, k, 0:1], n.rstd[:, k:k + 1],
                          ALU.subtract, ALU.mult).then_inc(done, 1)


def cols(x, start, n):
    return x[:, bass.ds(start, n)]


def tile_of(x, t):
    return x[:, bass.ds(t, 1), :].rearrange("p a c -> p (a c)")


def first_norm(nc, d, rows_d, h, xa_all, xb_all):
    with ExitStack() as ctx:
        m = Memory(nc, ctx, "norm")
        ident = m.sb("ident", [P, P])
        xn = [m.sb(f"xn{k}", [P, C]) for k in range(4)]
        n = NormGroup(m, "n0")
        ta = m.psum("ta", [P, 512])
        tb = m.psum("tb", [P, 512])
        rows_in = [m.sem(f"rows_in{g}") for g in range(GROUPS)]
        ident_in, xn_done, t_done, ta_out, tb_out = (
            m.sem(x) for x in ("ident_in", "xn_done", "t_done", "ta_out", "tb_out"))
        all_in = m.sem("all_in")
        with nc.Block() as block:
            @block.sync
            def _(sp):
                sp.dma_start(ident[:, :], d["ident"]).then_inc(ident_in, 16)
                for g in range(GROUPS):
                    sp.dma_start(h[:, 4 * g:4 * g + 4, :],
                                 rows_d[512 * g:512 * g + 512, :].rearrange("(t p) c -> p t c", p=P)).then_inc(rows_in[g], 16)
                for g in range(GROUPS):
                    sp.wait_ge(rows_in[g], 16)
                    sp.sem_inc(all_in, 1)

            @block.vector
            def _(dve):
                def group(g):
                    hold(dve, all_in, g + 1, n.turn)
                    rows = [tile_of(h, 4 * g + k) for k in range(4)]
                    norm_stats(dve, n, rows, g + 1)
                    after(dve, t_done, g)
                    norm_apply(dve, n, [x[:, :] for x in xn], rows, g + 1, xn_done)
                    dve.wait_ge(t_done, g + 1)
                    dve.tensor_copy(cols(xb_all, 512 * g, 512), tb[0:CB, :]).then_inc(tb_out, 1)

                group(0)
                with dve.Fori(1, GROUPS) as g:
                    group(g)

            @block.scalar
            def _(act):
                def group(g):
                    norm_root(act, n, g + 1)
                    act.wait_ge(t_done, g + 1)
                    act.activation(cols(xa_all, 512 * g, 512), ta[:, :], ACT.Copy).then_inc(ta_out, 1)

                group(0)
                with act.Fori(1, GROUPS) as g:
                    group(g)

            @block.tensor
            def _(pe):
                pe.wait_ge(ident_in, 16)

                def group(g):
                    after(pe, ta_out, g)
                    after(pe, tb_out, g)
                    for k in range(4):
                        pe.wait_ge(xn_done, 4 * g + k + 1)
                        pe.transpose(ta[:, P * k:P * k + P], xn[k][:, 0:P], ident[:, :])
                        mm = pe.transpose(tb[0:CB, P * k:P * k + P], xn[k][:, P:C], ident[:, :])
                    mm.then_inc(t_done, 1)

                group(0)
                with pe.Fori(1, GROUPS) as g:
                    group(g)


VALUE_AT = {0: 0, 4: 1, 5: 2, 6: 3}
QK_AT = {1: 0, 2: 1, 3: 2}


def projections(c, step, full):
    order = [s for s in range(8) if s in VALUE_AT or (full and s in QK_AT)]
    return 10 + 7 * c + order.index(step)


def attention(nc, d, parts_d, xa_all, xb_all, ot_all, w_name, bias_name, rope):
    with ExitStack() as ctx:
        m = Memory(nc, ctx, w_name)
        kb = CB + 1 if bias_name else CB
        wa = m.sb("wa", [P, 3 * C])
        wb = m.sb("wb", [kb, 3 * C])
        xa = [m.sb(f"xa{k}", [P, CHUNK]) for k in range(2)]
        xb = [m.sb(f"xb{k}", [kb, CHUNK]) for k in range(2)]
        qk = m.sb("qk", [P, 3, CHUNK])
        rest = m.sb("rest", [P, 3, CHUNK])
        part = [m.sb(f"part{k}", [P, 3, CHUNK], BF16) for k in range(3)]
        qs = [m.sb(f"qs{k}", [PARTS, HEADS, CHUNK], BF16) for k in range(2)]
        ks = [m.sb(f"ks{k}", [PARTS, HEADS, CHUNK], BF16) for k in range(2)]
        vp = [m.sb(f"vp{k}", [SEQ, CHUNK_B, HEADS, 2 * HD]) for k in range(2)]
        pt = [m.sb(f"pt{k}", [SEQ, 6, SEQ]) for k in range(2)]
        nm = [m.sb(f"nm{k}", [SEQ, HEADS]) for k in range(2)]
        nmr = [m.sb(f"nmr{k}", [SEQ, HEADS]) for k in range(2)]
        ms = [m.sb(f"ms{k}", [SEQ, 3, HEADS], BF16) for k in range(2)]
        mt = [m.sb(f"mt{k}", [PARTS, SEQ], BF16) for k in range(2)]
        pick1 = m.sb("pick1", [PARTS, HEADS])
        pick = m.sb("pick", [PARTS, HEADS, SEQ], BF16)
        identf = m.sb("identf", [P, P])
        identb = m.sb("identb", [P, P], BF16)
        rec = m.sb("rec", [P, 3, SEQ])
        if rope:
            swapped = m.sb("swapped", [P, 3, CHUNK])
            cos = m.sb("cos", [P, CHUNK])
            sin = m.sb("sin", [P, CHUNK])
        s_ps = [m.psum(f"s_ps{k}", [P, 512]) for k in range(2)]
        st_ps = [m.psum(f"st_ps{k}", [P, 512]) for k in range(2)]
        proj_ps = m.psum("proj_ps", [P, 512])
        mt_ps = m.psum("mt_ps", [P, 1024], BF16)
        o_ps = [m.psum(f"o_ps{k}", [P, 512]) for k in range(2)]

        const_in, const_done = m.sem("const_in"), m.sem("const_done")
        x_in = [m.sem(f"x_in{k}") for k in range(2)]
        proj_done, proj_out = m.sem("proj_done"), m.sem("proj_out")
        swap_done, cos_done, sin_done, rope_done = (m.sem(x) for x in ("swap", "cos_mul", "sin_mul", "rope"))
        p1_done, r1_done, p2_done, p3_done = (m.sem(x) for x in ("p1", "r1", "p2", "p3"))
        stack_in = [m.sem(f"stack_in{k}") for k in range(2)]
        parts_out = [m.sem(f"parts_out{k}") for k in range(3)]
        s_done, max_done, msplit, mt_done, mt_out = (m.sem(x) for x in ("s_done", "max_done", "msplit", "mt_done", "mt_out"))
        st_done, exp_done, pv_done = m.sem("st_done"), m.sem("exp_done"), m.sem("pv_done")
        dve_turn, pe_turn, sp_turn = (m.sem(x) for x in ("dve_turn", "pe_turn", "sp_turn"))
        den_done, rec_done, norm_done = m.sem("den_done"), m.sem("rec_done"), m.sem("norm_done")
        N_CONST = 4 + (1 if bias_name else 0) + (2 if rope else 0)
        N_STACK = 16 * 2 * (PARTS // HD)
        N_DONE = 7 + (2 if bias_name else 0)

        def load_x(eng, i, k):
            start = CHUNK * (2 * i + k)
            eng.dma_start(xa[k][:, :], cols(xa_all, start, CHUNK)).then_inc(x_in[k], 16)
            eng.dma_start(xb[k][0:CB, :], cols(xb_all, start, CHUNK)).then_inc(x_in[k], 16)

        def run(eng_fori, pair):
            pair(0, False)
            with eng_fori(1, CHUNKS // 2 - 1) as i:
                pair(i, False)
            pair(CHUNKS // 2 - 1, True)

        with nc.Block() as block:
            @block.sync
            def _(sp):
                sp.dma_start(wa[:, :], d[w_name][0:P, :]).then_inc(const_in, 16)
                sp.dma_start(wb[0:CB, :], d[w_name][P:C, :]).then_inc(const_in, 16)
                if bias_name:
                    sp.dma_start(wb[CB:CB + 1, :], d[bias_name].rearrange("(a n) -> a n", a=1)).then_inc(const_in, 16)
                sp.dma_start(pick1[:, :], d["pick"]).then_inc(const_in, 16)
                sp.dma_start(identf[:, :], d["ident"]).then_inc(const_in, 16)
                load_x(sp, 0, 0)
                load_x(sp, 0, 1)
                if rope:
                    sp.dma_start(cos[:, :], d["cos"]).then_inc(const_in, 16)
                    sp.dma_start(sin[:, :], d["sin"]).then_inc(const_in, 16)

                def stack(i, k, used):
                    c = 2 * i + k
                    if not isinstance(i, int) or i:
                        hold(sp, stack_in[k], N_STACK * i, sp_turn)
                    for n, made in enumerate((p1_done, p2_done, p3_done)):
                        sp.wait_ge(made, c + 1)
                        for a in range(2):
                            sp.dma_start(parts_d[k, n, a].rearrange("(m p) t -> p m t", p=CB),
                                         part[n][CB * a:CB * a + CB, :, :]).then_inc(parts_out[n], 16)
                    for n in range(3):
                        hold(sp, parts_out[n], 32 * (c + 1), sp_turn)
                    after(sp, st_done, used)
                    for a, dst, which in ((0, qs[k], (0, 0, 1, 1, 0, 2)), (1, ks[k], (0, 1, 0, 1, 2, 0))):
                        for r, n in enumerate(which):
                            sp.dma_start(dst[HD * r:HD * r + HD, :, :],
                                         parts_d[k, n, a].rearrange("(h e) t -> e h t", e=HD)).then_inc(stack_in[k], 16)

                stack(0, 0, 0)

                def chunk(i, k, full, more):
                    c = 2 * i + k
                    if full:
                        sp.wait_ge(proj_done, 10 + 7 * c)
                        load_x(sp, i + 1, k)
                    if more:
                        stack(*((i, 1) if k == 0 else (i + 1, 0)), 8 * c)

                def pair(i, last):
                    for k in range(2):
                        chunk(i, k, not last, not (last and k == 1))

                run(sp.Fori, pair)

            @block.scalar
            def _(act):
                def project_out_qk(n, j, chunk_no):
                    act.wait_ge(proj_done, n + 1)
                    if j == 0:
                        after(act, r1_done, chunk_no)
                    act.activation(qk[:, j, :], proj_ps[:, 0:CHUNK], ACT.Copy).then_inc(proj_out, 1)

                def project_out_v(n, k, b, used):
                    act.wait_ge(proj_done, n + 1)
                    after(act, pv_done, used)
                    act.activation(vp[k][:, b, :, 0:HD], proj_ps[0:SEQ, 0:C].rearrange("p (h e) -> p h e", e=HD),
                                   ACT.Copy).then_inc(proj_out, 1)

                def part1(i, k):
                    if rope:
                        act.wait_ge(rope_done, 2 * i + k + 1)
                    after(act, parts_out[0], 32 * (2 * i + k))
                    act.activation(part[0][:, :, :], qk[:, :, :], ACT.Copy).then_inc(p1_done, 1)

                def part2(i, k):
                    act.wait_ge(r1_done, 2 * i + k + 1)
                    after(act, parts_out[1], 32 * (2 * i + k))
                    act.activation(part[1][:, :, :], rest[:, :, :], ACT.Copy).then_inc(p2_done, 1)

                act.wait_ge(const_done, N_DONE)
                for n in range(3):
                    project_out_qk(n, n, 0)
                if not rope:
                    act.wait_ge(proj_out, 3)
                part1(0, 0)
                for b in range(4):
                    project_out_v(3 + b, 0, b, 0)
                part2(0, 0)
                for n in range(3):
                    project_out_qk(7 + n, n, 1)
                if not rope:
                    act.wait_ge(proj_out, 10)
                part1(0, 1)
                part2(0, 1)

                def chunk(i, k, first, full, more):
                    c = 2 * i + k
                    for s in range(8):
                        g = 8 * c + s
                        if s % 2 == 0:
                            b_no = 4 * c + s // 2
                            act.wait_ge(mt_done, b_no + 1)
                            after(act, st_done, 2 * b_no - 2)
                            act.activation(mt[s // 2 % 2][0:3 * HEADS, :], mt_ps[0:3 * HEADS, 0:SEQ], ACT.Copy).then_inc(mt_out, 1)
                        act.wait_ge(st_done, g + 1)
                        after(act, pv_done, g - 1)
                        act.activation(pt[s % 2][:, :, :],
                                       st_ps[s % 2][0:SEQ, 0:6 * SEQ].rearrange("p (h t) -> p h t", t=SEQ),
                                       ACT.Exp, scale=HD ** -0.5).then_inc(exp_done, 1)
                        if more and s in VALUE_AT:
                            project_out_v(projections(c, s, full), 1 - k, VALUE_AT[s], 8 * c)
                        if full and s in QK_AT:
                            project_out_qk(projections(c, s, full), QK_AT[s], c + 2)
                        if s == (6 if rope else 4) and full:
                            if not rope:
                                act.wait_ge(proj_out, projections(c, 3, full) + 1)
                            part1(i + 1, k)
                        if s == 7 and full:
                            part2(i + 1, k)

                def pair(i, last):
                    for k in range(2):
                        chunk(i, k, isinstance(i, int) and i == 0 and k == 0, not last, not (last and k == 1))

                run(act.Fori, pair)

            @block.gpsimd
            def _(pool):
                pool.memset(vp[0][:, :, :, HD:], 1.0).then_inc(const_done, 1)
                pool.memset(vp[1][:, :, :, HD:], 1.0).then_inc(const_done, 1)
                pool.memset(ot_all[:, :, TOKENS:ROWS], 0.0).then_inc(const_done, 1)
                pool.wait_ge(const_in, 16 * N_CONST)

                def chunk(i, k):
                    c = 2 * i + k
                    ready = 10 + 7 * (c - 2) + 4
                    if isinstance(c, int) and c < 2:
                        ready = (3, 10)[c]
                    after(pool, p3_done, c)
                    if rope:
                        pool.wait_ge(proj_out, ready)
                        pool.tensor_tensor(rest[:, :, :], qk[:, :, :], cos[:, :].unsqueeze(1).to_broadcast([P, 3, CHUNK]),
                                           ALU.mult).then_inc(cos_done, 1)
                        pool.wait_ge(rope_done, c + 1)
                    pool.wait_ge(p1_done, c + 1)
                    pool.tensor_tensor(rest[:, :, :], qk[:, :, :], part[0][:, :, :], ALU.subtract).then_inc(r1_done, 1)
                    pool.wait_ge(p2_done, c + 1)
                    after(pool, parts_out[2], 32 * c)
                    pool.tensor_tensor(part[2][:, :, :], rest[:, :, :], part[1][:, :, :], ALU.subtract).then_inc(p3_done, 1)

                chunk(0, 0)
                chunk(0, 1)
                with pool.Fori(1, CHUNKS // 2) as i:
                    for k in range(2):
                        chunk(i, k)

            @block.vector
            def _(dve):
                if bias_name:
                    for k in range(2):
                        dve.memset(xb[k][CB:CB + 1, :], 1.0).then_inc(const_done, 1)
                for k in range(2):
                    dve.memset(mt[k][:, :], 0.0).then_inc(const_done, 1)
                dve.wait_ge(const_in, 16 * N_CONST)
                dve.tensor_copy(identb[:, :], identf[:, :]).then_inc(const_done, 1)
                dve.tensor_copy(pick[:, :, :], pick1[:, :].unsqueeze(2).to_broadcast([PARTS, HEADS, SEQ])).then_inc(const_done, 1)

                def rope_swap(c, ready):
                    after(dve, rope_done, c)
                    hold(dve, proj_out, ready, dve_turn)
                    dve.stream_shuffle(swapped[:, :, :], qk[:, :, :], [l ^ 8 for l in range(32)]).then_inc(swap_done, 1)

                def rope_add(c):
                    dve.wait_ge(swap_done, c + 1)
                    dve.tensor_tensor(swapped[:, :, :], swapped[:, :, :], sin[:, :].unsqueeze(1).to_broadcast([P, 3, CHUNK]),
                                      ALU.mult).then_inc(sin_done, 1)
                    dve.wait_ge(sin_done, c + 1)
                    dve.wait_ge(cos_done, c + 1)
                    dve.tensor_tensor(qk[:, :, :], swapped[:, :, :], rest[:, :, :], ALU.add).then_inc(rope_done, 1)

                def negmax(g, place):
                    dve.wait_ge(s_done, g + 1)
                    half, b2 = place % 2, place // 2
                    dve.tensor_reduce(nm[b2][:, 6 * half:6 * half + 6],
                                      s_ps[half][0:SEQ, 0:6 * SEQ].rearrange("p (h t) -> p h t", t=SEQ),
                                      AX_X, ALU.max, negate=True).then_inc(max_done, 1)

                def split_max(b_no, b2):
                    x, r, s = nm[b2], nmr[b2], ms[b2]
                    dve.wait_ge(max_done, 2 * b_no + 2)
                    after(dve, mt_done, b_no - 1)
                    dve.tensor_copy(s[:, 0, :], x[:, :]).then_inc(msplit, 1)
                    dve.wait_ge(msplit, 4 * b_no + 1)
                    dve.tensor_tensor(r[:, :], x[:, :], s[:, 0, :], ALU.subtract).then_inc(msplit, 1)
                    dve.wait_ge(msplit, 4 * b_no + 2)
                    dve.tensor_copy(s[:, 1, :], r[:, :]).then_inc(msplit, 1)
                    dve.wait_ge(msplit, 4 * b_no + 3)
                    dve.tensor_tensor(s[:, 2, :], r[:, :], s[:, 1, :], ALU.subtract).then_inc(msplit, 1)

                def normalize(b_no, b2):
                    after(dve, norm_done, b_no)
                    hold(dve, pv_done, 2 * b_no + 2, dve_turn)
                    o = o_ps[b2][:, 0:3 * SEQ].rearrange("p (g t) -> p g t", t=SEQ)
                    dve.stream_shuffle(rec[:, :, :], o, [HD + l % HD for l in range(32)]).then_inc(den_done, 1)
                    dve.wait_ge(den_done, b_no + 1)
                    dve.reciprocal(rec[:, :, :], rec[:, :, :]).then_inc(rec_done, 1)
                    dve.wait_ge(rec_done, b_no + 1)
                    dve.tensor_tensor(ot_all[:, :, bass.ds(b_no * SEQ, SEQ)], o, rec[:, :, :], ALU.mult).then_inc(norm_done, 1)

                if rope:
                    rope_swap(0, 3)
                    rope_add(0)
                    rope_swap(1, 10)
                    rope_add(1)
                negmax(0, 0)
                negmax(1, 1)
                split_max(0, 0)
                negmax(2, 2)

                def chunk(i, k, first, full, more):
                    c = 2 * i + k
                    for s in range(8):
                        g = 8 * c + s
                        if more or s < 5:
                            negmax(g + 3, (s + 3) % 4)
                            if s % 2 == 0:
                                split_max(4 * c + s // 2 + 1, (s // 2 + 1) % 2)
                        if s % 2 == 0 and not (first and s == 0):
                            normalize(4 * c + s // 2 - 1, (s // 2 + 1) % 2)
                        if rope and full:
                            if s == 4:
                                rope_swap(c + 2, projections(c, 3, full) + 1)
                            if s == 5:
                                rope_add(c + 2)

                def pair(i, last):
                    for k in range(2):
                        chunk(i, k, isinstance(i, int) and i == 0 and k == 0, not last, not (last and k == 1))

                run(dve.Fori, pair)
                normalize(BATCH - 1, 1)
                dve.wait_ge(norm_done, BATCH)

            @block.tensor
            def _(pe):
                def project_qk(n, k, j, loads):
                    pe.wait_ge(x_in[k], 32 * loads)
                    after(pe, proj_out, n)
                    w = slice(P * j, P * j + P)
                    pe.matmul(proj_ps[:, 0:CHUNK], wa[:, w], xa[k][:, :], start=True, stop=False)
                    pe.matmul(proj_ps[:, 0:CHUNK], wb[:, w], xb[k][:, :], start=False, stop=True).then_inc(proj_done, 1)

                def project_v(n, k, b, loads):
                    pe.wait_ge(x_in[k], 32 * loads)
                    after(pe, proj_out, n)
                    t = slice(SEQ * b, SEQ * b + SEQ)
                    pe.matmul(proj_ps[0:SEQ, 0:C], xa[k][:, t], wa[:, 2 * C:3 * C], start=True, stop=False)
                    pe.matmul(proj_ps[0:SEQ, 0:C], xb[k][:, t], wb[:, 2 * C:3 * C], start=False, stop=True).then_inc(proj_done, 1)

                def score(g, i, k, b, half):
                    if b == 0 and half == 0:
                        pe.wait_ge(stack_in[k], N_STACK * (i + 1))
                    after(pe, max_done, g - 1)
                    for j in range(6):
                        t = slice(SEQ * b, SEQ * b + SEQ)
                        mm = pe.matmul(s_ps[half][0:SEQ, SEQ * j:SEQ * j + SEQ], qs[k][:, 6 * half + j, t],
                                       ks[k][:, 6 * half + j, t], start=True, stop=True)
                    mm.then_inc(s_done, 1)

                pe.wait_ge(const_in, 16 * N_CONST)
                pe.wait_ge(const_done, N_DONE)
                for j in range(3):
                    project_qk(j, 0, j, 1)
                for b in range(4):
                    project_v(3 + b, 0, b, 1)
                for j in range(3):
                    project_qk(7 + j, 1, j, 1)
                for g in range(3):
                    score(g, 0, 0, g // 2, g % 2)

                def values(c, k, b, half):
                    b_no, b2 = 4 * c + b, b % 2
                    pe.wait_ge(exp_done, 2 * b_no + half + 1)
                    if half == 0:
                        after(pe, norm_done, b_no - 1)
                    for j in range(6):
                        head = 6 * half + j
                        lane = 2 * HD * (head % 4)
                        col = SEQ * (head // 4)
                        mm = pe.matmul(o_ps[b2][lane:lane + 2 * HD, col:col + SEQ], vp[k][:, b, head, :],
                                       pt[half][:, j, :], start=True, stop=True, tile_position=(0, lane))
                    mm.then_inc(pv_done, 1)

                def chunk(i, k, first, full, more):
                    c = 2 * i + k
                    for s in range(8):
                        g = 8 * c + s
                        b_no, b, half, b2 = 4 * c + s // 2, s // 2, s % 2, s // 2 % 2
                        if half == 0:
                            after(pe, mt_out, b_no)
                            hold(pe, msplit, 4 * b_no + 4, pe_turn)
                            pe.transpose(mt_ps[0:3 * HEADS, 0:SEQ], ms[b2][:, :, :].rearrange("p a h -> p (a h)"),
                                         identb[0:SEQ, 0:SEQ]).then_inc(mt_done, 1)
                        if more or s < 5:
                            ahead = (i, k) if s < 5 else ((i, 1) if k == 0 else (i + 1, 0))
                            score(g + 3, *ahead, (s + 3) // 2 % 4, (s + 3) % 2)
                        if more and s in VALUE_AT:
                            project_v(projections(c, s, full), 1 - k, VALUE_AT[s], i + 1 + k)
                        if full and s in QK_AT:
                            project_qk(projections(c, s, full), k, QK_AT[s], i + 2)
                        if half == 0:
                            pe.wait_ge(mt_out, b_no + 1)
                        after(pe, exp_done, g - 1)
                        t = slice(SEQ * b, SEQ * b + SEQ)
                        for j in range(6):
                            o = st_ps[half][0:SEQ, SEQ * j:SEQ * j + SEQ]
                            pe.matmul(o, ks[k][:, 6 * half + j, t], qs[k][:, 6 * half + j, t], start=True, stop=False)
                            mm = pe.matmul(o, pick[:, 6 * half + j, :], mt[b2][:, :], start=False, stop=True)
                        mm.then_inc(st_done, 1)
                        if not (first and s == 0):
                            if s == 0:
                                values(c - 1, 1 - k, 3, 1)
                            else:
                                values(c, k, (s - 1) // 2, (s - 1) % 2)

                def pair(i, last):
                    for k in range(2):
                        chunk(i, k, isinstance(i, int) and i == 0 and k == 0, not last, not (last and k == 1))

                run(pe.Fori, pair)
                values(CHUNKS - 1, 1, 3, 1)



def load_heads(sp, ots, ots_in, acc_done, ot_all, g):
    for k in range(4):
        after(sp, acc_done, 4 * g - 3 + k if not isinstance(g, int) or g else 0)
        sp.dma_start(ots[k][:, :, :], ot_all[:, :, bass.ds(512 * g + P * k, P)]).then_inc(ots_in[k], 16)


def project_heads(pe, ots, ots_in, acc, acc_done, wp, g, acc_used):
    for k in range(4):
        pe.wait_ge(ots_in[k], 16 * (g + 1))
        after(pe, acc_used, 4 * g - 3 + k if not isinstance(g, int) or g else 0)
        for s in range(3):
            mm = pe.matmul(acc[k][:, 0:C], ots[k][:, s, :], wp[:, s, :], start=(s == 0), stop=(s == 2))
        mm.then_inc(acc_done, 1)


def groups(fori, group):
    group(0)
    with fori(1, GROUPS) as g:
        group(g)


def in_pairs(fori, group):
    group(1, 1)
    group(2, 0)
    with fori(2, GROUPS // 2) as i:
        group(2 * i - 1, 1)
        group(2 * i, 0)
    group(GROUPS - 2, 1)
    group(GROUPS - 1, 0)


def between(nc, d, h, ot_all, xa_all, xb_all, kept_d):
    with ExitStack() as ctx:
        m = Memory(nc, ctx, "mid")
        ident = m.sb("ident", [P, P])
        wp = m.sb("wp", [P, 3, C])
        gain = m.sb("gain", [P, 4])
        ots = [m.sb(f"ots{k}", [P, 3, P]) for k in range(4)]
        hp = m.sb("hp", [P, 4, C])
        xn = [m.sb(f"xn{k}", [P, C]) for k in range(4)]
        n1, n2 = NormGroup(m, "n1"), NormGroup(m, "n2")
        acc = [m.psum(f"acc{k}", [P, 512]) for k in range(4)]
        ta = m.psum("ta", [P, 512])
        tb = m.psum("tb", [P, 512])
        const_in = m.sem("const_in")
        ots_in = [m.sem(f"ots_in{k}") for k in range(4)]
        acc_done, hp_done, kept, y_done, xn_done, t_done, t_out = (
            m.sem(x) for x in ("acc_done", "hp_done", "kept", "y_done", "xn_done", "t_done", "t_out"))
        with nc.Block() as block:
            @block.sync
            def _(sp):
                sp.dma_start(ident[:, :], d["ident"]).then_inc(const_in, 16)
                sp.dma_start(wp[:, :, :], d["proj1_w"]).then_inc(const_in, 16)
                for j, name in enumerate(("ln1_g", "ln1_b")):
                    sp.dma_start(gain[:, j:j + 1], d[name][0:P].rearrange("(p a) -> p a", a=1)).then_inc(const_in, 16)
                    sp.dma_start(gain[0:CB, 2 + j:3 + j], d[name][P:C].rearrange("(p a) -> p a", a=1)).then_inc(const_in, 16)
                load_heads(sp, ots, ots_in, acc_done, ot_all, 0)

                def group(g, last=False):
                    if not last:
                        load_heads(sp, ots, ots_in, acc_done, ot_all, g + 1)
                    sp.wait_ge(hp_done, 4 * g + 4)
                    sp.dma_start(kept_d[bass.ds(512 * g, 512), :].rearrange("(t p) c -> p t c", p=P), hp[:, :, :]).then_inc(kept, 16)

                with sp.Fori(0, GROUPS - 1) as g:
                    group(g)
                group(GROUPS - 1, True)
                sp.wait_ge(kept, 16 * GROUPS)

            @block.vector
            def _(dve):
                def group(g):
                    rows = [tile_of(h, 4 * g + k) for k in range(4)]
                    hs = [hp[:, k, :] for k in range(4)]
                    after(dve, kept, 16 * g)
                    for k in range(4):
                        dve.wait_ge(acc_done, 4 * g + k + 1)
                        dve.tensor_tensor(hs[k], acc[k][:, 0:C], rows[k], ALU.add).then_inc(hp_done, 1)
                    norm_stats(dve, n1, hs, g + 1, hp_done)
                    norm_apply(dve, n1, rows, hs, g + 1, y_done)
                    norm_stats(dve, n2, rows, g + 1, y_done)
                    after(dve, t_done, g)
                    norm_apply(dve, n2, [x[:, :] for x in xn], rows, g + 1, xn_done)

                groups(dve.Fori, group)

            @block.scalar
            def _(act):
                act.wait_ge(const_in, 16 * 6)

                def group(g):
                    norm_root(act, n1, g + 1)
                    norm_root(act, n2, g + 1)
                    act.wait_ge(t_done, g + 1)
                    act.activation(cols(xa_all, 512 * g, 512), ta[:, :], ACT.Identity, scale=gain[:, 0:1], bias=gain[:, 1:2]).then_inc(t_out, 1)
                    act.activation(cols(xb_all, 512 * g, 512), tb[0:CB, :], ACT.Identity, scale=gain[0:CB, 2:3], bias=gain[0:CB, 3:4]).then_inc(t_out, 1)

                groups(act.Fori, group)

            @block.tensor
            def _(pe):
                pe.wait_ge(const_in, 16 * 6)

                def transposes(g):
                    after(pe, t_out, 2 * g)
                    for k in range(4):
                        pe.wait_ge(xn_done, 4 * g + k + 1)
                        pe.transpose(ta[:, P * k:P * k + P], xn[k][:, 0:P], ident[:, :])
                        mm = pe.transpose(tb[0:CB, P * k:P * k + P], xn[k][:, P:C], ident[:, :])
                    mm.then_inc(t_done, 1)

                project_heads(pe, ots, ots_in, acc, acc_done, wp, 0, hp_done)
                with pe.Fori(1, GROUPS) as g:
                    project_heads(pe, ots, ots_in, acc, acc_done, wp, g, hp_done)
                    transposes(g - 1)
                transposes(GROUPS - 1)


def dispatch(nc, d, h, ot_all, kept_d, queue_d, keep):
    with ExitStack() as ctx:
        m = Memory(nc, ctx, "disp")
        ident = m.sb("ident", [P, P])
        wp = m.sb("wp", [P, 3, C])
        gain = m.sb("gain", [P, 4])
        gate_a = m.sb("gate_a", [P, EXPERTS])
        gate_c = m.sb("gate_c", [CB, EXPERTS])
        gate_b = m.sb("gate_b", [P, EXPERTS])
        trif = m.sb("trif", [P, P])
        tri = m.sb("tri", [P, P], BF16)
        ones = m.sb("ones", [P, P], BF16)
        eight = m.sb("eight", [P, EXPERTS])
        region = m.sb("region", [P, EXPERTS])
        valid = m.sb("valid", [P, TILES])
        dump = m.sb("dump", [P, TILES, 2])
        ots = [m.sb(f"ots{k}", [P, 3, P]) for k in range(4)]
        xp = m.sb("xp", [P, 4, C])
        hk = m.sb("hk", [P, 4, C])
        picked = m.sb("picked", [P, 4, 2, EXPERTS])
        sl = m.sb("sl", [P, 4, 2])
        z0 = [m.sb(f"z0_{k}", [P, 4, QUEUED]) for k in range(2)]
        z1 = [m.sb(f"z1_{k}", [P, 4, QUEUED]) for k in range(2)]
        result_row = m.sb("result_row", [P, TILES, 2])
        za = m.sb("za", [P, 512])
        zb = m.sb("zb", [CB, 512])
        lg = m.sb("lg", [P, 4, EXPERTS])
        v8 = m.sb("v8", [P, 4, EXPERTS])
        i8 = m.sb("i8", [P, 4, EXPERTS], U32)
        idf = m.sb("idf", [P, 4, 2])
        mb = m.sb("mb", [P, 4, EXPERTS], BF16)
        seen_f = m.sb("seen_f", [P, EXPERTS])
        seen = m.sb("seen", [P, EXPERTS], BF16)
        group_sum = m.sb("group_sum", [P, EXPERTS])
        rank = m.sb("rank", [P, 4, EXPERTS])
        prod = m.sb("prod", [P, 4, 2, EXPERTS])
        slot_i = [m.sb(f"slot_i{k}", [P, 8], I32) for k in range(2)]
        n = NormGroup(m, "n3")
        acc = [m.psum(f"acc{k}", [P, 512]) for k in range(4)]
        ta = m.psum("ta", [P, 512])
        tb = m.psum("tb", [P, 512])
        lg_ps = m.psum("lg_ps", [P, 512])
        rk_ps = m.psum("rk_ps", [P, 512])
        const_in = m.sem("const_in")
        N_CONST = 15
        ots_in = [m.sem(f"ots_in{k}") for k in range(4)]
        (acc_done, z1_done, xp_done, hk_in, sum_done, z_done, t_done, z_out, lg_done, lg_out, top, pick, seen_done,
         rank_done, slot, sent, prep) = (m.sem(x) for x in (
             "acc_done", "z1_done", "xp_done", "hk_in", "sum_done", "z_done", "t_done", "z_out", "lg_done", "lg_out",
             "top", "pick", "seen_done", "rank_done", "slot", "sent", "prep"))
        pool_turn = m.sem("pool_turn")
        top2, counts = keep
        with nc.Block() as block:
            @block.sync
            def _(sp):
                def const(dst, src):
                    sp.dma_start(dst, src).then_inc(const_in, 16)

                const(ident[:, :], d["ident"])
                const(wp[:, :, :], d["proj2_w"])
                const(result_row[:, :, :], d["result_row"])
                for j, name in enumerate(("ln2_g", "ln2_b")):
                    const(gain[:, j:j + 1], d[name][0:P].rearrange("(p a) -> p a", a=1))
                    const(gain[0:CB, 2 + j:3 + j], d[name][P:C].rearrange("(p a) -> p a", a=1))
                const(gate_a[:, :], d["gate_wT"][0:P, :])
                const(gate_c[:, :], d["gate_wT"][P:C, :])
                const(gate_b[:, :], d["gate_b"].partition_broadcast(P))
                const(trif[:, :], d["tri"])
                const(eight[:, :], d["eight"])
                const(region[:, :], d["region"])
                const(valid[:, :], d["valid"])
                const(dump[:, :, :], d["dump"])
                load_heads(sp, ots, ots_in, acc_done, ot_all, 0)

                def group(g, last=False):
                    after(sp, sum_done, g)
                    sp.dma_start(hk[:, :, :], kept_d[bass.ds(512 * g, 512), :].rearrange("(t p) c -> p t c", p=P)).then_inc(hk_in, 16)
                    if not last:
                        load_heads(sp, ots, ots_in, acc_done, ot_all, g + 1)

                group(0)
                with sp.Fori(1, GROUPS - 1) as g:
                    group(g)
                group(GROUPS - 1, True)

            @block.gpsimd
            def _(pool):
                pool.memset(ones[:, :], 1.0).then_inc(prep, 1)

                def send(g, k):
                    pool.wait_ge(z1_done, 3 * g + 3)
                    hold(pool, slot, 4 * g + 4, pool_turn)
                    for j in range(8):
                        z = (z0, z1)[j % 2][k]
                        pool.indirect_dma_start(queue_d, bass.IndirectOffsetOnAxis(slot_i[k][:, j:j + 1], 0),
                                                z[:, j // 2, :], None).then_inc(sent, 16)

                send(0, 0)
                in_pairs(pool.Fori, send)
                pool.wait_ge(sent, 128 * GROUPS)

            @block.vector
            def _(dve):
                dve.memset(seen_f[:, :], 0.0).then_inc(prep, 1)
                dve.memset(seen[:, :], 0.0).then_inc(prep, 1)
                dve.wait_ge(const_in, 16 * N_CONST)
                dve.tensor_copy(tri[:, :], trif[:, :]).then_inc(prep, 1)

                xs = [xp[:, k, :] for k in range(4)]

                def rows_and_stats(g):
                    rows = [tile_of(h, 4 * g + k) for k in range(4)]
                    after(dve, z_done, 4 * g)
                    after(dve, sum_done, g)
                    for k in range(4):
                        dve.wait_ge(acc_done, 4 * g + k + 1)
                        dve.tensor_tensor(xs[k], acc[k][:, 0:C], rows[k], ALU.add).then_inc(xp_done, 1)
                    norm_stats(dve, n, xs, g + 1, xp_done)

                def normalized(g, k):
                    after(dve, sent, 128 * (g - 1))
                    after(dve, t_done, g - 1)
                    after(dve, z1_done, 3 * (g - 1))
                    norm_apply(dve, n, [z0[k][:, t, 1:QUEUED] for t in range(4)], xs, g + 1, z_done)
                    dve.wait_ge(hk_in, 16 * (g + 1))
                    dve.tensor_tensor(h[:, bass.ds(4 * g, 4), :], hk[:, :, :], xp[:, :, :], ALU.add).then_inc(sum_done, 1)

                def choose(g):
                    dve.wait_ge(lg_done, g + 1)
                    dve.tensor_tensor(lg[:, :, :], lg_ps[:, 0:32].rearrange("p (k e) -> p k e", e=EXPERTS),
                                      gate_b[:, :].unsqueeze(1).to_broadcast([P, 4, EXPERTS]), ALU.add).then_inc(lg_out, 1)
                    hold(dve, lg_out, g + 1, n.turn)
                    for k in range(4):
                        dve.max(v8[:, k, :], lg[:, k, :]).then_inc(top, 1)
                    hold(dve, top, 8 * g + 4, n.turn)
                    for k in range(4):
                        dve.max_index(i8[:, k, :], v8[:, k, :], lg[:, k, :]).then_inc(top, 1)
                    dve.tensor_copy(top2[:, bass.ds(4 * g, 4), :], v8[:, :, 0:2]).then_inc(pick, 1)
                    dve.wait_ge(top, 8 * g + 8)
                    dve.tensor_copy(idf[:, :, :], i8[:, :, 0:2]).then_inc(pick, 1)
                    dve.wait_ge(pick, 5 * g + 2)
                    for j in range(2):
                        dve.tensor_tensor(picked[:, :, j, :], eight[:, :].unsqueeze(1).to_broadcast([P, 4, EXPERTS]),
                                          idf[:, :, j:j + 1].to_broadcast([P, 4, EXPERTS]), ALU.is_equal).then_inc(pick, 1)
                    dve.wait_ge(pick, 5 * g + 4)
                    v = valid[:, bass.ds(4 * g, 4)]
                    dve.tensor_tensor(picked[:, :, :, :].rearrange("p t j e -> p t (j e)"), picked[:, :, :, :].rearrange("p t j e -> p t (j e)"),
                                      v.unsqueeze(2).to_broadcast([P, 4, 16]), ALU.mult).then_inc(pick, 1)
                    dve.wait_ge(pick, 5 * g + 5)
                    after(dve, rank_done, g)
                    dve.tensor_tensor(mb[:, :, :], picked[:, :, 0, :], picked[:, :, 1, :], ALU.add).then_inc(seen_done, 1)

                def place(g, k):
                    dve.wait_ge(seen_done, 2 * g + 1)
                    dve.tensor_reduce(group_sum[:, :], mb[:, :, :].rearrange("p k e -> p e k"), AX_X, ALU.add).then_inc(slot, 1)
                    dve.wait_ge(rank_done, g + 1)
                    dve.tensor_tensor(rank[:, :, :], rk_ps[:, 0:32].rearrange("p (k e) -> p k e", e=EXPERTS),
                                      region[:, :].unsqueeze(1).to_broadcast([P, 4, EXPERTS]), ALU.add).then_inc(slot, 1)
                    dve.wait_ge(slot, 4 * g + 2)
                    dve.tensor_tensor(seen_f[:, :], seen_f[:, :], group_sum[:, :], ALU.add).then_inc(lg_out_2, 1)
                    for j in range(2):
                        dve.tensor_tensor(prod[:, :, j, :], picked[:, :, j, :], rank[:, :, :], ALU.mult).then_inc(prod_done, 1)
                    dve.wait_ge(prod_done, 2 * g + 2)
                    dve.wait_ge(lg_out_2, g + 1)
                    dve.tensor_copy(seen[:, :], seen_f[:, :]).then_inc(seen_done, 1)
                    after(dve, sent, 128 * (g - 1))
                    dve.tensor_reduce(sl[:, :, :], prod[:, :, :, :], AX_X, ALU.add).then_inc(slot, 1)
                    dve.wait_ge(slot, 4 * g + 3)
                    dve.tensor_tensor(slot_i[k][:, :].rearrange("p (k j) -> p k j", j=2), sl[:, :, :],
                                      dump[:, bass.ds(4 * g, 4), :], ALU.add).then_inc(slot, 1)

                lg_out_2, prod_done = m.sem("seen_sum"), m.sem("prod_done")
                rows_and_stats(0)
                normalized(0, 0)

                def group(g, k):
                    rows_and_stats(g)
                    choose(g - 1)
                    normalized(g, k)
                    place(g - 1, 1 - k)

                in_pairs(dve.Fori, group)
                choose(GROUPS - 1)
                place(GROUPS - 1, 0)
                dve.wait_ge(rank_done, GROUPS + 1)
                dve.tensor_copy(counts[:, :], rk_ps[:, 64:64 + EXPERTS]).then_inc(prep, 1)
                dve.wait_ge(prep, 5)

            @block.scalar
            def _(act):
                act.wait_ge(const_in, 16 * N_CONST)

                def group(g, k):
                    norm_root(act, n, g + 1)
                    after(act, sent, 128 * (g - 1))
                    for j, z in enumerate((z0, z1)):
                        act.activation(z[k][:, :, 0], result_row[:, bass.ds(4 * g, 4), j], ACT.Copy).then_inc(z1_done, 1)
                    act.wait_ge(z_done, 4 * g + 4)
                    act.activation(z1[k][:, :, 1:QUEUED], z0[k][:, :, 1:QUEUED], ACT.Copy).then_inc(z1_done, 1)
                    act.wait_ge(t_done, g + 1)
                    after(act, lg_done, g)
                    act.activation(za[:, :], ta[:, :], ACT.Identity, scale=gain[:, 0:1], bias=gain[:, 1:2]).then_inc(z_out, 1)
                    act.activation(zb[:, :], tb[0:CB, :], ACT.Identity, scale=gain[0:CB, 2:3], bias=gain[0:CB, 3:4]).then_inc(z_out, 1)

                group(0, 0)
                in_pairs(act.Fori, group)

            @block.tensor
            def _(pe):
                pe.wait_ge(const_in, 16 * N_CONST)
                pe.wait_ge(prep, 4)

                def route(g, b2):
                    after(pe, z_out, 2 * g)
                    for k in range(4):
                        pe.wait_ge(z_done, 4 * g + k + 1)
                        pe.transpose(ta[:, P * k:P * k + P], z0[b2][:, k, 1:1 + P], ident[:, :])
                        mm = pe.transpose(tb[0:CB, P * k:P * k + P], z0[b2][:, k, 1 + P:QUEUED], ident[:, :])
                    mm.then_inc(t_done, 1)
                    pe.wait_ge(z_out, 2 * g + 2)
                    after(pe, lg_out, g)
                    for k in range(4):
                        o = lg_ps[:, EXPERTS * k:EXPERTS * k + EXPERTS]
                        pe.matmul(o, za[:, P * k:P * k + P], gate_a[:, :], start=True, stop=False)
                        mm = pe.matmul(o, zb[:, P * k:P * k + P], gate_c[:, :], start=False, stop=True)
                    mm.then_inc(lg_done, 1)

                def count(g):
                    pe.wait_ge(seen_done, 2 * g + 1)
                    after(pe, slot, 4 * g)
                    for k in range(4):
                        o = rk_ps[:, EXPERTS * k:EXPERTS * k + EXPERTS]
                        pe.matmul(o, tri[:, :], mb[:, k, :], start=True, stop=False)
                        for j in range(k):
                            pe.matmul(o, ones[:, :], mb[:, j, :], start=False, stop=False)
                        mm = pe.matmul(o, ones[:, :], seen[:, :], start=False, stop=True)
                    mm.then_inc(rank_done, 1)

                project_heads(pe, ots, ots_in, acc, acc_done, wp, 0, xp_done)
                project_heads(pe, ots, ots_in, acc, acc_done, wp, 1, xp_done)

                def group(g, k):
                    route(g - 1, 1 - k)
                    if not (isinstance(g, int) and g == GROUPS - 1):
                        project_heads(pe, ots, ots_in, acc, acc_done, wp, g + 1, xp_done)
                    count(g - 1)

                in_pairs(pe.Fori, group)
                route(GROUPS - 1, 0)
                count(GROUPS - 1)
                pe.wait_ge(seen_done, 2 * GROUPS)
                pe.wait_ge(slot, 4 * GROUPS)
                pe.matmul(rk_ps[:, 64:64 + EXPERTS], ones[:, :], seen[:, :], start=True, stop=True).then_inc(rank_done, 1)


def plan(nc, d, queue_d, keep, shares, table):
    top2, counts = keep
    with ExitStack() as ctx:
        m = Memory(nc, ctx, "plan")
        eight = m.sb("eight", [P, EXPERTS])
        region = m.sb("region", [P, EXPERTS])
        number = m.sb("number", [P, TUNE])
        cf = m.sb("cf", [P, EXPERTS])
        ci = m.sb("ci", [P, EXPERTS], I32)
        ct = m.sb("ct", [P, EXPERTS], I32)
        tiles = m.sb("tiles", [P, EXPERTS])
        end = [m.sb(f"end{k}", [P, EXPERTS]) for k in range(2)]
        begin = m.sb("begin", [P, EXPERTS])
        fill = m.sb("fill", [P, EXPERTS], I32)
        tn = m.sb("tn", [P, MOE_TILES])
        cmp = m.sb("cmp", [P, MOE_TILES, EXPERTS])
        te = m.sb("te", [P, MOE_TILES])
        hot = m.sb("hot", [P, MOE_TILES, EXPERTS])
        first = m.sb("first", [P, MOE_TILES])
        real = m.sb("real", [P, MOE_TILES])
        local = m.sb("local", [P, MOE_TILES])
        base = m.sb("base", [P, MOE_TILES])
        diff = m.sb("diff", [P, TILES])
        ex = m.sb("ex", [P, TILES])
        den = m.sb("den", [P, TILES])
        filler = m.sb("filler", [P, 4, C])
        filler_row = m.sb("filler_row", [P, EXPERTS + 2, 4])
        surplus_row = m.sb("surplus_row", [P, MOE_TILES])
        const_in, step, filled, ex_done, diff_done = (
            m.sem(x) for x in ("const_in", "step", "filled", "ex_done", "diff_done"))
        table_done = m.sem("table_done")
        with nc.Block() as block:
            @block.sync
            def _(sp):
                sp.dma_start(eight[:, :], d["eight"]).then_inc(const_in, 16)
                sp.dma_start(region[:, :], d["region"]).then_inc(const_in, 16)
                sp.dma_start(number[:, :], d["number"]).then_inc(const_in, 16)
                sp.dma_start(filler_row[:, :, :], d["filler_row"]).then_inc(const_in, 16)
                sp.dma_start(surplus_row[:, :], d["surplus_row"]).then_inc(const_in, 16)
                sp.wait_ge(const_in, 80)

                def fill_rows(start, e):
                    rows = queue_d[bass.ds(start, SLOTS), :].rearrange("(t p) c -> p t c", p=P)
                    sp.dma_start(rows[:, :, 1:QUEUED], filler[:, :, :]).then_inc(filled, 16)
                    sp.dma_start(rows[:, :, 0:1], filler_row[:, e, :].unsqueeze(2), allow_slow_non_contiguous=True).then_inc(filled, 16)

                sp.wait_ge(table_done, 1)
                for k in range(2):
                    fill_rows(SURPLUS + SLOTS * k, EXPERTS + k)
                sp.wait_ge(table_done, 2)
                for e in range(EXPERTS):
                    start = sp.value_load(fill[0:1, e:e + 1], min_val=e * REGION, max_val=e * REGION + TOKENS)
                    fill_rows(start, e)
                sp.wait_ge(filled, 32 * (EXPERTS + 2))

            @block.scalar
            def _(act):
                act.wait_ge(diff_done, 1)
                act.activation(ex[:, :], diff[:, :], ACT.Exp).then_inc(ex_done, 1)

            @block.vector
            def _(dve):
                said = [0]

                def then(ins):
                    said[0] += 1
                    ins.then_inc(step, 1)
                    dve.wait_ge(step, said[0])

                dve.tensor_tensor(diff[:, :], top2[:, :, 1], top2[:, :, 0], ALU.subtract).then_inc(diff_done, 1)
                dve.memset(filler[:, :, :], 0.0).then_inc(table_done, 1)
                dve.wait_ge(const_in, 80)
                then(dve.tensor_scalar(ci[:, :], counts[:, :], float(SLOTS - 1), None, ALU.add))
                then(dve.tensor_scalar(ct[:, :], ci[:, :], SLOTS.bit_length() - 1, None, ALU.logical_shift_right))
                then(dve.tensor_copy(tiles[:, :], ct[:, :]))
                dve.tensor_tensor(fill[:, :], counts[:, :], region[:, :], ALU.add).then_inc(table_done, 1)
                src = tiles
                for k, by in enumerate((1, 2, 4)):
                    dst = end[k % 2]
                    then(dve.tensor_copy(dst[:, :], src[:, :]))
                    then(dve.tensor_tensor(dst[:, by:], src[:, by:], src[:, :EXPERTS - by], ALU.add))
                    src = dst
                then(dve.tensor_tensor(begin[:, :], src[:, :], tiles[:, :], ALU.subtract))
                shape = [P, MOE_TILES, EXPERTS]
                then(dve.tensor_scalar(tn[:, :], number[:, 0:MOE_TILES], -1.0, None, ALU.add))
                then(dve.tensor_tensor(cmp[:, :, :], tn[:, :].unsqueeze(2).to_broadcast(shape),
                                       src[:, :].unsqueeze(1).to_broadcast(shape), ALU.is_ge))
                then(dve.tensor_reduce(te[:, :], cmp[:, :, :], AX_X, ALU.add))
                then(dve.tensor_tensor(hot[:, :, :], te[:, :].unsqueeze(2).to_broadcast(shape),
                                       eight[:, :].unsqueeze(1).to_broadcast(shape), ALU.is_equal))
                then(dve.tensor_tensor(hot[:, :, :], hot[:, :, :], begin[:, :].unsqueeze(1).to_broadcast(shape), ALU.mult))
                then(dve.tensor_reduce(first[:, :], hot[:, :, :], AX_X, ALU.add))
                then(dve.tensor_scalar(real[:, :], te[:, :], EXPERTS - 0.5, None, ALU.is_lt))
                then(dve.tensor_tensor(local[:, :], tn[:, :], first[:, :], ALU.subtract))
                then(dve.tensor_scalar(local[:, :], local[:, :], float(SLOTS), None, ALU.mult))
                then(dve.tensor_scalar(base[:, :], te[:, :], float(REGION), None, ALU.mult))
                then(dve.tensor_tensor(base[:, :], base[:, :], local[:, :], ALU.add))
                then(dve.tensor_tensor(table[:, 0, :], te[:, :], real[:, :], ALU.mult))
                then(dve.tensor_tensor(base[:, :], base[:, :], surplus_row[:, :], ALU.subtract))
                then(dve.tensor_tensor(base[:, :], base[:, :], real[:, :], ALU.mult))
                then(dve.tensor_tensor(table[:, 1, :], base[:, :], surplus_row[:, :], ALU.add))
                dve.wait_ge(ex_done, 1)
                then(dve.tensor_scalar(den[:, :], ex[:, :], 1.0, None, ALU.add))
                then(dve.reciprocal(den[:, :], den[:, :]))
                then(dve.tensor_copy(shares[:, :, 0], den[:, :]))
                then(dve.tensor_tensor(shares[:, :, 1], den[:, :], ex[:, :], ALU.mult))


def experts(nc, d, queue_d, y_d, table):
    with ExitStack() as ctx:
        m = Memory(nc, ctx, "moe")
        ident = m.sb("ident", [P, P])
        gain = m.sb("gain", [P, 4])
        xr = [m.sb(f"xr{k}", [P, 4, QUEUED + CB]) for k in range(2)]
        place = [m.sb(f"place{k}", [P, 4], I32) for k in range(2)]
        place_done, pool_turn = m.sem("place_done"), m.sem("pool_turn")
        raw = [m.sb(f"raw{k}", [P, 2, HIDDEN]) for k in range(2)]
        hi = [m.sb(f"hi{k}", [P, 2, HIDDEN], F32R) for k in range(2)]
        lo = [m.sb(f"lo{k}", [P, HIDDEN], F32R) for k in range(2)]
        w2 = [m.sb(f"w2_{k}", [P, 6, C]) for k in range(2)]
        b1 = [m.sb(f"b1_{k}", [P, 6]) for k in range(2)]
        b2 = [m.sb(f"b2_{k}", [P, C]) for k in range(2)]
        xf = m.sb("xf", [P, 2, SLOTS])
        xh = [m.sb(f"xh{k}", [P, 2, SLOTS], F32R) for k in range(2)]
        xl = [m.sb(f"xl{k}", [P, 2, SLOTS], F32R) for k in range(2)]
        ht = [m.sb(f"ht{k}", [P, 6, SLOTS]) for k in range(2)]
        y = [m.sb(f"y{k}", [P, 4, C]) for k in range(2)]
        ta = m.psum("ta", [P, 512])
        tc = m.psum("tc", [P, 512])
        up = [m.psum(f"up{k}", [P, 512]) for k in range(2)]
        down = [m.psum(f"down{k}", [P, 512]) for k in range(2)]
        const_in = m.sem("const_in")
        w1_in, w2_in, x_in = ([m.sem(f"{n}{k}") for k in range(2)] for n in ("w1_in", "w2_in", "x_in"))
        (t_done, xf_done, hi_done, lo_done, xh_done, xl_done, up_done, gelu_done, down_done, y_done) = (
            m.sem(x) for x in ("t_done", "xf_done", "hi_done", "lo_done", "xh_done", "xl_done", "up_done",
                               "gelu_done", "down_done", "y_done"))
        stored = [m.sem(f"stored{k}") for k in range(2)]

        def run(fori, tile):
            for k in range(2):
                tile(0, k, True)
            with fori(1, MOE_TILES // 2) as i:
                for k in range(2):
                    tile(i, k, True)
            tile(MOE_TILES // 2, 0, False)

        with nc.Block() as block:
            @block.sync
            def _(sp):
                sp.dma_start(ident[:, :], d["ident"]).then_inc(const_in, 16)
                for j, name in enumerate(("ln2_g", "ln2_b")):
                    sp.dma_start(gain[:, j:j + 1], d[name][0:P].rearrange("(p a) -> p a", a=1)).then_inc(const_in, 16)
                    for half in range(2):
                        sp.dma_start(gain[CB * half:CB * half + CB, 2 + j:3 + j],
                                     d[name][P:C].rearrange("(p a) -> p a", a=1)).then_inc(const_in, 16)

                def load(i, k, used):
                    t = 2 * i + k
                    e = sp.value_load(table[0:1, 0, bass.ds(t, 1)], min_val=0, max_val=EXPERTS - 1)
                    row = sp.value_load(table[0:1, 1, bass.ds(t, 1)], min_val=0, max_val=SURPLUS + SLOTS)
                    after(sp, t_done, t - 1 if used else 0)
                    after(sp, place_done, t - 1 if used else 0)
                    rows = queue_d[bass.ds(row, SLOTS), :].rearrange("(t p) c -> p t c", p=P)
                    sp.dma_start(xr[k][:, :, 0:QUEUED], rows).then_inc(x_in[k], 16)
                    sp.dma_start(xr[k][:, :, QUEUED:], rows[:, :, 1 + P:QUEUED]).then_inc(x_in[k], 16)
                    after(sp, lo_done, 2 * t - 2 if used else 0)
                    w = d["w1T"][bass.ds(e, 1)].rearrange("a c f -> (a c) f")
                    sp.dma_start(raw[k][:, 0, :], w[0:P, :]).then_inc(w1_in[k], 16)
                    for half in range(2):
                        sp.dma_start(raw[k][CB * half:CB * half + CB, 1, :], w[P:C, :]).then_inc(w1_in[k], 16)
                    after(sp, y_done, 4 * t - 4 if used else 0)
                    sp.dma_start(w2[k][:, :, :], d["w2T"][bass.ds(e, 1)].rearrange("a p s c -> (a p) s c")).then_inc(w2_in[k], 16)
                    sp.dma_start(b1[k][:, :], d["b1T"][bass.ds(e, 1)].rearrange("a p s -> (a p) s")).then_inc(w2_in[k], 16)
                    sp.dma_start(b2[k][:, :], d["b2"][bass.ds(e, 1), :].rearrange("a c -> (a c)").partition_broadcast(P)).then_inc(w2_in[k], 16)

                load(0, 0, False)
                load(0, 1, False)
                with sp.Fori(1, MOE_TILES // 2) as i:
                    for k in range(2):
                        load(i, k, True)
                load(MOE_TILES // 2, 0, True)

            @block.gpsimd
            def _(pool):
                def tile(i, k, more):
                    t = 2 * i + k
                    after(pool, stored[k], 64 * i)
                    hold(pool, x_in[k], 32 * (i + 1), pool_turn)
                    pool.tensor_copy(place[k][:, :], xr[k][:, :, 0]).then_inc(place_done, 1)
                    pool.wait_ge(place_done, t + 1)
                    for j in range(4):
                        hold(pool, y_done, 4 * t + j + 1, pool_turn)
                        pool.indirect_dma_start(y_d, bass.IndirectOffsetOnAxis(place[k][:, j:j + 1], 0),
                                                y[k][:, j, :], None).then_inc(stored[k], 16)

                run(pool.Fori, tile)
                pool.wait_ge(stored[0], 64 * (MOE_TILES // 2 + 1))
                pool.wait_ge(stored[1], 64 * (MOE_TILES // 2))

            @block.scalar
            def _(act):
                act.wait_ge(const_in, 16 * 7)

                def weights_hi(i, k):
                    t = 2 * i + k
                    act.wait_ge(w1_in[k], 48 * (i + 1))
                    after(act, up_done, 6 * t - 6 if not isinstance(t, int) or t > 1 else 0)
                    act.activation(hi[k][:, :, :], raw[k][:, :, :], ACT.Copy).then_inc(hi_done, 1)

                def affine(t):
                    act.wait_ge(t_done, t + 1)
                    after(act, xl_done, 2 * t)
                    act.activation(xf[:, 0, :], ta[:, :], ACT.Identity, scale=gain[:, 0:1], bias=gain[:, 1:2]).then_inc(xf_done, 1)
                    act.activation(xf[:, 1, :], tc[:, :], ACT.Identity, scale=gain[:, 2:3], bias=gain[:, 3:4]).then_inc(xf_done, 1)

                weights_hi(0, 0)
                affine(0)

                def tile(i, k, more):
                    t = 2 * i + k
                    act.wait_ge(w2_in[k], 48 * (i + 1))
                    after(act, down_done, 4 * t - 4 if not isinstance(t, int) or t > 1 else 0)
                    for j in range(6):
                        act.wait_ge(up_done, 6 * t + j + 1)
                        act.activation(ht[k][:, j, :], up[j % 2][:, :], ACT.Gelu, bias=b1[k][:, j:j + 1]).then_inc(gelu_done, 1)
                        if j == 2 and more:
                            weights_hi(*((i, 1) if k == 0 else (i + 1, 0)))
                    if more:
                        affine(t + 1)

                run(act.Fori, tile)

            @block.vector
            def _(dve):
                def split(i, k):
                    t = 2 * i + k
                    dve.wait_ge(hi_done, t + 1)
                    dve.tensor_tensor(lo[k][:, :], raw[k][:, 0, :], hi[k][:, 0, :].bitcast(F32), ALU.subtract).then_inc(lo_done, 1)
                    low = slice(CB, P)
                    dve.tensor_tensor(hi[k][low, 1, :], raw[k][low, 1, :], hi[k][low, 1, :].bitcast(F32), ALU.subtract).then_inc(lo_done, 1)

                def split_x(i, k):
                    t = 2 * i + k
                    dve.wait_ge(xf_done, 2 * t + 2)
                    after(dve, up_done, 6 * t - 6 if not isinstance(t, int) or t > 1 else 0)
                    dve.tensor_copy(xh[k][:, :, :], xf[:, :, :]).then_inc(xh_done, 1)
                    dve.wait_ge(xh_done, t + 1)
                    dve.tensor_tensor(xl[k][:, 0, :], xf[:, 0, :], xh[k][:, 0, :].bitcast(F32), ALU.subtract).then_inc(xl_done, 1)
                    dve.tensor_tensor(xl[k][0:CB, 1, :], xf[0:CB, 1, :], xh[k][0:CB, 1, :].bitcast(F32), ALU.subtract).then_inc(xl_done, 1)

                split(0, 0)
                split_x(0, 0)

                def tile(i, k, more):
                    t = 2 * i + k
                    nxt = (i, 1) if k == 0 else (i + 1, 0)
                    if more:
                        split(*nxt)
                        split_x(*nxt)
                    after(dve, stored[k], 64 * i)
                    dve.wait_ge(w2_in[k], 48 * (i + 1))
                    for j in range(4):
                        dve.wait_ge(down_done, 4 * t + j + 1)
                        dve.tensor_tensor(y[k][:, j, :], down[j % 2][:, 0:C], b2[k][:, :], ALU.add).then_inc(y_done, 1)

                run(dve.Fori, tile)

            @block.tensor
            def _(pe):
                pe.wait_ge(const_in, 16 * 7)

                def transposes(i, k):
                    t = 2 * i + k
                    pe.wait_ge(x_in[k], 32 * (i + 1))
                    after(pe, xf_done, 2 * t)
                    for j in range(4):
                        pe.transpose(ta[:, P * j:P * j + P], xr[k][:, j, 1:1 + P], ident[:, :])
                        mm = pe.transpose(tc[:, P * j:P * j + P], xr[k][:, j, 1 + P:], ident[:, :])
                    mm.then_inc(t_done, 1)

                transposes(0, 0)

                def tile(i, k, more):
                    t = 2 * i + k
                    pe.wait_ge(lo_done, 2 * t + 2)
                    pe.wait_ge(xl_done, 2 * t + 2)
                    for j in range(6):
                        after(pe, gelu_done, 6 * t + j - 1)
                        o, f = up[j % 2][:, :], slice(P * j, P * j + P)
                        pe.matmul(o, hi[k][:, 0, f], xh[k][:, 0, :], start=True, stop=False)
                        pe.matmul(o, hi[k][:, 0, f], xl[k][:, 0, :], start=False, stop=False)
                        pe.matmul(o, lo[k][:, f], xh[k][:, 0, :], start=False, stop=False)
                        pe.matmul(o, hi[k][:, 1, f], xh[k][:, 1, :], start=False, stop=False)
                        pe.matmul(o, hi[k][0:CB, 1, f], xl[k][0:CB, 1, :], start=False, stop=True).then_inc(up_done, 1)
                    if more:
                        transposes(*((i, 1) if k == 0 else (i + 1, 0)))
                    pe.wait_ge(w2_in[k], 48 * (i + 1))
                    pe.wait_ge(gelu_done, 6 * t + 6)
                    for j in range(4):
                        after(pe, y_done, 4 * t + j - 1)
                        for s in range(6):
                            mm = pe.matmul(down[j % 2][:, 0:C], ht[k][:, s, P * j:P * j + P], w2[k][:, s, :],
                                           start=(s == 0), stop=(s == 5))
                        mm.then_inc(down_done, 1)

                run(pe.Fori, tile)


def combine(nc, h, out_d, y_d, shares):
    with ExitStack() as ctx:
        m = Memory(nc, ctx, "comb")
        first = m.sb("first", [P, TILES, C])
        second = m.sb("second", [P, TILES, C])
        got_in = [m.sem(f"got_in{g}") for g in range(GROUPS)]
        half_done, row_done, stored = m.sem("half_done"), m.sem("row_done"), m.sem("stored")
        FULL = TOKENS // P
        PART = TOKENS - P * FULL

        def spans(g):
            end = min(4 * g + 4, FULL)
            yield (lambda x, at=0: x[at + 512 * g:at + P * end, :].rearrange("(t p) c -> p t c", p=P),
                   lambda b: b[:, 4 * g:end, :])
            if end == FULL:
                yield lambda x, at=0: x[at + P * FULL:at + TOKENS, :], lambda b: b[0:PART, FULL, :]

        with nc.Block() as block:
            @block.sync
            def _(sp):
                for g in range(GROUPS):
                    for rows, tiles in spans(g):
                        sp.dma_start(tiles(first), rows(y_d)).then_inc(got_in[g], 16)
                        sp.dma_start(tiles(second), rows(y_d, ROWS)).then_inc(got_in[g], 16)
                for g in range(GROUPS):
                    sp.wait_ge(row_done, min(4 * g + 4, FULL + 1))
                    for rows, tiles in spans(g):
                        sp.dma_start(rows(out_d), tiles(second)).then_inc(stored, 16)
                sp.wait_ge(stored, 16 * (GROUPS + 1))

            @block.vector
            def _(dve):
                for g in range(GROUPS):
                    dve.wait_ge(got_in[g], 32 if g + 1 < GROUPS else 64)
                    tiles = range(4 * g, min(4 * g + 4, FULL + 1))
                    for t in tiles:
                        n = P if t < FULL else PART
                        dve.scalar_tensor_tensor(out=h[0:n, t, :], in0=first[0:n, t, :], scalar=shares[0:n, t, 0:1],
                                                 in1=h[0:n, t, :], op0=ALU.mult, op1=ALU.add).then_inc(half_done, 1)
                    for t in tiles:
                        n = P if t < FULL else PART
                        dve.wait_ge(half_done, t + 1)
                        dve.scalar_tensor_tensor(out=second[0:n, t, :], in0=second[0:n, t, :], scalar=shares[0:n, t, 1:2],
                                                 in1=h[0:n, t, :], op0=ALU.mult, op1=ALU.add).then_inc(row_done, 1)


def vit_moe_layer(nc, d, out):
    rows_d = nc.dram_tensor("rows_scratch", [ROWS, C], F32, kind="Internal").ap()
    kept_d = nc.dram_tensor("kept_scratch", [ROWS, C], F32, kind="Internal").ap()
    queue_d = nc.dram_tensor("queue_scratch", [SURPLUS + 2 * SLOTS, QUEUED], F32, kind="Internal").ap()
    y_d = nc.dram_tensor("y_scratch", [Y_ROWS, C], F32, kind="Internal").ap()
    parts_d = nc.dram_tensor("parts_scratch", [2, 3, 2, C, CHUNK], BF16, kind="Internal").ap()
    out_rows = out.rearrange("b s c -> (b s) c")
    embed(nc, d, rows_d)
    with ExitStack() as ctx:
        m = Memory(nc, ctx, "all")
        h = m.sb("h", [P, TILES, C])
        keep = (m.sb("top2", [P, TILES, 2]), m.sb("counts", [P, EXPERTS]))
        with ExitStack() as wide:
            w = Memory(nc, wide, "all")
            ot_all = w.sb("ot_all", [P, 3, ROWS])
            with ExitStack() as feats:
                f = Memory(nc, feats, "all")
                xa_all = f.sb("xa_all", [P, ROWS])
                xb_all = f.sb("xb_all", [CB, ROWS])
                first_norm(nc, d, rows_d, h, xa_all, xb_all)
                attention(nc, d, parts_d, xa_all, xb_all, ot_all, "qkv1_w", "qkv1_b", True)
                between(nc, d, h, ot_all, xa_all, xb_all, kept_d)
                attention(nc, d, parts_d, xa_all, xb_all, ot_all, "qkv2_w", None, False)
            dispatch(nc, d, h, ot_all, kept_d, queue_d, keep)
        shares = m.sb("shares", [P, TILES, 2])
        table = m.sb("table", [P, 2, MOE_TILES], I32)
        plan(nc, d, queue_d, keep, shares, table)
        experts(nc, d, queue_d, y_d, table)
        combine(nc, h, out_rows, y_d, shares)


def kernel(**inputs):
    import numpy as _np
    import concourse.bacc as _bacc
    from concourse import mybir as _mybir
    from concourse.bass_utils import run_bass_kernel_spmd as _run

    arrays = lay_out(inputs)
    nc = _bacc.Bacc("TRN2", target_bir_lowering=False, num_devices=1)
    d = {name: nc.dram_tensor(name + "_dram", a.shape, _mybir.dt.from_np(a.dtype), kind="ExternalInput").ap()
         for name, a in arrays.items()}
    out = nc.dram_tensor("out_dram", (BATCH, SEQ, C), F32, kind="ExternalOutput").ap()
    vit_moe_layer(nc, d, out)
    r = _run(nc, [{name + "_dram": a for name, a in arrays.items()}], core_ids=[0])
    return r.results[0]["out_dram"]


def lay_out(inputs):
    import numpy as np

    a = {k: np.asarray(v) for k, v in inputs.items()}
    side = 96 // 16
    x = a["x"].reshape(BATCH, 3, side, 16, side, 16).transpose(0, 1, 2, 4, 3, 5).reshape(BATCH, IMG, PATCH)
    x = x.transpose(1, 0, 2).reshape(IMG // 2, P, 6, P)
    out = {"patches": x.transpose(0, 3, 2, 1).reshape(IMG // 2, P, 6 * P)}
    out["ids"] = a["x_txt"].T.reshape(16, P).T
    out["tune_ids"] = a["L0_txt_tune_ids"]
    out["base_w"], out["train_w"] = a["L0_txt_base_weight"], a["L0_txt_train_weight"]
    out["tok_wT"], out["tok_b"] = a["L0_tok_W"].T, a["L0_tok_b"]
    out["cls"], out["pos"] = a["L0_tok_class_token"], a["L0_tok_pos_embedding"]
    order = np.concatenate([w * C + CB * n + np.r_[0:CB] for n in range(3) for w in range(2)] + [2 * C + np.r_[0:C]])
    out["qkv1_w"], out["qkv1_b"] = a["L0_attn_w_qkv"].T[:, order], a["L0_attn_b_qkv"][order]
    out["qkv2_w"] = a["L0_ffn_qkv_w"].T[:, order]
    for name, w, b in (("proj1_w", a["L0_attn_w_proj"], a["L0_attn_b_proj"]), ("proj2_w", a["L0_ffn_proj_w"], a["L0_ffn_proj_b"])):
        wide = np.zeros((3, 4, 2, HD, C), w.dtype)
        wide[:, :, 0] = w.T.reshape(3, 4, HD, C)
        wide[0, 0, 1, 0] = b
        out[name] = wide.reshape(3, P, C).transpose(1, 0, 2)
    for name in ("ln1_g", "ln1_b", "ln2_g", "ln2_b", "gate_b", "b2"):
        out[name] = a["L0_ffn_" + name]
    out["gate_wT"] = a["L0_ffn_gate_w"].T
    out["w1T"] = a["L0_ffn_w1"].transpose(0, 2, 1)
    out["b1T"] = a["L0_ffn_b1"].reshape(EXPERTS, 6, P).transpose(0, 2, 1)
    out["w2T"] = a["L0_ffn_w2"].transpose(0, 2, 1).reshape(EXPERTS, 6, P, C).transpose(0, 2, 1, 3)
    f = np.float32
    inv = (f(1.0) / np.power(f(10000.0), np.arange(0, HD, 2, dtype=f) / f(HD))).astype(f)
    angle = (np.arange(SEQ, dtype=f)[:, None] * inv[None, :]).astype(f)
    cos, sin = np.cos(angle).T, np.sin(angle).T
    out["cos"] = np.tile(np.concatenate([cos, cos]), (P // HD, CHUNK_B)).astype(f)
    out["sin"] = np.tile(np.concatenate([-sin, sin]), (P // HD, CHUNK_B)).astype(f)
    out["ident"] = np.eye(P, dtype=f)
    pick = np.zeros((PARTS, HEADS), f)
    for j in range(3):
        pick[HEADS * j:HEADS * j + HEADS] = np.eye(HEADS)
    out["pick"] = pick
    out["tri"] = np.triu(np.ones((P, P), f), 1)
    out["number"] = np.tile(np.arange(1, TUNE + 1, dtype=f), (P, 1))
    out["eight"] = np.tile(np.arange(EXPERTS, dtype=f), (P, 1))
    out["region"] = np.tile(np.arange(EXPERTS, dtype=f) * REGION, (P, 1))
    token = np.arange(TILES)[None, :] * P + np.arange(P)[:, None]
    out["valid"] = (token < TOKENS).astype(f)
    dump = np.zeros((P, TILES, 2), f)
    for j in range(2):
        dump[:, :, j] = np.where(token < TOKENS, 0, DUMP + 2 * (token - TOKENS) + j)
    out["dump"] = dump
    out["result_row"] = np.stack([token, token + ROWS], 2).astype(f)
    fillers = np.arange(2 * ROWS, Y_ROWS).reshape(EXPERTS + 2, 4, P)
    out["filler_row"] = fillers.transpose(2, 0, 1).astype(f)
    out["surplus_row"] = np.tile(SURPLUS + SLOTS * (np.arange(MOE_TILES) % 2), (P, 1)).astype(f)
    return {k: np.ascontiguousarray(v) for k, v in out.items()}
```

```python
from contextlib import ExitStack

import concourse.bass as bass
from concourse import mybir

F32 = mybir.dt.float32
F32R = mybir.dt.float32r
BF16 = mybir.dt.bfloat16
I32 = mybir.dt.int32
U32 = mybir.dt.uint32
ALU = mybir.AluOpType
ACT = mybir.ActivationFunctionType
AX_X = mybir.AxisListType.X

P = 128
BATCH, IMG, TXT = 64, 36, 32
SEQ = 1 + IMG + TXT
TOKENS = BATCH * SEQ
TILES = 36
GROUPS = TILES // 4
ROWS = TILES * P
PAD = ROWS - TOKENS
C = 192
CB = C - P
HEADS, HD = 12, 16
PATCH = 768
TUNE = 256
EPS = 1e-5
CHUNK_B = 4
CHUNK = CHUNK_B * SEQ
CHUNKS = BATCH // CHUNK_B
PARTS = 96
EXPERTS, HIDDEN, TOPK = 8, 768, 2
SLOTS = 512
REGION = TOKENS + SLOTS
MOE_TILES = (TOPK * TOKENS + EXPERTS * (SLOTS - 1)) // SLOTS
DUMP = EXPERTS * REGION
SURPLUS = DUMP + 4 * P
Y_ROWS = 2 * ROWS + (EXPERTS + 2) * SLOTS
QUEUED = 1 + C


def after(eng, sem, count):
    if not isinstance(count, int) or count > 0:
        eng.wait_ge(sem, count)


def hold(eng, sem, count, turn):
    eng.wait_ge(sem, count)
    eng.sem_inc(turn, 1)


class Memory:

    def __init__(self, nc, ctx, phase):
        self.nc, self.ctx, self.phase = nc, ctx, phase + "_"
        self.sems = []
        ctx.callback(self.clear)

    def clear(self):
        if self.sems:
            self.nc.clear_and_free_semaphores(self.sems)
            self.nc.all_engine_barrier()

    def sb(self, name, shape, dt=F32):
        return self.ctx.enter_context(self.nc.sbuf_tensor(self.phase + name, shape, dt))

    def psum(self, name, shape, dt=F32):
        return self.ctx.enter_context(self.nc.psum_tensor(self.phase + name, shape, dt))

    def sem(self, name):
        self.sems.append(self.nc.alloc_semaphore(self.phase + name))
        return self.sems[-1]


RING = 6
ROUNDS = IMG // 2 // RING


def embed(nc, d, rows_d):
    with ExitStack() as ctx:
        m = Memory(nc, ctx, "emb")
        w = m.sb("tok_w", [P, 6, C])
        patch = [m.sb(f"patch{k}", [P, 6, P]) for k in range(RING)]
        place = m.sb("place", [P, IMG // 2, C])
        bias = m.sb("tok_bias", [P, C])
        emb = [m.sb(f"emb{k}", [P, C]) for k in range(RING)]
        cls = m.sb("cls", [BATCH, 2, C])
        zero = m.sb("zero", [P, C])
        ids = m.sb("ids", [P, 16], I32)
        idf = m.sb("idf", [P, 16])
        tune = m.sb("tune", [P, TUNE], I32)
        tunef = m.sb("tunef", [P, TUNE])
        number = m.sb("number", [P, TUNE])
        hit = m.sb("hit", [P, 16, TUNE])
        last = m.sb("last", [P, 16])
        mask = m.sb("mask", [P, 16])
        keep = m.sb("keep", [P, 16])
        rowf = m.sb("rowf", [P, 16])
        row = m.sb("row", [P, 16], I32)
        base = m.sb("base", [P, 16, C])
        train = m.sb("train", [P, 16, C])
        acc = [m.psum(f"emb_acc{k}", [P, 512]) for k in range(RING)]
        w_in, place_in, cls_in, ids_in = (m.sem(x) for x in ("w_in", "place_in", "cls_in", "ids_in"))
        patch_in = [m.sem(f"patch_in{k}") for k in range(RING)]
        place_done, cls_done, zero_done = m.sem("place_done"), m.sem("cls_done"), m.sem("zero_done")
        acc_done, emb_done = m.sem("acc_done"), m.sem("emb_done")
        stored = [m.sem(f"stored{k}") for k in range(RING)]
        text, kept_text = m.sem("text_step"), m.sem("kept_text")
        row_done, base_in, train_in, text_done, rest = (
            m.sem(x) for x in ("row_done", "base_in", "train_in", "text_done", "rest_stored"))
        token = rows_d[0:TOKENS, :].rearrange("(b s) c -> b s c", s=SEQ)

        with nc.Block() as block:
            @block.sync
            def _(sp):
                sp.dma_start(w[:, :, :], d["tok_wT"].rearrange("(k p) c -> p k c", p=P)).then_inc(w_in, 16)

                def load(t, k):
                    sp.dma_start(patch[k][:, :, :].rearrange("p k n -> p (k n)"),
                                 d["patches"][bass.ds(t, 1)].rearrange("a p n -> (a p) n")).then_inc(patch_in[k], 16)

                for k in range(2):
                    load(k, k)
                for half in range(2):
                    sp.dma_start(place[64 * half:64 * half + 64, :, :],
                                 d["pos"][1 + half:1 + half + 35:2, :].partition_broadcast(64)).then_inc(place_in, 16)
                sp.dma_start(bias[:, :], d["tok_b"].partition_broadcast(P)).then_inc(place_in, 16)
                for k in range(2, RING):
                    load(k, k)

                def store(t, k, n):
                    sp.wait_ge(emb_done, n)
                    for half in range(2):
                        sp.dma_start(token[:, bass.ds(2 * t + 1 + half, 1), :].rearrange("b a c -> b (a c)"),
                                     emb[k][64 * half:64 * half + 64, :]).then_inc(stored[k], 16)

                with sp.Fori(0, ROUNDS - 1) as i:
                    for k in range(RING):
                        sp.wait_ge(acc_done, RING * i + 1 + k)
                        load(RING * i + RING + k, k)
                        store(RING * i + k, k, RING * i + 1 + k)
                for t in range(RING * (ROUNDS - 1), RING * ROUNDS):
                    store(t, t % RING, t + 1)
                for k in range(RING):
                    sp.wait_ge(stored[k], 32 * ROUNDS)

            @block.scalar
            def _(act):
                act.dma_start(ids[:, :], d["ids"]).then_inc(ids_in, 16)
                act.dma_start(tune[:, :], d["tune_ids"].partition_broadcast(P)).then_inc(ids_in, 16)
                act.dma_start(number[:, :], d["number"]).then_inc(ids_in, 16)
                act.dma_start(cls[:, 0, :], d["cls"][0:1, :].rearrange("a c -> (a c)").partition_broadcast(BATCH)).then_inc(cls_in, 16)
                act.dma_start(cls[:, 1, :], d["pos"][0:1, :].rearrange("a c -> (a c)").partition_broadcast(BATCH)).then_inc(cls_in, 16)
                act.wait_ge(zero_done, 1)
                act.dma_start(rows_d[TOKENS:TOKENS + P, :], zero[:, :]).then_inc(rest, 16)
                act.dma_start(rows_d[TOKENS + P:ROWS, :], zero[0:PAD - P, :]).then_inc(rest, 16)
                act.wait_ge(cls_done, 1)
                act.dma_start(token[:, 0, :], cls[:, 0, :]).then_inc(rest, 16)
                act.wait_ge(text_done, 1)
                for half in range(2):
                    act.dma_start(token[:, 1 + IMG + half::2, :], base[64 * half:64 * half + 64, :, :]).then_inc(rest, 16)
                act.wait_ge(rest, 16 * 5)

            @block.gpsimd
            def _(pool):
                pool.wait_ge(ids_in, 48)
                for j in range(16):
                    pool.indirect_dma_start(base[:, j, :], None, d["base_w"],
                                            bass.IndirectOffsetOnAxis(ids[:, j:j + 1], 0)).then_inc(base_in, 16)
                pool.wait_ge(row_done, 1)
                for j in range(16):
                    pool.indirect_dma_start(train[:, j, :], None, d["train_w"],
                                            bass.IndirectOffsetOnAxis(row[:, j:j + 1], 0)).then_inc(train_in, 16)
                pool.wait_ge(base_in, 256)
                pool.wait_ge(text, 22)
                pool.tensor_tensor(base[:, :, :], base[:, :, :], keep[:, :].unsqueeze(2).to_broadcast([P, 16, C]),
                                   ALU.mult).then_inc(kept_text, 1)

            @block.tensor
            def _(pe):
                pe.wait_ge(w_in, 16)

                def tile(k, loads, n):
                    pe.wait_ge(patch_in[k], 16 * loads)
                    after(pe, emb_done, n)
                    for s in range(6):
                        mm = pe.matmul(acc[k][:, 0:C], patch[k][:, s, :], w[:, s, :], start=(s == 0), stop=(s == 5))
                    mm.then_inc(acc_done, 1)

                for k in range(RING):
                    tile(k, 1, 0)
                with pe.Fori(1, ROUNDS) as i:
                    for k in range(RING):
                        tile(k, i + 1, RING * (i - 1) + k + 1)

            @block.vector
            def _(dve):
                dve.memset(zero[:, :], 0.0).then_inc(zero_done, 1)
                dve.wait_ge(ids_in, 48)
                dve.tensor_copy(idf[:, :], ids[:, :]).then_inc(text, 1)
                dve.tensor_copy(tunef[:, :], tune[:, :]).then_inc(text, 1)
                dve.wait_ge(text, 2)
                for j in range(16):
                    dve.scalar_tensor_tensor(out=hit[:, j, :], in0=tunef[:, :], scalar=idf[:, j:j + 1], in1=number[:, :],
                                             op0=ALU.is_equal, op1=ALU.mult).then_inc(text, 1)
                dve.wait_ge(text, 18)
                dve.tensor_reduce(last[:, :], hit[:, :, :], AX_X, ALU.max).then_inc(text, 1)
                dve.wait_ge(text, 19)
                dve.tensor_scalar(mask[:, :], last[:, :], 0.5, None, ALU.is_gt).then_inc(text, 1)
                dve.tensor_scalar(keep[:, :], last[:, :], 0.5, None, ALU.is_lt).then_inc(text, 1)
                dve.tensor_scalar(rowf[:, :], last[:, :], -1.0, 0.0, ALU.add, ALU.max).then_inc(text, 1)
                dve.wait_ge(text, 22)
                dve.tensor_copy(row[:, :], rowf[:, :]).then_inc(row_done, 1)
                dve.wait_ge(place_in, 48)
                dve.tensor_tensor(place[:, :, :], place[:, :, :],
                                  bias[:, :].unsqueeze(1).to_broadcast([P, IMG // 2, C]), ALU.add).then_inc(place_done, 1)
                dve.wait_ge(cls_in, 32)
                dve.tensor_tensor(cls[:, 0, :], cls[:, 0, :], cls[:, 1, :], ALU.add).then_inc(cls_done, 1)
                dve.wait_ge(place_done, 1)

                def tile(t, k, n, stores):
                    dve.wait_ge(acc_done, n)
                    after(dve, stored[k], stores)
                    dve.tensor_tensor(emb[k][:, :], acc[k][:, 0:C],
                                      place[:, bass.ds(t, 1), :].rearrange("p a c -> p (a c)"),
                                      ALU.add).then_inc(emb_done, 1)

                for k in range(RING):
                    tile(k, k, 1 + k, 0)
                with dve.Fori(1, ROUNDS) as i:
                    for k in range(RING):
                        tile(RING * i + k, k, RING * i + 1 + k, 32 * i)
                wide = [P, 16, C]
                dve.wait_ge(train_in, 256)
                dve.tensor_tensor(train[:, :, :], train[:, :, :], mask[:, :].unsqueeze(2).to_broadcast(wide), ALU.mult).then_inc(text, 1)
                dve.wait_ge(text, 23)
                dve.wait_ge(kept_text, 1)
                dve.tensor_tensor(base[:, :, :], base[:, :, :], train[:, :, :], ALU.add).then_inc(text_done, 1)


class NormGroup:

    def __init__(self, m, name):
        self.stats = m.sb(name + "_stats", [P, 4, 6])
        self.mv = m.sb(name + "_mv", [P, 4, 2])
        self.inv = m.sb(name + "_inv", [P, 4])
        self.rstd = m.sb(name + "_rstd", [P, 4])
        self.stat_done, self.mv_done, self.eps_done, self.inv_done, self.rstd_done, self.turn = (
            m.sem(f"{name}_{x}") for x in ("stat", "mv", "eps", "inv", "rstd", "turn"))


def norm_stats(dve, n, rows, g, ready=None):
    if ready:
        hold(dve, ready, 4 * g, n.turn)
    for k in range(4):
        dve.bn_stats(n.stats[:, k, :], rows[k]).then_inc(n.stat_done, 1)


def norm_inverse(dve, n, g):
    hold(dve, n.stat_done, 4 * g, n.turn)
    for k in range(4):
        dve.bn_aggr(n.mv[:, k, :], n.stats[:, k, :]).then_inc(n.mv_done, 1)
    dve.wait_ge(n.mv_done, 4 * g)
    dve.tensor_scalar(n.inv[:, :], n.mv[:, :, 1], EPS, None, ALU.add).then_inc(n.eps_done, 1)
    dve.wait_ge(n.eps_done, g)
    dve.reciprocal(n.inv[:, :], n.inv[:, :]).then_inc(n.inv_done, 1)


def norm_root(act, n, g):
    act.wait_ge(n.inv_done, g)
    act.activation(n.rstd[:, :], n.inv[:, :], ACT.Sqrt).then_inc(n.rstd_done, 1)


def norm_apply(dve, n, outs, rows, g, done):
    dve.wait_ge(n.rstd_done, g)
    for k in range(4):
        dve.tensor_scalar(outs[k], rows[k], n.mv[:, k, 0:1], n.rstd[:, k:k + 1],
                          ALU.subtract, ALU.mult).then_inc(done, 1)


def cols(x, start, n):
    return x[:, bass.ds(start, n)]


def tile_of(x, t):
    return x[:, bass.ds(t, 1), :].rearrange("p a c -> p (a c)")


def first_norm(nc, d, rows_d, h, x_all):
    with ExitStack() as ctx:
        m = Memory(nc, ctx, "norm")
        ident = m.sb("ident", [P, P])
        xn = [m.sb(f"xn{k}", [P, C]) for k in range(4)]
        n = NormGroup(m, "n0")
        ta = m.psum("ta", [P, 512])
        tb = m.psum("tb", [P, 512])
        rows_in = [m.sem(f"rows_in{g}") for g in range(GROUPS)]
        ident_in, xn_done, t_done, ta_out, tb_out = (
            m.sem(x) for x in ("ident_in", "xn_done", "t_done", "ta_out", "tb_out"))
        all_in = m.sem("all_in")
        with nc.Block() as block:
            @block.sync
            def _(sp):
                sp.dma_start(ident[:, :], d["ident"]).then_inc(ident_in, 16)
                for g in range(GROUPS):
                    sp.dma_start(h[:, 4 * g:4 * g + 4, :],
                                 rows_d[512 * g:512 * g + 512, :].rearrange("(t p) c -> p t c", p=P)).then_inc(rows_in[g], 16)
                for g in range(GROUPS):
                    sp.wait_ge(rows_in[g], 16)
                    sp.sem_inc(all_in, 1)

            @block.vector
            def _(dve):
                def rows_of(g):
                    return [tile_of(h, 4 * g + k) for k in range(4)]

                def stats(g):
                    hold(dve, all_in, g + 1, n.turn)
                    norm_stats(dve, n, rows_of(g), g + 1)

                def apply(g):
                    after(dve, t_done, g)
                    norm_apply(dve, n, [x[:, :] for x in xn], rows_of(g), g + 1, xn_done)

                def group(g):
                    stats(g)
                    apply(g - 1)
                    hold(dve, xn_done, 4 * g, n.turn)
                    norm_inverse(dve, n, g + 1)

                stats(0)
                norm_inverse(dve, n, 1)
                group(1)
                with dve.Fori(2, GROUPS) as g:
                    group(g)
                apply(GROUPS - 1)

            @block.scalar
            def _(act):
                def group(g):
                    norm_root(act, n, g + 1)
                    act.wait_ge(t_done, g + 1)
                    act.activation(x_all[:, 0, bass.ds(512 * g, 512)], ta[:, :], ACT.Copy).then_inc(ta_out, 1)
                    act.activation(x_all[0:CB, 1, bass.ds(512 * g, 512)], tb[0:CB, :], ACT.Copy).then_inc(tb_out, 1)

                group(0)
                with act.Fori(1, GROUPS) as g:
                    group(g)

            @block.tensor
            def _(pe):
                pe.wait_ge(ident_in, 16)

                def group(g):
                    after(pe, ta_out, g)
                    after(pe, tb_out, g)
                    for k in range(4):
                        pe.wait_ge(xn_done, 4 * g + k + 1)
                        pe.transpose(ta[:, P * k:P * k + P], xn[k][:, 0:P], ident[:, :])
                        mm = pe.transpose(tb[0:CB, P * k:P * k + P], xn[k][:, P:C], ident[:, :])
                    mm.then_inc(t_done, 1)

                group(0)
                with pe.Fori(1, GROUPS) as g:
                    group(g)


VALUE_AT = {0: 0, 4: 1, 5: 2, 6: 3}
QK_AT = {1: 0, 2: 1, 3: 2}


def projections(c, step, full):
    order = [s for s in range(8) if s in VALUE_AT or (full and s in QK_AT)]
    return 10 + 7 * c + order.index(step)


def qk_out(c, j):
    if isinstance(c, int) and c < 2:
        return 7 * c + j + 1
    return projections(c - 2, 1 + j, True) + 1


def attention(nc, d, parts_d, x_all, ot_all, w_name, bias_name, rope):
    with ExitStack() as ctx:
        m = Memory(nc, ctx, w_name)
        raw = [m.sb(f"raw{k}", [P, 3 * C]) for k in range(3)]
        hi = [m.sb(f"hi{k}", [P, 3 * C], F32R) for k in range(3)]
        lo = m.sb("lo", [P, 3 * C], F32R)
        low_row = m.sb("low_row", [P, 1])
        one_rows = m.sb("one_rows", [P, CHUNK])
        xh = [m.sb(f"xh{k}", [P, 2, CHUNK], F32R) for k in range(2)]
        xl = [m.sb(f"xl{k}", [P, 2, CHUNK], F32R) for k in range(2)]
        qk = m.sb("qk", [P, 3, CHUNK])
        rest = m.sb("rest", [P, 3, CHUNK])
        part = [m.sb(f"part{k}", [P, 3, CHUNK], BF16) for k in range(3)]
        qs = [m.sb(f"qs{k}", [PARTS, HEADS, CHUNK], BF16) for k in range(2)]
        ks = [m.sb(f"ks{k}", [PARTS, HEADS, CHUNK], BF16) for k in range(2)]
        vp = [m.sb(f"vp{k}", [SEQ, CHUNK_B, HEADS, 2 * HD]) for k in range(2)]
        pt = [m.sb(f"pt{k}", [SEQ, 6, SEQ]) for k in range(2)]
        nm = [m.sb(f"nm{k}", [SEQ, HEADS]) for k in range(2)]
        nmr = [m.sb(f"nmr{k}", [SEQ, HEADS]) for k in range(2)]
        ms = [m.sb(f"ms{k}", [SEQ, 3, HEADS], BF16) for k in range(2)]
        mt = [m.sb(f"mt{k}", [PARTS, SEQ], BF16) for k in range(2)]
        pick1 = m.sb("pick1", [PARTS, HEADS])
        pick = m.sb("pick", [PARTS, HEADS, SEQ], BF16)
        identf = m.sb("identf", [P, P])
        identb = m.sb("identb", [P, P], BF16)
        rec = m.sb("rec", [P, 3, SEQ])
        if rope:
            swapped = m.sb("swapped", [P, 3, CHUNK])
            cos = m.sb("cos", [P, CHUNK])
            sin = m.sb("sin", [P, CHUNK])
        s_ps = [m.psum(f"s_ps{k}", [P, 512]) for k in range(2)]
        st_ps = [m.psum(f"st_ps{k}", [P, 512]) for k in range(2)]
        proj_ps = m.psum("proj_ps", [P, 512])
        mt_ps = m.psum("mt_ps", [P, 1024], BF16)
        o_ps = [m.psum(f"o_ps{k}", [P, 512]) for k in range(2)]

        const_in, const_done = m.sem("const_in"), m.sem("const_done")
        twice_in = [m.sem(f"twice_in{k}") for k in range(2)]
        w_hi, w_lo, xh_done, xl_done = (m.sem(x) for x in ("w_hi", "w_lo", "xh_done", "xl_done"))
        proj_done, proj_out = m.sem("proj_done"), m.sem("proj_out")
        swap_done, cos_done, sin_done, rope_done = (m.sem(x) for x in ("swap", "cos_mul", "sin_mul", "rope"))
        p1_done, r1_done, p2_done, p3_done = (m.sem(x) for x in ("p1", "r1", "p2", "p3"))
        stack_in = [m.sem(f"stack_in{k}") for k in range(2)]
        parts_out = [m.sem(f"parts_out{k}") for k in range(3)]
        s_done, max_done, msplit, mt_done, mt_out = (m.sem(x) for x in ("s_done", "max_done", "msplit", "mt_done", "mt_out"))
        st_done, exp_done, pv_done = m.sem("st_done"), m.sem("exp_done"), m.sem("pv_done")
        rows_zero, ones_done = m.sem("rows_zero"), m.sem("ones_done")
        dve_turn, pe_turn, sp_turn = (m.sem(x) for x in ("dve_turn", "pe_turn", "sp_turn"))
        den_done, rec_done, norm_done = m.sem("den_done"), m.sem("rec_done"), m.sem("norm_done")
        N_CONST = 7 + (2 if bias_name else 0) + (2 if rope else 0)
        N_STACK = 16 * 2 * (PARTS // HD)
        N_DONE = 9

        def chunk_of(x, c):
            return x[:, :, bass.ds(CHUNK * c, CHUNK)]

        def run(eng_fori, pair):
            pair(0, False)
            with eng_fori(1, CHUNKS // 2 - 1) as i:
                pair(i, False)
            pair(CHUNKS // 2 - 1, True)

        with nc.Block() as block:
            @block.sync
            def _(sp):
                for k, part_of in enumerate((slice(0, 2 * CHUNK), slice(2 * CHUNK, ROWS))):
                    sp.dma_start(x_all[CB:P, 1, part_of], x_all[0:CB, 1, part_of]).then_inc(twice_in[k], 16)
                sp.dma_start(raw[0][:, :], d[w_name][0:P, :]).then_inc(const_in, 16)
                for dst in (raw[1][0:CB, :], raw[1][CB:P, :], raw[2][0:CB, :]):
                    sp.dma_start(dst, d[w_name][P:C, :]).then_inc(const_in, 16)
                sp.dma_start(low_row[:, :], d["low_row"]).then_inc(const_in, 16)
                sp.wait_ge(rows_zero, 1)
                if bias_name:
                    for row in (CB, CB + 1):
                        sp.dma_start(raw[2][row:row + 1, :], d[bias_name].rearrange("(a n) -> a n", a=1)).then_inc(const_in, 16)
                sp.dma_start(pick1[:, :], d["pick"]).then_inc(const_in, 16)
                sp.dma_start(identf[:, :], d["ident"]).then_inc(const_in, 16)
                if rope:
                    sp.dma_start(cos[:, :], d["cos"]).then_inc(const_in, 16)
                    sp.dma_start(sin[:, :], d["sin"]).then_inc(const_in, 16)

                def stack(i, k, used):
                    c = 2 * i + k
                    if not isinstance(i, int) or i:
                        hold(sp, stack_in[k], N_STACK * i, sp_turn)
                    for n, made in enumerate((p1_done, p2_done, p3_done)):
                        sp.wait_ge(made, c + 1)
                        for a in range(2):
                            sp.dma_start(parts_d[k, n, a].rearrange("(m p) t -> p m t", p=CB),
                                         part[n][CB * a:CB * a + CB, :, :]).then_inc(parts_out[n], 16)
                    for n in range(3):
                        hold(sp, parts_out[n], 32 * (c + 1), sp_turn)
                    after(sp, st_done, used)
                    for a, dst, which in ((0, qs[k], (0, 0, 1, 1, 0, 2)), (1, ks[k], (0, 1, 0, 1, 2, 0))):
                        for r, n in enumerate(which):
                            sp.dma_start(dst[HD * r:HD * r + HD, :, :],
                                         parts_d[k, n, a].rearrange("(h e) t -> e h t", e=HD)).then_inc(stack_in[k], 16)

                stack(0, 0, 0)

                def chunk(i, k, full, more):
                    c = 2 * i + k
                    if more:
                        stack(*((i, 1) if k == 0 else (i + 1, 0)), 8 * c)

                def pair(i, last):
                    for k in range(2):
                        chunk(i, k, not last, not (last and k == 1))

                run(sp.Fori, pair)

            @block.scalar
            def _(act):
                def project_out_qk(n, j, chunk_no):
                    act.wait_ge(proj_done, n + 1)
                    if j == 0:
                        after(act, r1_done, chunk_no)
                    act.activation(qk[:, j, :], proj_ps[:, 0:CHUNK], ACT.Copy).then_inc(proj_out, 1)

                def project_out_v(n, k, b, used):
                    act.wait_ge(proj_done, n + 1)
                    after(act, pv_done, used)
                    act.activation(vp[k][:, b, :, 0:HD], proj_ps[0:SEQ, 0:C].rearrange("p (h e) -> p h e", e=HD),
                                   ACT.Copy).then_inc(proj_out, 1)

                def part1(i, k):
                    if rope:
                        act.wait_ge(rope_done, 3 * (2 * i + k + 1))
                    after(act, parts_out[0], 32 * (2 * i + k))
                    act.activation(part[0][:, :, :], qk[:, :, :], ACT.Copy).then_inc(p1_done, 1)

                def part2(i, k):
                    act.wait_ge(r1_done, 2 * i + k + 1)
                    after(act, parts_out[1], 32 * (2 * i + k))
                    act.activation(part[1][:, :, :], rest[:, :, :], ACT.Copy).then_inc(p2_done, 1)

                def x_high(c, k):
                    act.activation(xh[k][:, :, :], chunk_of(x_all, c), ACT.Copy).then_inc(xh_done, 1)

                act.wait_ge(twice_in[0], 16)
                x_high(0, 0)
                x_high(1, 1)
                act.wait_ge(const_in, 16 * N_CONST)
                for k in range(3):
                    act.activation(hi[k][:, :], raw[k][:, :], ACT.Copy).then_inc(w_hi, 1)
                act.wait_ge(twice_in[1], 16)
                act.wait_ge(const_done, N_DONE)
                for n in range(3):
                    project_out_qk(n, n, 0)
                if not rope:
                    act.wait_ge(proj_out, 3)
                part1(0, 0)
                for b in range(4):
                    project_out_v(3 + b, 0, b, 0)
                part2(0, 0)
                for n in range(3):
                    project_out_qk(7 + n, n, 1)
                if not rope:
                    act.wait_ge(proj_out, 10)
                part1(0, 1)
                part2(0, 1)

                def chunk(i, k, first, full, more):
                    c = 2 * i + k
                    if full:
                        act.wait_ge(proj_done, 10 + 7 * c)
                        act.wait_ge(xl_done, 2 * c + 2)
                        x_high(c + 2, k)
                    for s in range(8):
                        g = 8 * c + s
                        if s % 2 == 0:
                            b_no = 4 * c + s // 2
                            act.wait_ge(mt_done, b_no + 1)
                            after(act, st_done, 2 * b_no - 2)
                            act.activation(mt[s // 2 % 2][0:3 * HEADS, :], mt_ps[0:3 * HEADS, 0:SEQ], ACT.Copy).then_inc(mt_out, 1)
                        act.wait_ge(st_done, g + 1)
                        after(act, pv_done, g - 1)
                        act.activation(pt[s % 2][:, :, :],
                                       st_ps[s % 2][0:SEQ, 0:6 * SEQ].rearrange("p (h t) -> p h t", t=SEQ),
                                       ACT.Exp, scale=HD ** -0.5).then_inc(exp_done, 1)
                        if more and s in VALUE_AT:
                            project_out_v(projections(c, s, full), 1 - k, VALUE_AT[s], 8 * c)
                        if full and s in QK_AT:
                            project_out_qk(projections(c, s, full), QK_AT[s], c + 2)
                        if s == (5 if rope else 4) and full:
                            if not rope:
                                act.wait_ge(proj_out, projections(c, 3, full) + 1)
                            part1(i + 1, k)
                        if s == (6 if rope else 5) and full:
                            part2(i + 1, k)

                def pair(i, last):
                    for k in range(2):
                        chunk(i, k, isinstance(i, int) and i == 0 and k == 0, not last, not (last and k == 1))

                run(act.Fori, pair)

            @block.gpsimd
            def _(pool):
                pool.memset(vp[0][:, :, :, HD:], 1.0).then_inc(const_done, 1)
                pool.memset(vp[1][:, :, :, HD:], 1.0).then_inc(const_done, 1)
                pool.memset(ot_all[:, :, TOKENS:ROWS], 0.0).then_inc(const_done, 1)
                pool.wait_ge(const_in, 16 * N_CONST)

                def chunk(i, k):
                    c = 2 * i + k
                    after(pool, p3_done, c)
                    if rope:
                        for j in range(3):
                            pool.wait_ge(proj_out, qk_out(c, j))
                            pool.tensor_tensor(rest[:, j, :], qk[:, j, :], cos[:, :], ALU.mult).then_inc(cos_done, 1)
                            pool.wait_ge(swap_done, 3 * c + j + 1)
                            pool.tensor_tensor(swapped[:, j, :], swapped[:, j, :], sin[:, :], ALU.mult).then_inc(sin_done, 1)
                            pool.wait_ge(sin_done, 3 * c + j + 1)
                            pool.tensor_tensor(qk[:, j, :], swapped[:, j, :], rest[:, j, :], ALU.add).then_inc(rope_done, 1)
                        pool.wait_ge(rope_done, 3 * (c + 1))
                    pool.wait_ge(p1_done, c + 1)
                    pool.tensor_tensor(rest[:, :, :], qk[:, :, :], part[0][:, :, :], ALU.subtract).then_inc(r1_done, 1)
                    pool.wait_ge(p2_done, c + 1)
                    after(pool, parts_out[2], 32 * c)
                    pool.tensor_tensor(part[2][:, :, :], rest[:, :, :], part[1][:, :, :], ALU.subtract).then_inc(p3_done, 1)

                chunk(0, 0)
                chunk(0, 1)
                with pool.Fori(1, CHUNKS // 2) as i:
                    for k in range(2):
                        chunk(i, k)

            @block.vector
            def _(dve):
                dve.memset(raw[2][CB:P, :], 0.0).then_inc(rows_zero, 1)
                dve.memset(one_rows[CB:P, :], 0.0).then_inc(ones_done, 1)
                dve.wait_ge(ones_done, 1)
                dve.memset(one_rows[CB:CB + 2, :], 1.0).then_inc(ones_done, 1)
                dve.wait_ge(ones_done, 2)
                for k in range(2):
                    dve.tensor_copy(xl[k][CB:P, 1, :], one_rows[CB:P, :]).then_inc(const_done, 1)
                for k in range(2):
                    dve.memset(mt[k][:, :], 0.0).then_inc(const_done, 1)
                dve.wait_ge(const_in, 16 * N_CONST)
                dve.tensor_copy(identb[:, :], identf[:, :]).then_inc(const_done, 1)
                dve.tensor_copy(pick[:, :, :], pick1[:, :].unsqueeze(2).to_broadcast([PARTS, HEADS, SEQ])).then_inc(const_done, 1)

                def x_low(c, k):
                    dve.wait_ge(xh_done, c + 1)
                    x = chunk_of(x_all, c)
                    dve.tensor_tensor(xl[k][:, 0, :], x[:, 0, :], xh[k][:, 0, :].bitcast(F32), ALU.subtract).then_inc(xl_done, 1)
                    dve.tensor_tensor(xl[k][0:CB, 1, :], x[0:CB, 1, :], xh[k][0:CB, 1, :].bitcast(F32), ALU.subtract).then_inc(xl_done, 1)

                x_low(0, 0)
                x_low(1, 1)
                dve.wait_ge(w_hi, 3)
                dve.tensor_tensor(lo[:, :], raw[0][:, :], hi[0][:, :].bitcast(F32), ALU.subtract).then_inc(w_lo, 1)
                low = slice(CB, P)
                dve.tensor_tensor(hi[1][low, :], raw[1][low, :], hi[1][low, :].bitcast(F32), ALU.subtract).then_inc(w_lo, 1)
                dve.scalar_tensor_tensor(out=hi[2][low, :], in0=hi[2][low, :].bitcast(F32), scalar=low_row[low, 0:1],
                                         in1=raw[2][low, :], op0=ALU.mult, op1=ALU.add).then_inc(w_lo, 1)

                def swap_halves(c, j):
                    after(dve, rope_done, 3 * c)
                    hold(dve, proj_out, qk_out(c, j), dve_turn)
                    dve.stream_shuffle(swapped[:, j, :], qk[:, j, :], [l ^ 8 for l in range(32)]).then_inc(swap_done, 1)

                def negmax(g, place):
                    dve.wait_ge(s_done, g + 1)
                    half, b2 = place % 2, place // 2
                    dve.tensor_reduce(nm[b2][:, 6 * half:6 * half + 6],
                                      s_ps[half][0:SEQ, 0:6 * SEQ].rearrange("p (h t) -> p h t", t=SEQ),
                                      AX_X, ALU.max, negate=True).then_inc(max_done, 1)

                def split_max(b_no, b2):
                    x, r, s = nm[b2], nmr[b2], ms[b2]
                    dve.wait_ge(max_done, 2 * b_no + 2)
                    after(dve, mt_done, b_no - 1)
                    dve.tensor_copy(s[:, 0, :], x[:, :]).then_inc(msplit, 1)
                    dve.wait_ge(msplit, 4 * b_no + 1)
                    dve.tensor_tensor(r[:, :], x[:, :], s[:, 0, :], ALU.subtract).then_inc(msplit, 1)
                    dve.wait_ge(msplit, 4 * b_no + 2)
                    dve.tensor_copy(s[:, 1, :], r[:, :]).then_inc(msplit, 1)
                    dve.wait_ge(msplit, 4 * b_no + 3)
                    dve.tensor_tensor(s[:, 2, :], r[:, :], s[:, 1, :], ALU.subtract).then_inc(msplit, 1)

                def normalize(b_no, b2):
                    after(dve, norm_done, b_no)
                    hold(dve, pv_done, 2 * b_no + 2, dve_turn)
                    o = o_ps[b2][:, 0:3 * SEQ].rearrange("p (g t) -> p g t", t=SEQ)
                    dve.stream_shuffle(rec[:, :, :], o, [HD + l % HD for l in range(32)]).then_inc(den_done, 1)
                    dve.wait_ge(den_done, b_no + 1)
                    dve.reciprocal(rec[:, :, :], rec[:, :, :]).then_inc(rec_done, 1)
                    dve.wait_ge(rec_done, b_no + 1)
                    dve.tensor_tensor(ot_all[:, :, bass.ds(b_no * SEQ, SEQ)], o, rec[:, :, :], ALU.mult).then_inc(norm_done, 1)

                if rope:
                    for c in range(2):
                        for j in range(3):
                            swap_halves(c, j)
                negmax(0, 0)
                negmax(1, 1)
                split_max(0, 0)
                negmax(2, 2)

                def chunk(i, k, first, full, more):
                    c = 2 * i + k
                    for s in range(8):
                        g = 8 * c + s
                        if s == 0 and full:
                            x_low(c + 2, k)
                        if more or s < 5:
                            negmax(g + 3, (s + 3) % 4)
                            if s % 2 == 0:
                                split_max(4 * c + s // 2 + 1, (s // 2 + 1) % 2)
                        if s % 2 == 0 and not (first and s == 0):
                            normalize(4 * c + s // 2 - 1, (s // 2 + 1) % 2)
                        if rope and full and s - 1 in QK_AT:
                            swap_halves(c + 2, QK_AT[s - 1])

                def pair(i, last):
                    for k in range(2):
                        chunk(i, k, isinstance(i, int) and i == 0 and k == 0, not last, not (last and k == 1))

                run(dve.Fori, pair)
                normalize(BATCH - 1, 1)
                dve.wait_ge(norm_done, BATCH)

            @block.tensor
            def _(pe):
                def products(o, k, w, t, stationary_w):
                    pairs = ((hi[0], xh[k][:, 0, t]), (hi[0], xl[k][:, 0, t]), (lo, xh[k][:, 0, t]),
                             (hi[1], xh[k][:, 1, t]), (hi[2], xl[k][:, 1, t]))
                    for n, (a, x) in enumerate(pairs):
                        left, right = (a[:, w], x) if stationary_w else (x, a[:, w])
                        mm = pe.matmul(o, left, right, start=(n == 0), stop=(n == len(pairs) - 1))
                    mm.then_inc(proj_done, 1)

                def project_qk(n, k, j, c):
                    pe.wait_ge(xl_done, 2 * c + 2)
                    after(pe, proj_out, n)
                    products(proj_ps[:, 0:CHUNK], k, slice(P * j, P * j + P), slice(0, CHUNK), True)

                def project_v(n, k, b, c):
                    pe.wait_ge(xl_done, 2 * c + 2)
                    after(pe, proj_out, n)
                    products(proj_ps[0:SEQ, 0:C], k, slice(2 * C, 3 * C), slice(SEQ * b, SEQ * b + SEQ), False)

                def score(g, i, k, b, half):
                    if b == 0 and half == 0:
                        pe.wait_ge(stack_in[k], N_STACK * (i + 1))
                    after(pe, max_done, g - 1)
                    for j in range(6):
                        t = slice(SEQ * b, SEQ * b + SEQ)
                        mm = pe.matmul(s_ps[half][0:SEQ, SEQ * j:SEQ * j + SEQ], qs[k][:, 6 * half + j, t],
                                       ks[k][:, 6 * half + j, t], start=True, stop=True)
                    mm.then_inc(s_done, 1)

                pe.wait_ge(const_in, 16 * N_CONST)
                pe.wait_ge(const_done, N_DONE)
                pe.wait_ge(w_lo, 3)
                for j in range(3):
                    project_qk(j, 0, j, 0)
                for b in range(4):
                    project_v(3 + b, 0, b, 0)
                for j in range(3):
                    project_qk(7 + j, 1, j, 1)
                for g in range(3):
                    score(g, 0, 0, g // 2, g % 2)

                def values(c, k, b, half):
                    b_no, b2 = 4 * c + b, b % 2
                    pe.wait_ge(exp_done, 2 * b_no + half + 1)
                    if half == 0:
                        after(pe, norm_done, b_no - 1)
                    for j in range(6):
                        head = 6 * half + j
                        lane = 2 * HD * (head % 4)
                        col = SEQ * (head // 4)
                        mm = pe.matmul(o_ps[b2][lane:lane + 2 * HD, col:col + SEQ], vp[k][:, b, head, :],
                                       pt[half][:, j, :], start=True, stop=True, tile_position=(0, lane))
                    mm.then_inc(pv_done, 1)

                def chunk(i, k, first, full, more):
                    c = 2 * i + k
                    for s in range(8):
                        g = 8 * c + s
                        b_no, b, half, b2 = 4 * c + s // 2, s // 2, s % 2, s // 2 % 2
                        if half == 0:
                            after(pe, mt_out, b_no)
                            hold(pe, msplit, 4 * b_no + 4, pe_turn)
                            pe.transpose(mt_ps[0:3 * HEADS, 0:SEQ], ms[b2][:, :, :].rearrange("p a h -> p (a h)"),
                                         identb[0:SEQ, 0:SEQ]).then_inc(mt_done, 1)
                        if more or s < 5:
                            ahead = (i, k) if s < 5 else ((i, 1) if k == 0 else (i + 1, 0))
                            score(g + 3, *ahead, (s + 3) // 2 % 4, (s + 3) % 2)
                        if more and s in VALUE_AT:
                            project_v(projections(c, s, full), 1 - k, VALUE_AT[s], c + 1)
                        if full and s in QK_AT:
                            project_qk(projections(c, s, full), k, QK_AT[s], c + 2)
                        if half == 0:
                            pe.wait_ge(mt_out, b_no + 1)
                        after(pe, exp_done, g - 1)
                        t = slice(SEQ * b, SEQ * b + SEQ)
                        for j in range(6):
                            o = st_ps[half][0:SEQ, SEQ * j:SEQ * j + SEQ]
                            pe.matmul(o, ks[k][:, 6 * half + j, t], qs[k][:, 6 * half + j, t], start=True, stop=False)
                            mm = pe.matmul(o, pick[:, 6 * half + j, :], mt[b2][:, :], start=False, stop=True)
                        mm.then_inc(st_done, 1)
                        if not (first and s == 0):
                            if s == 0:
                                values(c - 1, 1 - k, 3, 1)
                            else:
                                values(c, k, (s - 1) // 2, (s - 1) % 2)

                def pair(i, last):
                    for k in range(2):
                        chunk(i, k, isinstance(i, int) and i == 0 and k == 0, not last, not (last and k == 1))

                run(pe.Fori, pair)
                values(CHUNKS - 1, 1, 3, 1)



def load_heads(sp, ots, ots_in, acc_done, ot_all, g):
    for k in range(4):
        after(sp, acc_done, 4 * g - 3 + k if not isinstance(g, int) or g else 0)
        sp.dma_start(ots[k][:, :, :], ot_all[:, :, bass.ds(512 * g + P * k, P)]).then_inc(ots_in[k], 16)


def project_heads(pe, ots, ots_in, acc, acc_done, wp, g, acc_used, tiles=range(4)):
    for k in tiles:
        pe.wait_ge(ots_in[k], 16 * (g + 1))
        after(pe, acc_used, 4 * g - 3 + k if not isinstance(g, int) or g else 0)
        for s in range(3):
            mm = pe.matmul(acc[k][:, 0:C], ots[k][:, s, :], wp[:, s, :], start=(s == 0), stop=(s == 2))
        mm.then_inc(acc_done, 1)


def in_pairs(fori, group):
    group(1, 1)
    group(2, 0)
    with fori(2, GROUPS // 2) as i:
        group(2 * i - 1, 1)
        group(2 * i, 0)
    group(GROUPS - 2, 1)
    group(GROUPS - 1, 0)


def between(nc, d, h, ot_all, x_all, kept_d):
    with ExitStack() as ctx:
        m = Memory(nc, ctx, "mid")
        ident = m.sb("ident", [P, P])
        wp = m.sb("wp", [P, 3, C])
        gain = m.sb("gain", [P, 4])
        ots = [m.sb(f"ots{k}", [P, 3, P]) for k in range(4)]
        hp = m.sb("hp", [P, 4, C])
        xn = [m.sb(f"xn{k}", [P, C]) for k in range(4)]
        n1, n2 = NormGroup(m, "n1"), NormGroup(m, "n2")
        acc = [m.psum(f"acc{k}", [P, 512]) for k in range(4)]
        ta = m.psum("ta", [P, 512])
        tb = m.psum("tb", [P, 512])
        const_in = m.sem("const_in")
        ots_in = [m.sem(f"ots_in{k}") for k in range(4)]
        acc_done, hp_done, kept, y_done, xn_done, t_done, t_out = (
            m.sem(x) for x in ("acc_done", "hp_done", "kept", "y_done", "xn_done", "t_done", "t_out"))
        with nc.Block() as block:
            @block.sync
            def _(sp):
                sp.dma_start(ident[:, :], d["ident"]).then_inc(const_in, 16)
                sp.dma_start(wp[:, :, :], d["proj1_w"]).then_inc(const_in, 16)
                for j, name in enumerate(("ln1_g", "ln1_b")):
                    sp.dma_start(gain[:, j:j + 1], d[name][0:P].rearrange("(p a) -> p a", a=1)).then_inc(const_in, 16)
                    sp.dma_start(gain[0:CB, 2 + j:3 + j], d[name][P:C].rearrange("(p a) -> p a", a=1)).then_inc(const_in, 16)
                load_heads(sp, ots, ots_in, acc_done, ot_all, 0)

                def group(g, last=False):
                    if not last:
                        load_heads(sp, ots, ots_in, acc_done, ot_all, g + 1)
                    sp.wait_ge(hp_done, 4 * g + 4)
                    sp.dma_start(kept_d[bass.ds(512 * g, 512), :].rearrange("(t p) c -> p t c", p=P), hp[:, :, :]).then_inc(kept, 16)

                with sp.Fori(0, GROUPS - 1) as g:
                    group(g)
                group(GROUPS - 1, True)
                sp.wait_ge(kept, 16 * GROUPS)

            @block.vector
            def _(dve):
                hs = [hp[:, k, :] for k in range(4)]

                def rows_of(g):
                    return [tile_of(h, 4 * g + k) for k in range(4)]

                def add(g):
                    after(dve, kept, 16 * g)
                    after(dve, y_done, 4 * g)
                    for k in range(4):
                        dve.wait_ge(acc_done, 4 * g + k + 1)
                        dve.tensor_tensor(hs[k], acc[k][:, 0:C], rows_of(g)[k], ALU.add).then_inc(hp_done, 1)
                    norm_stats(dve, n1, hs, g + 1, hp_done)
                    norm_inverse(dve, n1, g + 1)

                def second(g):
                    after(dve, t_done, g)
                    norm_apply(dve, n2, [x[:, :] for x in xn], rows_of(g), g + 1, xn_done)

                def first(g):
                    norm_apply(dve, n1, rows_of(g), hs, g + 1, y_done)
                    after(dve, xn_done, 4 * g)
                    norm_stats(dve, n2, rows_of(g), g + 1, y_done)
                    norm_inverse(dve, n2, g + 1)

                def group(g):
                    add(g)
                    second(g - 1)
                    first(g)

                add(0)
                first(0)
                group(1)
                with dve.Fori(2, GROUPS) as g:
                    group(g)
                second(GROUPS - 1)

            @block.scalar
            def _(act):
                act.wait_ge(const_in, 16 * 6)

                def group(g):
                    norm_root(act, n2, g + 1)
                    if not (isinstance(g, int) and g == GROUPS - 1):
                        norm_root(act, n1, g + 2)
                    act.wait_ge(t_done, g + 1)
                    act.activation(x_all[:, 0, bass.ds(512 * g, 512)], ta[:, :], ACT.Identity, scale=gain[:, 0:1], bias=gain[:, 1:2]).then_inc(t_out, 1)
                    act.activation(x_all[0:CB, 1, bass.ds(512 * g, 512)], tb[0:CB, :], ACT.Identity, scale=gain[0:CB, 2:3], bias=gain[0:CB, 3:4]).then_inc(t_out, 1)

                norm_root(act, n1, 1)
                group(0)
                with act.Fori(1, GROUPS - 1) as g:
                    group(g)
                group(GROUPS - 1)

            @block.tensor
            def _(pe):
                pe.wait_ge(const_in, 16 * 6)

                def transposes(g):
                    after(pe, t_out, 2 * g)
                    for k in range(4):
                        pe.wait_ge(xn_done, 4 * g + k + 1)
                        pe.transpose(ta[:, P * k:P * k + P], xn[k][:, 0:P], ident[:, :])
                        mm = pe.transpose(tb[0:CB, P * k:P * k + P], xn[k][:, P:C], ident[:, :])
                    mm.then_inc(t_done, 1)

                def group(g):
                    project_heads(pe, ots, ots_in, acc, acc_done, wp, g + 1, hp_done)
                    transposes(g - 1)

                for g in range(2):
                    project_heads(pe, ots, ots_in, acc, acc_done, wp, g, hp_done)
                group(1)
                with pe.Fori(2, GROUPS - 1) as g:
                    group(g)
                for g in range(GROUPS - 2, GROUPS):
                    transposes(g)


def dispatch(nc, d, h, ot_all, kept_d, queue_d, keep):
    with ExitStack() as ctx:
        m = Memory(nc, ctx, "disp")
        ident = m.sb("ident", [P, P])
        wp = m.sb("wp", [P, 3, C])
        gain = m.sb("gain", [P, 4])
        gate_a = m.sb("gate_a", [P, EXPERTS])
        gate_c = m.sb("gate_c", [CB, EXPERTS])
        gate_b = m.sb("gate_b", [P, EXPERTS])
        trif = m.sb("trif", [P, P])
        tri = m.sb("tri", [P, P], BF16)
        ones = m.sb("ones", [P, P], BF16)
        eight = m.sb("eight", [P, EXPERTS])
        region = m.sb("region", [P, EXPERTS])
        valid = m.sb("valid", [P, TILES])
        dump = m.sb("dump", [P, TILES, 2])
        ots = [m.sb(f"ots{k}", [P, 3, P]) for k in range(4)]
        xp = m.sb("xp", [P, 4, C])
        hk = m.sb("hk", [P, 4, C])
        picked = m.sb("picked", [P, 4, 2, EXPERTS])
        sl = m.sb("sl", [P, 4, 2])
        z0 = [m.sb(f"z0_{k}", [P, 4, QUEUED]) for k in range(2)]
        z1 = [m.sb(f"z1_{k}", [P, 4, QUEUED]) for k in range(2)]
        result_row = m.sb("result_row", [P, TILES, 2])
        za = m.sb("za", [P, 512])
        zb = m.sb("zb", [CB, 512])
        lg = m.sb("lg", [P, 4, EXPERTS])
        v8 = m.sb("v8", [P, 4, EXPERTS])
        i8 = m.sb("i8", [P, 4, EXPERTS], U32)
        idf = m.sb("idf", [P, 4, 2])
        mb = m.sb("mb", [P, 4, EXPERTS], BF16)
        seen_f = m.sb("seen_f", [P, EXPERTS])
        seen = m.sb("seen", [P, EXPERTS], BF16)
        group_sum = m.sb("group_sum", [P, EXPERTS])
        rank = m.sb("rank", [P, 4, EXPERTS])
        prod = m.sb("prod", [P, 4, 2, EXPERTS])
        slot_i = [m.sb(f"slot_i{k}", [P, 8], I32) for k in range(2)]
        n = NormGroup(m, "n3")
        acc = [m.psum(f"acc{k}", [P, 512]) for k in range(4)]
        ta = m.psum("ta", [P, 512])
        tb = m.psum("tb", [P, 512])
        lg_ps = m.psum("lg_ps", [P, 512])
        rk_ps = m.psum("rk_ps", [P, 512])
        const_in = m.sem("const_in")
        N_CONST = 15
        ots_in = [m.sem(f"ots_in{k}") for k in range(4)]
        (acc_done, z1_done, xp_done, hk_in, sum_done, z_done, t_done, z_out, lg_done, lg_out, top, pick, seen_done,
         rank_done, slot, prep) = (m.sem(x) for x in (
             "acc_done", "z1_done", "xp_done", "hk_in", "sum_done", "z_done", "t_done", "z_out", "lg_done", "lg_out",
             "top", "pick", "seen_done", "rank_done", "slot", "prep"))
        pool_turn = m.sem("pool_turn")
        sent = [m.sem(f"sent{k}") for k in range(2)]
        top2, counts = keep
        with nc.Block() as block:
            @block.sync
            def _(sp):
                def const(dst, src):
                    sp.dma_start(dst, src).then_inc(const_in, 16)

                const(ident[:, :], d["ident"])
                const(wp[:, :, :], d["proj2_w"])
                const(result_row[:, :, :], d["result_row"])
                for j, name in enumerate(("ln2_g", "ln2_b")):
                    const(gain[:, j:j + 1], d[name][0:P].rearrange("(p a) -> p a", a=1))
                    const(gain[0:CB, 2 + j:3 + j], d[name][P:C].rearrange("(p a) -> p a", a=1))
                const(gate_a[:, :], d["gate_wT"][0:P, :])
                const(gate_c[:, :], d["gate_wT"][P:C, :])
                const(gate_b[:, :], d["gate_b"].partition_broadcast(P))
                const(trif[:, :], d["tri"])
                const(eight[:, :], d["eight"])
                const(region[:, :], d["region"])
                const(valid[:, :], d["valid"])
                const(dump[:, :, :], d["dump"])
                load_heads(sp, ots, ots_in, acc_done, ot_all, 0)

                def group(g, last=False):
                    if not last:
                        load_heads(sp, ots, ots_in, acc_done, ot_all, g + 1)
                    after(sp, sum_done, g)
                    sp.dma_start(hk[:, :, :], kept_d[bass.ds(512 * g, 512), :].rearrange("(t p) c -> p t c", p=P)).then_inc(hk_in, 16)

                group(0)
                with sp.Fori(1, GROUPS - 1) as g:
                    group(g)
                group(GROUPS - 1, True)

            @block.gpsimd
            def _(pool):
                pool.memset(ones[:, :], 1.0).then_inc(prep, 1)

                def send(g, k):
                    pool.wait_ge(z1_done, 3 * g + 3)
                    hold(pool, slot, 4 * g + 4, pool_turn)
                    for j in range(8):
                        z = (z0, z1)[j % 2][k]
                        pool.indirect_dma_start(queue_d, bass.IndirectOffsetOnAxis(slot_i[k][:, j:j + 1], 0),
                                                z[:, j // 2, :], None).then_inc(sent[k], 16)

                send(0, 0)
                in_pairs(pool.Fori, send)
                pool.wait_ge(sent[0], 128 * (GROUPS // 2 + 1))
                pool.wait_ge(sent[1], 128 * (GROUPS // 2))

            @block.vector
            def _(dve):
                dve.memset(seen_f[:, :], 0.0).then_inc(prep, 1)
                dve.memset(seen[:, :], 0.0).then_inc(prep, 1)
                dve.wait_ge(const_in, 16 * N_CONST)
                dve.tensor_copy(tri[:, :], trif[:, :]).then_inc(prep, 1)

                xs = [xp[:, k, :] for k in range(4)]

                def rows_and_stats(g):
                    rows = [tile_of(h, 4 * g + k) for k in range(4)]
                    after(dve, z_done, 4 * g)
                    after(dve, sum_done, g)
                    for k in range(4):
                        dve.wait_ge(acc_done, 4 * g + k + 1)
                        dve.tensor_tensor(xs[k], acc[k][:, 0:C], rows[k], ALU.add).then_inc(xp_done, 1)
                    norm_stats(dve, n, xs, g + 1, xp_done)
                    norm_inverse(dve, n, g + 1)

                def normalized(g, k):
                    after(dve, sent[k], 64 * (g - k))
                    after(dve, t_done, g - 1)
                    after(dve, z1_done, 3 * (g - 1))
                    norm_apply(dve, n, [z0[k][:, t, 1:QUEUED] for t in range(4)], xs, g + 1, z_done)
                    dve.wait_ge(hk_in, 16 * (g + 1))
                    dve.tensor_tensor(h[:, bass.ds(4 * g, 4), :], hk[:, :, :], xp[:, :, :], ALU.add).then_inc(sum_done, 1)

                def choose(g):
                    dve.wait_ge(lg_done, g + 1)
                    dve.tensor_tensor(lg[:, :, :], lg_ps[:, 0:32].rearrange("p (k e) -> p k e", e=EXPERTS),
                                      gate_b[:, :].unsqueeze(1).to_broadcast([P, 4, EXPERTS]), ALU.add).then_inc(lg_out, 1)
                    hold(dve, lg_out, g + 1, n.turn)
                    for k in range(4):
                        dve.max(v8[:, k, :], lg[:, k, :]).then_inc(top, 1)
                    hold(dve, top, 8 * g + 4, n.turn)
                    for k in range(4):
                        dve.max_index(i8[:, k, :], v8[:, k, :], lg[:, k, :]).then_inc(top, 1)
                    dve.tensor_copy(top2[:, bass.ds(4 * g, 4), :], v8[:, :, 0:2]).then_inc(pick, 1)
                    dve.wait_ge(top, 8 * g + 8)
                    dve.tensor_copy(idf[:, :, :], i8[:, :, 0:2]).then_inc(pick, 1)
                    dve.wait_ge(pick, 5 * g + 2)
                    for j in range(2):
                        dve.tensor_tensor(picked[:, :, j, :], eight[:, :].unsqueeze(1).to_broadcast([P, 4, EXPERTS]),
                                          idf[:, :, j:j + 1].to_broadcast([P, 4, EXPERTS]), ALU.is_equal).then_inc(pick, 1)
                    dve.wait_ge(pick, 5 * g + 4)
                    v = valid[:, bass.ds(4 * g, 4)]
                    dve.tensor_tensor(picked[:, :, :, :].rearrange("p t j e -> p t (j e)"), picked[:, :, :, :].rearrange("p t j e -> p t (j e)"),
                                      v.unsqueeze(2).to_broadcast([P, 4, 16]), ALU.mult).then_inc(pick, 1)
                    dve.wait_ge(pick, 5 * g + 5)
                    after(dve, rank_done, g)
                    dve.tensor_tensor(mb[:, :, :], picked[:, :, 0, :], picked[:, :, 1, :], ALU.add).then_inc(seen_done, 1)

                def place(g, k):
                    dve.wait_ge(seen_done, 2 * g + 1)
                    dve.tensor_reduce(group_sum[:, :], mb[:, :, :].rearrange("p k e -> p e k"), AX_X, ALU.add).then_inc(slot, 1)
                    dve.wait_ge(rank_done, g + 1)
                    dve.tensor_tensor(rank[:, :, :], rk_ps[:, 0:32].rearrange("p (k e) -> p k e", e=EXPERTS),
                                      region[:, :].unsqueeze(1).to_broadcast([P, 4, EXPERTS]), ALU.add).then_inc(slot, 1)
                    dve.wait_ge(slot, 4 * g + 2)
                    dve.tensor_tensor(seen_f[:, :], seen_f[:, :], group_sum[:, :], ALU.add).then_inc(lg_out_2, 1)
                    for j in range(2):
                        dve.tensor_tensor(prod[:, :, j, :], picked[:, :, j, :], rank[:, :, :], ALU.mult).then_inc(prod_done, 1)
                    dve.wait_ge(prod_done, 2 * g + 2)
                    dve.wait_ge(lg_out_2, g + 1)
                    dve.tensor_copy(seen[:, :], seen_f[:, :]).then_inc(seen_done, 1)
                    after(dve, sent[k], 64 * (g - k))
                    dve.tensor_reduce(sl[:, :, :], prod[:, :, :, :], AX_X, ALU.add).then_inc(slot, 1)
                    dve.wait_ge(slot, 4 * g + 3)
                    dve.tensor_tensor(slot_i[k][:, :].rearrange("p (k j) -> p k j", j=2), sl[:, :, :],
                                      dump[:, bass.ds(4 * g, 4), :], ALU.add).then_inc(slot, 1)

                lg_out_2, prod_done = m.sem("seen_sum"), m.sem("prod_done")
                rows_and_stats(0)
                normalized(0, 0)

                def group(g, k):
                    rows_and_stats(g)
                    choose(g - 1)
                    place(g - 1, 1 - k)
                    normalized(g, k)

                in_pairs(dve.Fori, group)
                choose(GROUPS - 1)
                place(GROUPS - 1, 0)
                dve.wait_ge(rank_done, GROUPS + 1)
                dve.tensor_copy(counts[:, :], rk_ps[:, 64:64 + EXPERTS]).then_inc(prep, 1)
                dve.wait_ge(prep, 5)

            @block.scalar
            def _(act):
                act.wait_ge(const_in, 16 * N_CONST)

                def group(g, k):
                    norm_root(act, n, g + 1)
                    after(act, sent[k], 64 * (g - k))
                    for j, z in enumerate((z0, z1)):
                        act.activation(z[k][:, :, 0], result_row[:, bass.ds(4 * g, 4), j], ACT.Copy).then_inc(z1_done, 1)
                    act.wait_ge(z_done, 4 * g + 4)
                    act.activation(z1[k][:, :, 1:QUEUED], z0[k][:, :, 1:QUEUED], ACT.Copy).then_inc(z1_done, 1)
                    act.wait_ge(t_done, g + 1)
                    after(act, lg_done, g)
                    act.activation(za[:, :], ta[:, :], ACT.Identity, scale=gain[:, 0:1], bias=gain[:, 1:2]).then_inc(z_out, 1)
                    act.activation(zb[:, :], tb[0:CB, :], ACT.Identity, scale=gain[0:CB, 2:3], bias=gain[0:CB, 3:4]).then_inc(z_out, 1)

                group(0, 0)
                in_pairs(act.Fori, group)

            @block.tensor
            def _(pe):
                pe.wait_ge(const_in, 16 * N_CONST)
                pe.wait_ge(prep, 4)

                def transposes(g, b2):
                    after(pe, z_out, 2 * g)
                    for k in range(4):
                        pe.wait_ge(z_done, 4 * g + k + 1)
                        pe.transpose(ta[:, P * k:P * k + P], z0[b2][:, k, 1:1 + P], ident[:, :])
                        mm = pe.transpose(tb[0:CB, P * k:P * k + P], z0[b2][:, k, 1 + P:QUEUED], ident[:, :])
                    mm.then_inc(t_done, 1)

                def logits(g):
                    pe.wait_ge(z_out, 2 * g + 2)
                    after(pe, lg_out, g)
                    for k in range(4):
                        o = lg_ps[:, EXPERTS * k:EXPERTS * k + EXPERTS]
                        pe.matmul(o, za[:, P * k:P * k + P], gate_a[:, :], start=True, stop=False)
                        mm = pe.matmul(o, zb[:, P * k:P * k + P], gate_c[:, :], start=False, stop=True)
                    mm.then_inc(lg_done, 1)

                def count(g):
                    pe.wait_ge(seen_done, 2 * g + 1)
                    after(pe, slot, 4 * g)
                    for k in range(4):
                        o = rk_ps[:, EXPERTS * k:EXPERTS * k + EXPERTS]
                        pe.matmul(o, tri[:, :], mb[:, k, :], start=True, stop=False)
                        for j in range(k):
                            pe.matmul(o, ones[:, :], mb[:, j, :], start=False, stop=False)
                        mm = pe.matmul(o, ones[:, :], seen[:, :], start=False, stop=True)
                    mm.then_inc(rank_done, 1)

                project_heads(pe, ots, ots_in, acc, acc_done, wp, 0, xp_done)
                project_heads(pe, ots, ots_in, acc, acc_done, wp, 1, xp_done)

                def group(g, k):
                    def project(*tiles):
                        if not (isinstance(g, int) and g == GROUPS - 1):
                            project_heads(pe, ots, ots_in, acc, acc_done, wp, g + 1, xp_done, tiles)

                    transposes(g - 1, 1 - k)
                    project(0, 1)
                    logits(g - 1)
                    project(2)
                    count(g - 1)
                    project(3)

                in_pairs(pe.Fori, group)
                transposes(GROUPS - 1, 0)
                logits(GROUPS - 1)
                count(GROUPS - 1)
                pe.wait_ge(seen_done, 2 * GROUPS)
                pe.wait_ge(slot, 4 * GROUPS)
                pe.matmul(rk_ps[:, 64:64 + EXPERTS], ones[:, :], seen[:, :], start=True, stop=True).then_inc(rank_done, 1)


def plan(nc, d, queue_d, keep, shares, table):
    top2, counts = keep
    with ExitStack() as ctx:
        m = Memory(nc, ctx, "plan")
        eight = m.sb("eight", [P, EXPERTS])
        region = m.sb("region", [P, EXPERTS])
        number = m.sb("number", [P, TUNE])
        cf = m.sb("cf", [P, EXPERTS])
        ci = m.sb("ci", [P, EXPERTS], I32)
        ct = m.sb("ct", [P, EXPERTS], I32)
        tiles = m.sb("tiles", [P, EXPERTS])
        end = [m.sb(f"end{k}", [P, EXPERTS]) for k in range(2)]
        begin = m.sb("begin", [P, EXPERTS])
        fill = m.sb("fill", [P, EXPERTS], I32)
        tn = m.sb("tn", [P, MOE_TILES])
        cmp = m.sb("cmp", [P, MOE_TILES, EXPERTS])
        te = m.sb("te", [P, MOE_TILES])
        hot = m.sb("hot", [P, MOE_TILES, EXPERTS])
        first = m.sb("first", [P, MOE_TILES])
        real = m.sb("real", [P, MOE_TILES])
        local = m.sb("local", [P, MOE_TILES])
        base = m.sb("base", [P, MOE_TILES])
        diff = m.sb("diff", [P, TILES])
        ex = m.sb("ex", [P, TILES])
        den = m.sb("den", [P, TILES])
        filler = m.sb("filler", [P, 4, C])
        filler_row = m.sb("filler_row", [P, EXPERTS + 2, 4])
        surplus_row = m.sb("surplus_row", [P, MOE_TILES])
        const_in, step, filled, ex_done, diff_done = (
            m.sem(x) for x in ("const_in", "step", "filled", "ex_done", "diff_done"))
        table_done = m.sem("table_done")
        with nc.Block() as block:
            @block.sync
            def _(sp):
                sp.dma_start(eight[:, :], d["eight"]).then_inc(const_in, 16)
                sp.dma_start(region[:, :], d["region"]).then_inc(const_in, 16)
                sp.dma_start(number[:, :], d["number"]).then_inc(const_in, 16)
                sp.dma_start(filler_row[:, :, :], d["filler_row"]).then_inc(const_in, 16)
                sp.dma_start(surplus_row[:, :], d["surplus_row"]).then_inc(const_in, 16)
                sp.wait_ge(const_in, 80)

                def fill_rows(start, e):
                    rows = queue_d[bass.ds(start, SLOTS), :].rearrange("(t p) c -> p t c", p=P)
                    sp.dma_start(rows[:, :, 1:QUEUED], filler[:, :, :]).then_inc(filled, 16)
                    sp.dma_start(rows[:, :, 0:1], filler_row[:, e, :].unsqueeze(2), allow_slow_non_contiguous=True).then_inc(filled, 16)

                sp.wait_ge(table_done, 1)
                for k in range(2):
                    fill_rows(SURPLUS + SLOTS * k, EXPERTS + k)
                sp.wait_ge(table_done, 2)
                for e in range(EXPERTS):
                    start = sp.value_load(fill[0:1, e:e + 1], min_val=e * REGION, max_val=e * REGION + TOKENS)
                    fill_rows(start, e)
                sp.wait_ge(filled, 32 * (EXPERTS + 2))

            @block.scalar
            def _(act):
                act.wait_ge(diff_done, 1)
                act.activation(ex[:, :], diff[:, :], ACT.Exp).then_inc(ex_done, 1)

            @block.vector
            def _(dve):
                said = [0]

                def then(ins):
                    said[0] += 1
                    ins.then_inc(step, 1)
                    dve.wait_ge(step, said[0])

                dve.tensor_tensor(diff[:, :], top2[:, :, 1], top2[:, :, 0], ALU.subtract).then_inc(diff_done, 1)
                dve.memset(filler[:, :, :], 0.0).then_inc(table_done, 1)
                dve.wait_ge(const_in, 80)
                then(dve.tensor_scalar(ci[:, :], counts[:, :], float(SLOTS - 1), None, ALU.add))
                then(dve.tensor_scalar(ct[:, :], ci[:, :], SLOTS.bit_length() - 1, None, ALU.logical_shift_right))
                then(dve.tensor_copy(tiles[:, :], ct[:, :]))
                dve.tensor_tensor(fill[:, :], counts[:, :], region[:, :], ALU.add).then_inc(table_done, 1)
                src = tiles
                for k, by in enumerate((1, 2, 4)):
                    dst = end[k % 2]
                    then(dve.tensor_copy(dst[:, :], src[:, :]))
                    then(dve.tensor_tensor(dst[:, by:], src[:, by:], src[:, :EXPERTS - by], ALU.add))
                    src = dst
                then(dve.tensor_tensor(begin[:, :], src[:, :], tiles[:, :], ALU.subtract))
                shape = [P, MOE_TILES, EXPERTS]
                then(dve.tensor_scalar(tn[:, :], number[:, 0:MOE_TILES], -1.0, None, ALU.add))
                then(dve.tensor_tensor(cmp[:, :, :], tn[:, :].unsqueeze(2).to_broadcast(shape),
                                       src[:, :].unsqueeze(1).to_broadcast(shape), ALU.is_ge))
                then(dve.tensor_reduce(te[:, :], cmp[:, :, :], AX_X, ALU.add))
                then(dve.tensor_tensor(hot[:, :, :], te[:, :].unsqueeze(2).to_broadcast(shape),
                                       eight[:, :].unsqueeze(1).to_broadcast(shape), ALU.is_equal))
                then(dve.tensor_tensor(hot[:, :, :], hot[:, :, :], begin[:, :].unsqueeze(1).to_broadcast(shape), ALU.mult))
                then(dve.tensor_reduce(first[:, :], hot[:, :, :], AX_X, ALU.add))
                then(dve.tensor_scalar(real[:, :], te[:, :], EXPERTS - 0.5, None, ALU.is_lt))
                then(dve.tensor_tensor(local[:, :], tn[:, :], first[:, :], ALU.subtract))
                then(dve.tensor_scalar(local[:, :], local[:, :], float(SLOTS), None, ALU.mult))
                then(dve.tensor_scalar(base[:, :], te[:, :], float(REGION), None, ALU.mult))
                then(dve.tensor_tensor(base[:, :], base[:, :], local[:, :], ALU.add))
                then(dve.tensor_tensor(table[:, 0, :], te[:, :], real[:, :], ALU.mult))
                then(dve.tensor_tensor(base[:, :], base[:, :], surplus_row[:, :], ALU.subtract))
                then(dve.tensor_tensor(base[:, :], base[:, :], real[:, :], ALU.mult))
                then(dve.tensor_tensor(table[:, 1, :], base[:, :], surplus_row[:, :], ALU.add))
                dve.wait_ge(ex_done, 1)
                then(dve.tensor_scalar(den[:, :], ex[:, :], 1.0, None, ALU.add))
                then(dve.reciprocal(den[:, :], den[:, :]))
                then(dve.tensor_copy(shares[:, :, 0], den[:, :]))
                then(dve.tensor_tensor(shares[:, :, 1], den[:, :], ex[:, :], ALU.mult))


def experts(nc, d, queue_d, y_d, table):
    with ExitStack() as ctx:
        m = Memory(nc, ctx, "moe")
        ident = m.sb("ident", [P, P])
        gain = m.sb("gain", [P, 4])
        xr = [m.sb(f"xr{k}", [P, 4, QUEUED + CB]) for k in range(2)]
        place = [m.sb(f"place{k}", [P, 4], I32) for k in range(2)]
        place_done, pool_turn = m.sem("place_done"), m.sem("pool_turn")
        raw = [m.sb(f"raw{k}", [P, 2, HIDDEN]) for k in range(2)]
        hi = [m.sb(f"hi{k}", [P, 2, HIDDEN], F32R) for k in range(2)]
        lo = [m.sb(f"lo{k}", [P, HIDDEN], F32R) for k in range(2)]
        w2 = [m.sb(f"w2_{k}", [P, 6, C]) for k in range(2)]
        b1 = [m.sb(f"b1_{k}", [P, 6]) for k in range(2)]
        b2 = [m.sb(f"b2_{k}", [P, C]) for k in range(2)]
        xf = m.sb("xf", [P, 2, SLOTS])
        xh = [m.sb(f"xh{k}", [P, 2, SLOTS], F32R) for k in range(2)]
        xl = [m.sb(f"xl{k}", [P, 2, SLOTS], F32R) for k in range(2)]
        ht = [m.sb(f"ht{k}", [P, 6, SLOTS]) for k in range(2)]
        y = [m.sb(f"y{k}", [P, 4, C]) for k in range(2)]
        ta = m.psum("ta", [P, 512])
        tc = m.psum("tc", [P, 512])
        up = [m.psum(f"up{k}", [P, 512]) for k in range(2)]
        down = [m.psum(f"down{k}", [P, 512]) for k in range(2)]
        const_in = m.sem("const_in")
        w1_in, w2_in, x_in = ([m.sem(f"{n}{k}") for k in range(2)] for n in ("w1_in", "w2_in", "x_in"))
        (t_done, xf_done, hi_done, lo_done, xh_done, xl_done, up_done, gelu_done, down_done, y_done) = (
            m.sem(x) for x in ("t_done", "xf_done", "hi_done", "lo_done", "xh_done", "xl_done", "up_done",
                               "gelu_done", "down_done", "y_done"))
        stored = [m.sem(f"stored{k}") for k in range(2)]

        def run(fori, tile):
            for k in range(2):
                tile(0, k, True)
            with fori(1, MOE_TILES // 2) as i:
                for k in range(2):
                    tile(i, k, True)
            tile(MOE_TILES // 2, 0, False)

        with nc.Block() as block:
            @block.sync
            def _(sp):
                sp.dma_start(ident[:, :], d["ident"]).then_inc(const_in, 16)
                for j, name in enumerate(("ln2_g", "ln2_b")):
                    sp.dma_start(gain[:, j:j + 1], d[name][0:P].rearrange("(p a) -> p a", a=1)).then_inc(const_in, 16)
                    for half in range(2):
                        sp.dma_start(gain[CB * half:CB * half + CB, 2 + j:3 + j],
                                     d[name][P:C].rearrange("(p a) -> p a", a=1)).then_inc(const_in, 16)

                def load(i, k, used):
                    t = 2 * i + k
                    e = sp.value_load(table[0:1, 0, bass.ds(t, 1)], min_val=0, max_val=EXPERTS - 1)
                    row = sp.value_load(table[0:1, 1, bass.ds(t, 1)], min_val=0, max_val=SURPLUS + SLOTS)
                    after(sp, t_done, t - 1 if used else 0)
                    after(sp, place_done, t - 1 if used else 0)
                    rows = queue_d[bass.ds(row, SLOTS), :].rearrange("(t p) c -> p t c", p=P)
                    sp.dma_start(xr[k][:, :, 0:QUEUED], rows).then_inc(x_in[k], 16)
                    sp.dma_start(xr[k][:, :, QUEUED:], rows[:, :, 1 + P:QUEUED]).then_inc(x_in[k], 16)
                    after(sp, lo_done, 2 * t - 2 if used else 0)
                    w = d["w1T"][bass.ds(e, 1)].rearrange("a c f -> (a c) f")
                    sp.dma_start(raw[k][:, 0, :], w[0:P, :]).then_inc(w1_in[k], 16)
                    for half in range(2):
                        sp.dma_start(raw[k][CB * half:CB * half + CB, 1, :], w[P:C, :]).then_inc(w1_in[k], 16)
                    after(sp, y_done, 4 * t - 4 if used else 0)
                    sp.dma_start(w2[k][:, :, :], d["w2T"][bass.ds(e, 1)].rearrange("a p s c -> (a p) s c")).then_inc(w2_in[k], 16)
                    sp.dma_start(b1[k][:, :], d["b1T"][bass.ds(e, 1)].rearrange("a p s -> (a p) s")).then_inc(w2_in[k], 16)
                    sp.dma_start(b2[k][:, :], d["b2"][bass.ds(e, 1), :].rearrange("a c -> (a c)").partition_broadcast(P)).then_inc(w2_in[k], 16)

                load(0, 0, False)
                load(0, 1, False)
                with sp.Fori(1, MOE_TILES // 2) as i:
                    for k in range(2):
                        load(i, k, True)
                load(MOE_TILES // 2, 0, True)

            @block.gpsimd
            def _(pool):
                def tile(i, k, more):
                    t = 2 * i + k
                    after(pool, stored[k], 64 * i)
                    hold(pool, x_in[k], 32 * (i + 1), pool_turn)
                    pool.tensor_copy(place[k][:, :], xr[k][:, :, 0]).then_inc(place_done, 1)
                    pool.wait_ge(place_done, t + 1)
                    for j in range(4):
                        hold(pool, y_done, 4 * t + j + 1, pool_turn)
                        pool.indirect_dma_start(y_d, bass.IndirectOffsetOnAxis(place[k][:, j:j + 1], 0),
                                                y[k][:, j, :], None).then_inc(stored[k], 16)

                run(pool.Fori, tile)
                pool.wait_ge(stored[0], 64 * (MOE_TILES // 2 + 1))
                pool.wait_ge(stored[1], 64 * (MOE_TILES // 2))

            @block.scalar
            def _(act):
                act.wait_ge(const_in, 16 * 7)

                def weights_hi(i, k):
                    t = 2 * i + k
                    act.wait_ge(w1_in[k], 48 * (i + 1))
                    after(act, up_done, 6 * t - 6 if not isinstance(t, int) or t > 1 else 0)
                    act.activation(hi[k][:, :, :], raw[k][:, :, :], ACT.Copy).then_inc(hi_done, 1)

                def affine(t):
                    act.wait_ge(t_done, t + 1)
                    after(act, xl_done, 2 * t)
                    act.activation(xf[:, 0, :], ta[:, :], ACT.Identity, scale=gain[:, 0:1], bias=gain[:, 1:2]).then_inc(xf_done, 1)
                    act.activation(xf[:, 1, :], tc[:, :], ACT.Identity, scale=gain[:, 2:3], bias=gain[:, 3:4]).then_inc(xf_done, 1)

                weights_hi(0, 0)
                affine(0)

                def tile(i, k, more):
                    t = 2 * i + k
                    act.wait_ge(w2_in[k], 48 * (i + 1))
                    after(act, down_done, 4 * t - 4 if not isinstance(t, int) or t > 1 else 0)
                    for j in range(6):
                        act.wait_ge(up_done, 6 * t + j + 1)
                        act.activation(ht[k][:, j, :], up[j % 2][:, :], ACT.Gelu, bias=b1[k][:, j:j + 1]).then_inc(gelu_done, 1)
                        if j == 2 and more:
                            weights_hi(*((i, 1) if k == 0 else (i + 1, 0)))
                    if more:
                        affine(t + 1)

                run(act.Fori, tile)

            @block.vector
            def _(dve):
                def split(i, k):
                    t = 2 * i + k
                    dve.wait_ge(hi_done, t + 1)
                    dve.tensor_tensor(lo[k][:, :], raw[k][:, 0, :], hi[k][:, 0, :].bitcast(F32), ALU.subtract).then_inc(lo_done, 1)
                    low = slice(CB, P)
                    dve.tensor_tensor(hi[k][low, 1, :], raw[k][low, 1, :], hi[k][low, 1, :].bitcast(F32), ALU.subtract).then_inc(lo_done, 1)

                def split_x(i, k):
                    t = 2 * i + k
                    dve.wait_ge(xf_done, 2 * t + 2)
                    after(dve, up_done, 6 * t - 6 if not isinstance(t, int) or t > 1 else 0)
                    dve.tensor_copy(xh[k][:, :, :], xf[:, :, :]).then_inc(xh_done, 1)
                    dve.wait_ge(xh_done, t + 1)
                    dve.tensor_tensor(xl[k][:, 0, :], xf[:, 0, :], xh[k][:, 0, :].bitcast(F32), ALU.subtract).then_inc(xl_done, 1)
                    dve.tensor_tensor(xl[k][0:CB, 1, :], xf[0:CB, 1, :], xh[k][0:CB, 1, :].bitcast(F32), ALU.subtract).then_inc(xl_done, 1)

                split(0, 0)
                split_x(0, 0)

                def tile(i, k, more):
                    t = 2 * i + k
                    nxt = (i, 1) if k == 0 else (i + 1, 0)
                    if more:
                        split(*nxt)
                        split_x(*nxt)
                    after(dve, stored[k], 64 * i)
                    dve.wait_ge(w2_in[k], 48 * (i + 1))
                    for j in range(4):
                        dve.wait_ge(down_done, 4 * t + j + 1)
                        dve.tensor_tensor(y[k][:, j, :], down[j % 2][:, 0:C], b2[k][:, :], ALU.add).then_inc(y_done, 1)

                run(dve.Fori, tile)

            @block.tensor
            def _(pe):
                pe.wait_ge(const_in, 16 * 7)

                def transposes(i, k):
                    t = 2 * i + k
                    pe.wait_ge(x_in[k], 32 * (i + 1))
                    after(pe, xf_done, 2 * t)
                    for j in range(4):
                        pe.transpose(ta[:, P * j:P * j + P], xr[k][:, j, 1:1 + P], ident[:, :])
                        mm = pe.transpose(tc[:, P * j:P * j + P], xr[k][:, j, 1 + P:], ident[:, :])
                    mm.then_inc(t_done, 1)

                transposes(0, 0)

                def tile(i, k, more):
                    t = 2 * i + k
                    pe.wait_ge(lo_done, 2 * t + 2)
                    pe.wait_ge(xl_done, 2 * t + 2)
                    for j in range(6):
                        after(pe, gelu_done, 6 * t + j - 1)
                        o, f = up[j % 2][:, :], slice(P * j, P * j + P)
                        pe.matmul(o, hi[k][:, 0, f], xh[k][:, 0, :], start=True, stop=False)
                        pe.matmul(o, hi[k][:, 0, f], xl[k][:, 0, :], start=False, stop=False)
                        pe.matmul(o, lo[k][:, f], xh[k][:, 0, :], start=False, stop=False)
                        pe.matmul(o, hi[k][:, 1, f], xh[k][:, 1, :], start=False, stop=False)
                        pe.matmul(o, hi[k][0:CB, 1, f], xl[k][0:CB, 1, :], start=False, stop=True).then_inc(up_done, 1)
                    if more:
                        transposes(*((i, 1) if k == 0 else (i + 1, 0)))
                    pe.wait_ge(w2_in[k], 48 * (i + 1))
                    pe.wait_ge(gelu_done, 6 * t + 6)
                    for j in range(4):
                        after(pe, y_done, 4 * t + j - 1)
                        for s in range(6):
                            mm = pe.matmul(down[j % 2][:, 0:C], ht[k][:, s, P * j:P * j + P], w2[k][:, s, :],
                                           start=(s == 0), stop=(s == 5))
                        mm.then_inc(down_done, 1)

                run(pe.Fori, tile)


def combine(nc, h, out_d, y_d, shares):
    with ExitStack() as ctx:
        m = Memory(nc, ctx, "comb")
        first = m.sb("first", [P, TILES, C])
        second = m.sb("second", [P, TILES, C])
        got_in = [m.sem(f"got_in{g}") for g in range(GROUPS)]
        half_done, row_done, stored = m.sem("half_done"), m.sem("row_done"), m.sem("stored")
        FULL = TOKENS // P
        PART = TOKENS - P * FULL

        def spans(g):
            end = min(4 * g + 4, FULL)
            yield (lambda x, at=0: x[at + 512 * g:at + P * end, :].rearrange("(t p) c -> p t c", p=P),
                   lambda b: b[:, 4 * g:end, :])
            if end == FULL:
                yield lambda x, at=0: x[at + P * FULL:at + TOKENS, :], lambda b: b[0:PART, FULL, :]

        with nc.Block() as block:
            @block.sync
            def _(sp):
                for g in range(GROUPS):
                    for rows, tiles in spans(g):
                        sp.dma_start(tiles(first), rows(y_d)).then_inc(got_in[g], 16)
                        sp.dma_start(tiles(second), rows(y_d, ROWS)).then_inc(got_in[g], 16)
                for g in range(GROUPS):
                    sp.wait_ge(row_done, min(4 * g + 4, FULL + 1))
                    for rows, tiles in spans(g):
                        sp.dma_start(rows(out_d), tiles(second)).then_inc(stored, 16)
                sp.wait_ge(stored, 16 * (GROUPS + 1))

            @block.vector
            def _(dve):
                for g in range(GROUPS):
                    dve.wait_ge(got_in[g], 32 if g + 1 < GROUPS else 64)
                    tiles = range(4 * g, min(4 * g + 4, FULL + 1))
                    for t in tiles:
                        n = P if t < FULL else PART
                        dve.scalar_tensor_tensor(out=h[0:n, t, :], in0=first[0:n, t, :], scalar=shares[0:n, t, 0:1],
                                                 in1=h[0:n, t, :], op0=ALU.mult, op1=ALU.add).then_inc(half_done, 1)
                    for t in tiles:
                        n = P if t < FULL else PART
                        dve.wait_ge(half_done, t + 1)
                        dve.scalar_tensor_tensor(out=second[0:n, t, :], in0=second[0:n, t, :], scalar=shares[0:n, t, 1:2],
                                                 in1=h[0:n, t, :], op0=ALU.mult, op1=ALU.add).then_inc(row_done, 1)


def vit_moe_layer(nc, d, out):
    rows_d = nc.dram_tensor("rows_scratch", [ROWS, C], F32, kind="Internal").ap()
    kept_d = nc.dram_tensor("kept_scratch", [ROWS, C], F32, kind="Internal").ap()
    queue_d = nc.dram_tensor("queue_scratch", [SURPLUS + 2 * SLOTS, QUEUED], F32, kind="Internal").ap()
    y_d = nc.dram_tensor("y_scratch", [Y_ROWS, C], F32, kind="Internal").ap()
    parts_d = nc.dram_tensor("parts_scratch", [2, 3, 2, C, CHUNK], BF16, kind="Internal").ap()
    out_rows = out.rearrange("b s c -> (b s) c")
    embed(nc, d, rows_d)
    with ExitStack() as ctx:
        m = Memory(nc, ctx, "all")
        h = m.sb("h", [P, TILES, C])
        keep = (m.sb("top2", [P, TILES, 2]), m.sb("counts", [P, EXPERTS]))
        with ExitStack() as wide:
            w = Memory(nc, wide, "all")
            ot_all = w.sb("ot_all", [P, 3, ROWS])
            with ExitStack() as feats:
                f = Memory(nc, feats, "all")
                x_all = f.sb("x_all", [P, 2, ROWS])
                first_norm(nc, d, rows_d, h, x_all)
                attention(nc, d, parts_d, x_all, ot_all, "qkv1_w", "qkv1_b", True)
                between(nc, d, h, ot_all, x_all, kept_d)
                attention(nc, d, parts_d, x_all, ot_all, "qkv2_w", None, False)
            dispatch(nc, d, h, ot_all, kept_d, queue_d, keep)
        shares = m.sb("shares", [P, TILES, 2])
        table = m.sb("table", [P, 2, MOE_TILES], I32)
        plan(nc, d, queue_d, keep, shares, table)
        experts(nc, d, queue_d, y_d, table)
        combine(nc, h, out_rows, y_d, shares)


def kernel(**inputs):
    import numpy as _np
    import concourse.bacc as _bacc
    from concourse import mybir as _mybir
    from concourse.bass_utils import run_bass_kernel_spmd as _run

    arrays = lay_out(inputs)
    nc = _bacc.Bacc("TRN2", target_bir_lowering=False, num_devices=1)
    d = {name: nc.dram_tensor(name + "_dram", a.shape, _mybir.dt.from_np(a.dtype), kind="ExternalInput").ap()
         for name, a in arrays.items()}
    out = nc.dram_tensor("out_dram", (BATCH, SEQ, C), F32, kind="ExternalOutput").ap()
    vit_moe_layer(nc, d, out)
    r = _run(nc, [{name + "_dram": a for name, a in arrays.items()}], core_ids=[0])
    return r.results[0]["out_dram"]


def lay_out(inputs):
    import numpy as np

    a = {k: np.asarray(v) for k, v in inputs.items()}
    side = 96 // 16
    x = a["x"].reshape(BATCH, 3, side, 16, side, 16).transpose(0, 1, 2, 4, 3, 5).reshape(BATCH, IMG, PATCH)
    x = x.transpose(1, 0, 2).reshape(IMG // 2, P, 6, P)
    out = {"patches": x.transpose(0, 3, 2, 1).reshape(IMG // 2, P, 6 * P)}
    out["ids"] = a["x_txt"].T.reshape(16, P).T
    out["tune_ids"] = a["L0_txt_tune_ids"]
    out["base_w"], out["train_w"] = a["L0_txt_base_weight"], a["L0_txt_train_weight"]
    out["tok_wT"], out["tok_b"] = a["L0_tok_W"].T, a["L0_tok_b"]
    out["cls"], out["pos"] = a["L0_tok_class_token"], a["L0_tok_pos_embedding"]
    order = np.concatenate([w * C + CB * n + np.r_[0:CB] for n in range(3) for w in range(2)] + [2 * C + np.r_[0:C]])
    out["qkv1_w"], out["qkv1_b"] = a["L0_attn_w_qkv"].T[:, order], a["L0_attn_b_qkv"][order]
    out["qkv2_w"] = a["L0_ffn_qkv_w"].T[:, order]
    for name, w, b in (("proj1_w", a["L0_attn_w_proj"], a["L0_attn_b_proj"]), ("proj2_w", a["L0_ffn_proj_w"], a["L0_ffn_proj_b"])):
        wide = np.zeros((3, 4, 2, HD, C), w.dtype)
        wide[:, :, 0] = w.T.reshape(3, 4, HD, C)
        wide[0, 0, 1, 0] = b
        out[name] = wide.reshape(3, P, C).transpose(1, 0, 2)
    for name in ("ln1_g", "ln1_b", "ln2_g", "ln2_b", "gate_b", "b2"):
        out[name] = a["L0_ffn_" + name]
    out["gate_wT"] = a["L0_ffn_gate_w"].T
    out["w1T"] = a["L0_ffn_w1"].transpose(0, 2, 1)
    out["b1T"] = a["L0_ffn_b1"].reshape(EXPERTS, 6, P).transpose(0, 2, 1)
    out["w2T"] = a["L0_ffn_w2"].transpose(0, 2, 1).reshape(EXPERTS, 6, P, C).transpose(0, 2, 1, 3)
    f = np.float32
    inv = (f(1.0) / np.power(f(10000.0), np.arange(0, HD, 2, dtype=f) / f(HD))).astype(f)
    angle = (np.arange(SEQ, dtype=f)[:, None] * inv[None, :]).astype(f)
    cos, sin = np.cos(angle).T, np.sin(angle).T
    out["cos"] = np.tile(np.concatenate([cos, cos]), (P // HD, CHUNK_B)).astype(f)
    out["sin"] = np.tile(np.concatenate([-sin, sin]), (P // HD, CHUNK_B)).astype(f)
    out["ident"] = np.eye(P, dtype=f)
    pick = np.zeros((PARTS, HEADS), f)
    for j in range(3):
        pick[HEADS * j:HEADS * j + HEADS] = np.eye(HEADS)
    out["pick"] = pick
    out["low_row"] = -(np.arange(P) == CB + 1).astype(f)[:, None]
    out["tri"] = np.triu(np.ones((P, P), f), 1)
    out["number"] = np.tile(np.arange(1, TUNE + 1, dtype=f), (P, 1))
    out["eight"] = np.tile(np.arange(EXPERTS, dtype=f), (P, 1))
    out["region"] = np.tile(np.arange(EXPERTS, dtype=f) * REGION, (P, 1))
    token = np.arange(TILES)[None, :] * P + np.arange(P)[:, None]
    out["valid"] = (token < TOKENS).astype(f)
    dump = np.zeros((P, TILES, 2), f)
    for j in range(2):
        dump[:, :, j] = np.where(token < TOKENS, 0, DUMP + 2 * (token - TOKENS) + j)
    out["dump"] = dump
    out["result_row"] = np.stack([token, token + ROWS], 2).astype(f)
    fillers = np.arange(2 * ROWS, Y_ROWS).reshape(EXPERTS + 2, 4, P)
    out["filler_row"] = fillers.transpose(2, 0, 1).astype(f)
    out["surplus_row"] = np.tile(SURPLUS + SLOTS * (np.arange(MOE_TILES) % 2), (P, 1)).astype(f)
    return {k: np.ascontiguousarray(v) for k, v in out.items()}
```
